# Optimizing a Trainium2 kernel written in Bass

```python
import numpy as np
import jax
import jax.numpy as jnp

def _softmax(x, axis=-1):
    return jax.nn.softmax(x, axis=axis)

def _gelu(x):
    return jax.nn.gelu(x, approximate=True)

def _silu(x):
    return jax.nn.silu(x)

def _sigmoid(x):
    return jax.nn.sigmoid(x)

def _layernorm(x, axis=-1, eps=1e-05):
    m = jnp.mean(x, axis=axis, keepdims=True)
    v = jnp.var(x, axis=axis, keepdims=True)
    return (x - m) / jnp.sqrt(v + eps)

def _scatter_add(tgt, idx, src, axis=0):
    return tgt.at[idx].add(src)

def _segment_sum(src, seg, n):
    return jax.ops.segment_sum(src, seg, n)
kernel_name = 'mk_lm_tower_d2_tok_ids512_r4_1322f5'

def setup_inputs(seed: int=0):
    np.random.seed(seed)
    _w = jnp.asarray

    def _rec_inputs():
        import jax
        import jax.numpy as jnp
        _rk = jax.random.key(seed)
        x = jax.random.randint(jax.random.fold_in(_rk, 1), (64, 128), 0, 15, jnp.int32)
        return x
    x = _rec_inputs()

    def _L0_tok_setup():
        import jax, jax.numpy as jnp
        import numpy as np
        PAD, BOS, EOS, ROW, SEP = (10, 11, 12, 13, 14)
        VOCAB, D_MODEL, MAX_SEQ, MAX_H, MAX_W = (15, 128, 1024, 30, 30)
        B, T = (16, 1024)
        LN_EPS = 1e-05

        def _build_2d_ids(ids):

            def step(carry, tok):
                row, col, in_grid = carry
                is_bos = tok == BOS
                is_sep = tok == SEP
                is_row = tok == ROW
                is_end = (tok == EOS) | (tok == PAD)
                grid_color = in_grid & (tok >= 0) & (tok <= 9)
                emit_r = jnp.where(grid_color, row, 0)
                emit_c = jnp.where(grid_color, col, 0)
                n_grid = jnp.where(is_bos, True, jnp.where(is_end, False, in_grid))
                n_row = jnp.where(is_bos | is_sep, 0, jnp.where(is_row, row + 1, row))
                n_col = jnp.where(is_bos | is_sep | is_row, 0, jnp.where(grid_color, col + 1, col))
                return ((n_row, n_col, n_grid), (emit_r, emit_c))

            def scan_one(seq):
                init = (jnp.int32(0), jnp.int32(0), jnp.bool_(False))
                _, (r, c) = jax.lax.scan(step, init, seq)
                return (r, c)
            r, c = jax.vmap(scan_one)(ids)
            return (jnp.clip(r, 0, MAX_H - 1), jnp.clip(c, 0, MAX_W - 1))
        key = jax.random.key(seed)
        ks = jax.random.split(key, 8)
        input_ids = jax.random.randint(ks[0], (B, T), 0, VOCAB, dtype=jnp.int32)
        s = 0.02
        token_table = jax.random.normal(ks[1], (VOCAB, D_MODEL), jnp.float32) * s
        token_table = token_table.at[PAD].set(0.0)
        pos_table = jax.random.normal(ks[2], (MAX_SEQ, D_MODEL), jnp.float32) * s
        row_table = jax.random.normal(ks[3], (MAX_H, D_MODEL // 2), jnp.float32) * s
        col_table = jax.random.normal(ks[4], (MAX_W, D_MODEL // 2), jnp.float32) * s
        w_spatial = jax.random.normal(ks[5], (D_MODEL, D_MODEL), jnp.float32) * s
        ln_gamma = jnp.ones((D_MODEL,), jnp.float32)
        ln_beta = jnp.zeros((D_MODEL,), jnp.float32)
        return {'input_ids': input_ids, 'token_table': token_table, 'pos_table': pos_table, 'row_table': row_table, 'col_table': col_table, 'w_spatial': w_spatial, 'ln_gamma': ln_gamma, 'ln_beta': ln_beta}
    _L0_tok_all = _L0_tok_setup()
    _L0_tok_in = {k: v for k, v in _L0_tok_all.items() if k in ('token_table', 'pos_table', 'row_table', 'col_table', 'w_spatial', 'ln_gamma', 'ln_beta')}
    del _L0_tok_all

    def _L0_attn_setup():
        import jax, jax.numpy as jnp
        import numpy as np
        B, N, E, H = (4, 512, 128, 8)
        key = jax.random.key(seed)
        ks = jax.random.split(key, 9)
        s_in = 1.0 / np.sqrt(E)
        s_out = 1.0 / np.sqrt(E * H)
        return {'x': jax.random.normal(ks[0], (B, N, E), dtype=jnp.float32), 'Wq': jax.random.normal(ks[1], (E, E * H), dtype=jnp.float32) * s_in, 'bq': jax.random.normal(ks[2], (E * H,), dtype=jnp.float32) * s_in, 'Wk': jax.random.normal(ks[3], (E, E * H), dtype=jnp.float32) * s_in, 'bk': jax.random.normal(ks[4], (E * H,), dtype=jnp.float32) * s_in, 'Wv': jax.random.normal(ks[5], (E, E * H), dtype=jnp.float32) * s_in, 'bv': jax.random.normal(ks[6], (E * H,), dtype=jnp.float32) * s_in, 'Wp': jax.random.normal(ks[7], (E * H, E), dtype=jnp.float32) * s_out, 'bp': jax.random.normal(ks[8], (E,), dtype=jnp.float32) * s_out}
    _L0_attn_all = _L0_attn_setup()
    _L0_attn_in = {k: v for k, v in _L0_attn_all.items() if k in ('Wq', 'bq', 'Wk', 'bk', 'Wv', 'bv', 'Wp', 'bp')}
    del _L0_attn_all

    def _L0_ffn_setup():
        import jax, jax.numpy as jnp
        import numpy as np
        N_CONST = 6
        PARTITIONS_OF_6 = [(6,), (5, 1), (4, 2), (4, 1, 1), (3, 3), (3, 2, 1), (3, 1, 1, 1), (2, 2, 2), (2, 2, 1, 1), (2, 1, 1, 1, 1), (1, 1, 1, 1, 1, 1)]
        N_EXPERTS = 6
        TOP_K = 2

        def _partition_weights():
            w = np.zeros((len(PARTITIONS_OF_6), N_EXPERTS), dtype=np.float32)
            for i, partition in enumerate(PARTITIONS_OF_6):
                for j, part in enumerate(partition):
                    if j < N_EXPERTS:
                        w[i, j] = part / N_CONST
            return jnp.asarray(w)
        key = jax.random.key(seed)
        ks = jax.random.split(key, 6)
        B, S, D, F, E, P = (32, 512, 128, 341, 6, 11)
        scale_in = 1.0 / np.sqrt(D)
        scale_hid = 1.0 / np.sqrt(F)
        return {'x': jax.random.normal(ks[0], (B, S, D), dtype=jnp.float32), 'router_w': jax.random.normal(ks[1], (P, D), dtype=jnp.float32) * scale_in, 'W1': jax.random.normal(ks[2], (E, D, F), dtype=jnp.float32) * scale_in, 'b1': jax.random.normal(ks[3], (E, F), dtype=jnp.float32) * 0.01, 'W2': jax.random.normal(ks[4], (E, F, D), dtype=jnp.float32) * scale_hid, 'b2': jax.random.normal(ks[5], (E, D), dtype=jnp.float32) * 0.01}
    _L0_ffn_all = _L0_ffn_setup()
    _L0_ffn_in = {k: v for k, v in _L0_ffn_all.items() if k in ('router_w', 'W1', 'b1', 'W2', 'b2')}
    del _L0_ffn_all

    def _L1_attn_setup():
        import jax, jax.numpy as jnp
        import numpy as np
        B, L = (2, 512)
        IN_DIM, HD_DIM, STATE_DIM = (128, 1024, 16)
        NUM_PATHS, ENT_DEPTH = (2, 2)
        ENT_STRENGTH, WALK_TIME = (0.3, 1.0)

        def _glorot(key, shape):
            lim = np.sqrt(6.0 / (shape[0] + shape[1]))
            return jax.random.uniform(key, shape, jnp.float32, -lim, lim)

        def _qhd_forward(x, input_proj, output_proj, a_log, b_proj, c_proj, dt_proj, skip_proj, amp_r, amp_i, rot, walk_h):
            Bb, Ll, _ = x.shape
            K = amp_r.shape[0]
            dt = jax.nn.softplus(dt_proj)
            hd = jnp.einsum('bld,dh->blh', x, input_proj)
            Xf = jnp.fft.rfft(hd, axis=1)
            F = Xf.shape[1]
            band = jnp.clip(jnp.arange(F) * K // F, 0, K - 1)
            masks = (band[None, :] == jnp.arange(K)[:, None]).astype(hd.dtype)
            x_paths = jnp.fft.irfft(Xf[None] * masks[:, None, :, None], n=Ll, axis=2)
            a = -jnp.exp(a_log)
            dt_bar = jnp.mean(dt)
            t_idx = jnp.arange(Ll, dtype=hd.dtype)
            decay = jnp.exp(a[None, :] * dt_bar * t_idx[:, None])
            Bt = jnp.einsum('kbld,dn->kbln', x_paths * dt, b_proj)
            n2 = 2 * Ll
            h = jnp.fft.irfft(jnp.fft.rfft(Bt, n=n2, axis=2) * jnp.fft.rfft(decay, n=n2, axis=0), n=n2, axis=2)[:, :, :Ll, :]
            y_paths = jnp.einsum('kbln,dn->kbld', h, c_proj)
            alpha = amp_r.astype(jnp.complex64) + 1j * amp_i.astype(jnp.complex64)
            A = 1j * (ENT_STRENGTH * WALK_TIME) * walk_h.astype(jnp.complex64)
            U = jnp.eye(K, dtype=jnp.complex64) + A + A @ A / 2.0 + A @ A @ A / 6.0
            for d in range(rot.shape[0]):
                alpha = jnp.exp(1j * rot[d].astype(jnp.complex64)) * alpha
                alpha = U @ alpha
            w = jnp.abs(alpha) ** 2
            w = (w / jnp.sum(w)).astype(hd.dtype)
            y = jnp.einsum('k,kbld->bld', w, y_paths) + hd * skip_proj
            return jnp.einsum('blh,hd->bld', y, output_proj)
        key = jax.random.key(seed)
        ks = jax.random.split(key, 10)
        x = jax.random.normal(ks[0], (B, L, IN_DIM), jnp.float32)
        input_proj = _glorot(ks[1], (IN_DIM, HD_DIM))
        output_proj = _glorot(ks[2], (HD_DIM, IN_DIM))
        a_log = jax.random.uniform(ks[3], (STATE_DIM,), jnp.float32, -4.0, -1.0)
        b_proj = _glorot(ks[4], (HD_DIM, STATE_DIM))
        c_proj = _glorot(ks[5], (HD_DIM, STATE_DIM))
        dt_proj = jnp.full((HD_DIM,), 0.01, jnp.float32)
        skip_proj = jnp.ones((HD_DIM,), jnp.float32)
        amplitudes_real = jnp.full((NUM_PATHS,), 1.0 / np.sqrt(NUM_PATHS), jnp.float32)
        amplitudes_imag = 0.01 * jax.random.normal(ks[6], (NUM_PATHS,), jnp.float32)
        rotation_angles = jax.random.uniform(ks[7], (ENT_DEPTH, NUM_PATHS), jnp.float32, 0.0, 2.0 * np.pi)
        wh, _ = jnp.linalg.qr(jax.random.normal(ks[8], (NUM_PATHS, NUM_PATHS), jnp.float32))
        return dict(x=x, input_proj=input_proj, output_proj=output_proj, a_log=a_log, b_proj=b_proj, c_proj=c_proj, dt_proj=dt_proj, skip_proj=skip_proj, amplitudes_real=amplitudes_real, amplitudes_imag=amplitudes_imag, rotation_angles=rotation_angles, walk_hamiltonian=wh)
    _L1_attn_all = _L1_attn_setup()
    _L1_attn_in = {k: v for k, v in _L1_attn_all.items() if k in ('input_proj', 'output_proj', 'a_log', 'b_proj', 'c_proj', 'dt_proj', 'skip_proj', 'amplitudes_real', 'amplitudes_imag', 'rotation_angles', 'walk_hamiltonian')}
    del _L1_attn_all

    def _L1_ffn_setup():
        import jax, jax.numpy as jnp
        import numpy as np
        D_MODEL = 128
        D_FF = 512
        N_HEADS = 8
        N_EXPERTS = 8
        TOP_K = 2
        CAPACITY_FACTOR = 1.6
        BATCH = 1024
        SEQ = 16
        LN_EPS = 1e-05

        def _layernorm(x, g, b):
            mu = x.mean(-1, keepdims=True)
            var = ((x - mu) ** 2).mean(-1, keepdims=True)
            return (x - mu) * jax.lax.rsqrt(var + LN_EPS) * g + b

        def _moe(xf, router_w, router_b, w1, b1, w2, b2):
            T = xf.shape[0]
            probs = jax.nn.softmax(xf @ router_w + router_b, axis=-1)
            _, topk_idx = jax.lax.top_k(probs, TOP_K)
            capacity = int(np.ceil(T * CAPACITY_FACTOR / N_EXPERTS))
            out = jnp.zeros_like(xf)
            tok = jnp.arange(T)
            for i in range(N_EXPERTS):
                mask = (topk_idx == i).any(-1)
                pos = jnp.where(mask, tok, T)
                sel = jnp.sort(pos)[:capacity]
                xi = xf[jnp.minimum(sel, T - 1)]
                hi = jax.nn.gelu(xi @ w1[i] + b1[i], approximate=False)
                yi = hi @ w2[i] + b2[i]
                out = out.at[sel].set(yi, mode='drop')
            return out
        key = jax.random.key(seed)
        ks = jax.random.split(key, 24)
        s = 0.02
        d, f, e = (D_MODEL, D_FF, N_EXPERTS)
        inp = {'x': jax.random.normal(ks[0], (BATCH, SEQ, d), dtype=jnp.float32), 'ln1_g': jnp.ones((d,), jnp.float32), 'ln1_b': jnp.zeros((d,), jnp.float32), 'ln2_g': jnp.ones((d,), jnp.float32), 'ln2_b': jnp.zeros((d,), jnp.float32), 'wq': jax.random.normal(ks[1], (d, d)) * s, 'bq': jnp.zeros((d,)), 'wk': jax.random.normal(ks[2], (d, d)) * s, 'bk': jnp.zeros((d,)), 'wv': jax.random.normal(ks[3], (d, d)) * s, 'bv': jnp.zeros((d,)), 'wo': jax.random.normal(ks[4], (d, d)) * s, 'bo': jnp.zeros((d,)), 'router_w': jax.random.normal(ks[5], (d, e)) * s, 'router_b': jnp.zeros((e,)), 'w1': jax.random.normal(ks[6], (e, d, f)) * s, 'b1': jnp.zeros((e, f)), 'w2': jax.random.normal(ks[7], (e, f, d)) * s, 'b2': jnp.zeros((e, d))}
        return inp
    _L1_ffn_all = _L1_ffn_setup()
    _L1_ffn_in = {k: v for k, v in _L1_ffn_all.items() if k in ('ln1_g', 'ln1_b', 'ln2_g', 'ln2_b', 'wq', 'bq', 'wk', 'bk', 'wv', 'bv', 'wo', 'bo', 'router_w', 'router_b', 'w1', 'b1', 'w2', 'b2')}
    del _L1_ffn_all
    return {'x': x, 'L0_tok_token_table': _L0_tok_in['token_table'], 'L0_tok_pos_table': _L0_tok_in['pos_table'], 'L0_tok_row_table': _L0_tok_in['row_table'], 'L0_tok_col_table': _L0_tok_in['col_table'], 'L0_tok_w_spatial': _L0_tok_in['w_spatial'], 'L0_tok_ln_gamma': _L0_tok_in['ln_gamma'], 'L0_tok_ln_beta': _L0_tok_in['ln_beta'], 'L0_attn_Wq': _L0_attn_in['Wq'], 'L0_attn_bq': _L0_attn_in['bq'], 'L0_attn_Wk': _L0_attn_in['Wk'], 'L0_attn_bk': _L0_attn_in['bk'], 'L0_attn_Wv': _L0_attn_in['Wv'], 'L0_attn_bv': _L0_attn_in['bv'], 'L0_attn_Wp': _L0_attn_in['Wp'], 'L0_attn_bp': _L0_attn_in['bp'], 'L0_ffn_router_w': _L0_ffn_in['router_w'], 'L0_ffn_W1': _L0_ffn_in['W1'], 'L0_ffn_b1': _L0_ffn_in['b1'], 'L0_ffn_W2': _L0_ffn_in['W2'], 'L0_ffn_b2': _L0_ffn_in['b2'], 'L1_attn_input_proj': _L1_attn_in['input_proj'], 'L1_attn_output_proj': _L1_attn_in['output_proj'], 'L1_attn_a_log': _L1_attn_in['a_log'], 'L1_attn_b_proj': _L1_attn_in['b_proj'], 'L1_attn_c_proj': _L1_attn_in['c_proj'], 'L1_attn_dt_proj': _L1_attn_in['dt_proj'], 'L1_attn_skip_proj': _L1_attn_in['skip_proj'], 'L1_attn_amplitudes_real': _L1_attn_in['amplitudes_real'], 'L1_attn_amplitudes_imag': _L1_attn_in['amplitudes_imag'], 'L1_attn_rotation_angles': _L1_attn_in['rotation_angles'], 'L1_attn_walk_hamiltonian': _L1_attn_in['walk_hamiltonian'], 'L1_ffn_ln1_g': _L1_ffn_in['ln1_g'], 'L1_ffn_ln1_b': _L1_ffn_in['ln1_b'], 'L1_ffn_ln2_g': _L1_ffn_in['ln2_g'], 'L1_ffn_ln2_b': _L1_ffn_in['ln2_b'], 'L1_ffn_wq': _L1_ffn_in['wq'], 'L1_ffn_bq': _L1_ffn_in['bq'], 'L1_ffn_wk': _L1_ffn_in['wk'], 'L1_ffn_bk': _L1_ffn_in['bk'], 'L1_ffn_wv': _L1_ffn_in['wv'], 'L1_ffn_bv': _L1_ffn_in['bv'], 'L1_ffn_wo': _L1_ffn_in['wo'], 'L1_ffn_bo': _L1_ffn_in['bo'], 'L1_ffn_router_w': _L1_ffn_in['router_w'], 'L1_ffn_router_b': _L1_ffn_in['router_b'], 'L1_ffn_w1': _L1_ffn_in['w1'], 'L1_ffn_b1': _L1_ffn_in['b1'], 'L1_ffn_w2': _L1_ffn_in['w2'], 'L1_ffn_b2': _L1_ffn_in['b2']}

def reference(x, L0_tok_token_table, L0_tok_pos_table, L0_tok_row_table, L0_tok_col_table, L0_tok_w_spatial, L0_tok_ln_gamma, L0_tok_ln_beta, L0_attn_Wq, L0_attn_bq, L0_attn_Wk, L0_attn_bk, L0_attn_Wv, L0_attn_bv, L0_attn_Wp, L0_attn_bp, L0_ffn_router_w, L0_ffn_W1, L0_ffn_b1, L0_ffn_W2, L0_ffn_b2, L1_attn_input_proj, L1_attn_output_proj, L1_attn_a_log, L1_attn_b_proj, L1_attn_c_proj, L1_attn_dt_proj, L1_attn_skip_proj, L1_attn_amplitudes_real, L1_attn_amplitudes_imag, L1_attn_rotation_angles, L1_attn_walk_hamiltonian, L1_ffn_ln1_g, L1_ffn_ln1_b, L1_ffn_ln2_g, L1_ffn_ln2_b, L1_ffn_wq, L1_ffn_bq, L1_ffn_wk, L1_ffn_bk, L1_ffn_wv, L1_ffn_bv, L1_ffn_wo, L1_ffn_bo, L1_ffn_router_w, L1_ffn_router_b, L1_ffn_w1, L1_ffn_b1, L1_ffn_w2, L1_ffn_b2):
    import jax
    import jax.numpy as jnp

    def _L0_tok_ref(input_ids, token_table, pos_table, row_table, col_table, w_spatial, ln_gamma, ln_beta):
        import jax, jax.numpy as jnp
        import numpy as np
        PAD, BOS, EOS, ROW, SEP = (10, 11, 12, 13, 14)
        VOCAB, D_MODEL, MAX_SEQ, MAX_H, MAX_W = (15, 128, 1024, 30, 30)
        B, T = (16, 1024)
        LN_EPS = 1e-05

        def _build_2d_ids(ids):

            def step(carry, tok):
                row, col, in_grid = carry
                is_bos = tok == BOS
                is_sep = tok == SEP
                is_row = tok == ROW
                is_end = (tok == EOS) | (tok == PAD)
                grid_color = in_grid & (tok >= 0) & (tok <= 9)
                emit_r = jnp.where(grid_color, row, 0)
                emit_c = jnp.where(grid_color, col, 0)
                n_grid = jnp.where(is_bos, True, jnp.where(is_end, False, in_grid))
                n_row = jnp.where(is_bos | is_sep, 0, jnp.where(is_row, row + 1, row))
                n_col = jnp.where(is_bos | is_sep | is_row, 0, jnp.where(grid_color, col + 1, col))
                return ((n_row, n_col, n_grid), (emit_r, emit_c))

            def scan_one(seq):
                init = (jnp.int32(0), jnp.int32(0), jnp.bool_(False))
                _, (r, c) = jax.lax.scan(step, init, seq)
                return (r, c)
            r, c = jax.vmap(scan_one)(ids)
            return (jnp.clip(r, 0, MAX_H - 1), jnp.clip(c, 0, MAX_W - 1))
        Bv, Tv = input_ids.shape
        tok_emb = token_table[input_ids]
        pos_emb = pos_table[:Tv][None, :, :]
        row_ids, col_ids = _build_2d_ids(input_ids)
        rc = jnp.concatenate([row_table[row_ids], col_table[col_ids]], axis=-1)
        spatial = jnp.einsum('btd,ed->bte', rc, w_spatial)
        mask = ((input_ids >= 0) & (input_ids <= 9)).astype(tok_emb.dtype)[..., None]
        x = tok_emb + pos_emb + spatial * mask
        mu = jnp.mean(x, axis=-1, keepdims=True)
        var = jnp.var(x, axis=-1, keepdims=True)
        x = (x - mu) * jax.lax.rsqrt(var + LN_EPS) * ln_gamma + ln_beta
        return x

    def _L0_attn_ref(x, Wq, bq, Wk, bk, Wv, bv, Wp, bp):
        import jax, jax.numpy as jnp
        import numpy as np
        B, N, E, H = (4, 512, 128, 8)
        b, n, e = x.shape
        h = Wq.shape[1] // e

        def split_heads(t):
            return jnp.transpose(t.reshape(b, n, e, h), (0, 3, 2, 1))
        q = split_heads(x @ Wq + bq)
        k = split_heads(x @ Wk + bk)
        v = split_heads(x @ Wv + bv)
        scale = 1.0 / np.sqrt(n).astype(np.float32)
        att = jnp.einsum('bhen,bhfn->bhef', q, k) * scale
        att = jax.nn.softmax(att, axis=-1)
        y = jnp.einsum('bhef,bhfn->bhen', att, v)
        y = jnp.transpose(y, (0, 2, 1, 3)).reshape(b, n, e * h)
        return y @ Wp + bp

    def _L0_ffn_ref(x, router_w, W1, b1, W2, b2):
        import jax, jax.numpy as jnp
        import numpy as np
        N_CONST = 6
        PARTITIONS_OF_6 = [(6,), (5, 1), (4, 2), (4, 1, 1), (3, 3), (3, 2, 1), (3, 1, 1, 1), (2, 2, 2), (2, 2, 1, 1), (2, 1, 1, 1, 1), (1, 1, 1, 1, 1, 1)]
        N_EXPERTS = 6
        TOP_K = 2

        def _partition_weights():
            w = np.zeros((len(PARTITIONS_OF_6), N_EXPERTS), dtype=np.float32)
            for i, partition in enumerate(PARTITIONS_OF_6):
                for j, part in enumerate(partition):
                    if j < N_EXPERTS:
                        w[i, j] = part / N_CONST
            return jnp.asarray(w)
        pw = _partition_weights()
        token_repr = x.mean(axis=1)
        logits = token_repr @ router_w.T
        probs = jax.nn.softmax(logits, axis=-1)
        topk_vals, topk_idx = jax.lax.top_k(probs, TOP_K)
        topk_vals = topk_vals / topk_vals.sum(axis=-1, keepdims=True)
        expert_weights = jnp.einsum('bk,bke->be', topk_vals, pw[topk_idx])
        expert_weights = jnp.where(expert_weights > 1e-06, expert_weights, 0.0)
        h = jax.nn.gelu(jnp.einsum('bsd,edf->ebsf', x, W1) + b1[:, None, None, :], approximate=False)
        out_e = jnp.einsum('ebsf,efd->ebsd', h, W2) + b2[:, None, None, :]
        return jnp.einsum('be,ebsd->bsd', expert_weights, out_e)

    def _L1_attn_ref(x, input_proj, output_proj, a_log, b_proj, c_proj, dt_proj, skip_proj, amplitudes_real, amplitudes_imag, rotation_angles, walk_hamiltonian):
        import jax, jax.numpy as jnp
        import numpy as np
        B, L = (2, 512)
        IN_DIM, HD_DIM, STATE_DIM = (128, 1024, 16)
        NUM_PATHS, ENT_DEPTH = (2, 2)
        ENT_STRENGTH, WALK_TIME = (0.3, 1.0)

        def _glorot(key, shape):
            lim = np.sqrt(6.0 / (shape[0] + shape[1]))
            return jax.random.uniform(key, shape, jnp.float32, -lim, lim)

        def _qhd_forward(x, input_proj, output_proj, a_log, b_proj, c_proj, dt_proj, skip_proj, amp_r, amp_i, rot, walk_h):
            Bb, Ll, _ = x.shape
            K = amp_r.shape[0]
            dt = jax.nn.softplus(dt_proj)
            hd = jnp.einsum('bld,dh->blh', x, input_proj)
            Xf = jnp.fft.rfft(hd, axis=1)
            F = Xf.shape[1]
            band = jnp.clip(jnp.arange(F) * K // F, 0, K - 1)
            masks = (band[None, :] == jnp.arange(K)[:, None]).astype(hd.dtype)
            x_paths = jnp.fft.irfft(Xf[None] * masks[:, None, :, None], n=Ll, axis=2)
            a = -jnp.exp(a_log)
            dt_bar = jnp.mean(dt)
            t_idx = jnp.arange(Ll, dtype=hd.dtype)
            decay = jnp.exp(a[None, :] * dt_bar * t_idx[:, None])
            Bt = jnp.einsum('kbld,dn->kbln', x_paths * dt, b_proj)
            n2 = 2 * Ll
            h = jnp.fft.irfft(jnp.fft.rfft(Bt, n=n2, axis=2) * jnp.fft.rfft(decay, n=n2, axis=0), n=n2, axis=2)[:, :, :Ll, :]
            y_paths = jnp.einsum('kbln,dn->kbld', h, c_proj)
            alpha = amp_r.astype(jnp.complex64) + 1j * amp_i.astype(jnp.complex64)
            A = 1j * (ENT_STRENGTH * WALK_TIME) * walk_h.astype(jnp.complex64)
            U = jnp.eye(K, dtype=jnp.complex64) + A + A @ A / 2.0 + A @ A @ A / 6.0
            for d in range(rot.shape[0]):
                alpha = jnp.exp(1j * rot[d].astype(jnp.complex64)) * alpha
                alpha = U @ alpha
            w = jnp.abs(alpha) ** 2
            w = (w / jnp.sum(w)).astype(hd.dtype)
            y = jnp.einsum('k,kbld->bld', w, y_paths) + hd * skip_proj
            return jnp.einsum('blh,hd->bld', y, output_proj)
        return _qhd_forward(x, input_proj, output_proj, a_log, b_proj, c_proj, dt_proj, skip_proj, amplitudes_real, amplitudes_imag, rotation_angles, walk_hamiltonian)

    def _L1_ffn_ref(x, ln1_g, ln1_b, ln2_g, ln2_b, wq, bq, wk, bk, wv, bv, wo, bo, router_w, router_b, w1, b1, w2, b2):
        import jax, jax.numpy as jnp
        import numpy as np
        D_MODEL = 128
        D_FF = 512
        N_HEADS = 8
        N_EXPERTS = 8
        TOP_K = 2
        CAPACITY_FACTOR = 1.6
        BATCH = 1024
        SEQ = 16
        LN_EPS = 1e-05

        def _layernorm(x, g, b):
            mu = x.mean(-1, keepdims=True)
            var = ((x - mu) ** 2).mean(-1, keepdims=True)
            return (x - mu) * jax.lax.rsqrt(var + LN_EPS) * g + b

        def _moe(xf, router_w, router_b, w1, b1, w2, b2):
            T = xf.shape[0]
            probs = jax.nn.softmax(xf @ router_w + router_b, axis=-1)
            _, topk_idx = jax.lax.top_k(probs, TOP_K)
            capacity = int(np.ceil(T * CAPACITY_FACTOR / N_EXPERTS))
            out = jnp.zeros_like(xf)
            tok = jnp.arange(T)
            for i in range(N_EXPERTS):
                mask = (topk_idx == i).any(-1)
                pos = jnp.where(mask, tok, T)
                sel = jnp.sort(pos)[:capacity]
                xi = xf[jnp.minimum(sel, T - 1)]
                hi = jax.nn.gelu(xi @ w1[i] + b1[i], approximate=False)
                yi = hi @ w2[i] + b2[i]
                out = out.at[sel].set(yi, mode='drop')
            return out
        B, S, D = x.shape
        dk = D // N_HEADS
        h = _layernorm(x, ln1_g, ln1_b)
        q = (h @ wq + bq).reshape(B, S, N_HEADS, dk)
        k = (h @ wk + bk).reshape(B, S, N_HEADS, dk)
        v = (h @ wv + bv).reshape(B, S, N_HEADS, dk)
        scores = jnp.einsum('bqhd,bkhd->bhqk', q, k) / np.sqrt(dk).astype(np.float32)
        attn = jax.nn.softmax(scores, axis=-1)
        ctx = jnp.einsum('bhqk,bkhd->bqhd', attn, v).reshape(B, S, D)
        x = x + ctx @ wo + bo
        h2 = _layernorm(x, ln2_g, ln2_b)
        moe_out = _moe(h2.reshape(-1, D), router_w, router_b, w1, b1, w2, b2)
        return x + moe_out.reshape(B, S, D)
    h = _L0_tok_ref(x, L0_tok_token_table, L0_tok_pos_table, L0_tok_row_table, L0_tok_col_table, L0_tok_w_spatial, L0_tok_ln_gamma, L0_tok_ln_beta)
    h = h + _L0_attn_ref(_layernorm(h, axis=-1), L0_attn_Wq, L0_attn_bq, L0_attn_Wk, L0_attn_bk, L0_attn_Wv, L0_attn_bv, L0_attn_Wp, L0_attn_bp)
    h = h + _L0_ffn_ref(_layernorm(h, axis=-1), L0_ffn_router_w, L0_ffn_W1, L0_ffn_b1, L0_ffn_W2, L0_ffn_b2)
    h = h + _L1_attn_ref(_layernorm(h, axis=-1), L1_attn_input_proj, L1_attn_output_proj, L1_attn_a_log, L1_attn_b_proj, L1_attn_c_proj, L1_attn_dt_proj, L1_attn_skip_proj, L1_attn_amplitudes_real, L1_attn_amplitudes_imag, L1_attn_rotation_angles, L1_attn_walk_hamiltonian)
    h = h + _L1_ffn_ref(_layernorm(h, axis=-1), L1_ffn_ln1_g, L1_ffn_ln1_b, L1_ffn_ln2_g, L1_ffn_ln2_b, L1_ffn_wq, L1_ffn_bq, L1_ffn_wk, L1_ffn_bk, L1_ffn_wv, L1_ffn_bv, L1_ffn_wo, L1_ffn_bo, L1_ffn_router_w, L1_ffn_router_b, L1_ffn_w1, L1_ffn_b1, L1_ffn_w2, L1_ffn_b2)
    return h

_drawn_inputs = setup_inputs


def setup_inputs(seed=0):
    import zlib

    import numpy as np

    out = dict(_drawn_inputs(seed))
    spreads = {'L0_tok_ln_gamma': (1.0, 0.2),
     'L0_tok_ln_beta': (0.0, 0.1),
     'L1_attn_dt_proj': (0.009999999776482582, 0.6),
     'L1_attn_skip_proj': (1.0, 0.2),
     'L1_attn_amplitudes_real': (0.7071067690849304, 0.6),
     'L1_ffn_ln1_g': (1.0, 0.6),
     'L1_ffn_ln1_b': (0.0, 0.8),
     'L1_ffn_ln2_g': (1.0, 0.6),
     'L1_ffn_ln2_b': (0.0, 0.532),
     'L1_ffn_bq': (0.0, 0.8),
     'L1_ffn_bk': (0.0, 2.0),
     'L1_ffn_bv': (0.0, 0.645),
     'L1_ffn_bo': (0.0, 0.1),
     'L1_ffn_router_b': (0.0, 0.1),
     'L1_ffn_b1': (0.0, 0.8),
     'L1_ffn_b2': (0.0, 0.27)}
    factors = {'L0_ffn_b1': 8.0,
     'L0_ffn_b2': 4.985,
     'L1_attn_amplitudes_imag': 8.0,
     'L1_ffn_wq': 8.0,
     'L1_ffn_wk': 8.0,
     'L1_ffn_wv': 4.855,
     'L1_ffn_wo': 3.938,
     'L1_ffn_w1': 2.86}
    for name, (base, spread) in spreads.items():
        noise = np.random.default_rng([zlib.crc32(name.encode()), seed]).standard_normal(out[name].shape)
        drawn = base * np.exp(spread * noise) if base else spread * noise
        out[name] = jnp.asarray(drawn.astype(out[name].dtype))
    for name, factor in factors.items():
        out[name] = (out[name] * factor).astype(out[name].dtype)
    return out
```

```python
import math
from contextlib import ExitStack

import numpy as np

import concourse.bass as bass
from concourse import mybir

F32 = mybir.dt.float32
I32 = mybir.dt.int32
ALU = mybir.AluOpType
ACT = mybir.ActivationFunctionType
X = mybir.AxisListType.X

P = 128
LN_EPS = 1e-5
BOS, EOS, PAD, ROW, SEP = 11, 12, 10, 13, 14
VOCAB, MAX_H, MAX_W = 15, 30, 30
NO_CELL = 99.0
HEADS = 8
ATT_SHIFT = 0.125
FFN_E, FFN_F, PARTS = 6, 341, 11
FFN_ROWS = FFN_E * FFN_F
CHUNKS = -(-FFN_ROWS // P)
STATES = 16
HD = 1024
HDC = HD // P
ENT = 0.3
DK = P // HEADS
MOE_E, MOE_F = 8, 512
MOE_C = MOE_F // P
TABLE_ROWS = 96
SCALE = 1.0 / math.sqrt(P)
TWO_PI = 2.0 * math.pi
ROUND = 1.5 * 2.0 ** 23
PARTITIONS_OF_6 = [(6,), (5, 1), (4, 2), (4, 1, 1), (3, 3), (3, 2, 1), (3, 1, 1, 1), (2, 2, 2),
                   (2, 2, 1, 1), (2, 1, 1, 1, 1), (1, 1, 1, 1, 1, 1)]


def sizes(nb):
    tokens = nb * P
    cap = int(np.ceil(tokens * 1.6 / MOE_E))
    tiles = tokens // P + MOE_E - 1
    return tokens, cap, tiles


def constants(nb):
    tokens, cap, tiles = sizes(nb)
    i = np.arange(P)
    f = np.arange(P // 2 + 1)
    band0 = (f * 2 // len(f)) == 0
    weight = np.where((f == 0) | (f == P // 2), 1.0, 2.0)
    wave = np.cos(2 * np.pi * f[None, None, :] * (i[:, None, None] - i[None, :, None]) / P) * weight / P
    parts = {
        "ident": np.eye(P),
        "centre": np.eye(P) - 1.0 / P,
        "low_band": wave[:, :, band0].sum(-1),
        "high_band": wave[:, :, ~band0].sum(-1),
        "before": (i[:, None] < i[None, :]) * 1.0,
        "ones": np.ones((P, P)),
        "age": np.maximum(i[None, :] - i[:, None], 0) * 1.0,
        "causal": (i[None, :] >= i[:, None]) * 1.0,
        "head_of_row": (i[:, None] // DK == np.arange(HEADS)[None, :]) * 1.0,
        "octet_of_row": (i[:, None] // STATES == np.arange(8)[None, :]) * 1.0,
    }
    key = np.full((P, 1), -7.0)
    key[:VOCAB, 0] = np.arange(VOCAB)
    key[32:32 + MAX_H, 0] = np.arange(MAX_H)
    key[64:64 + MAX_W, 0] = np.arange(MAX_W)
    parts["key"] = key
    spread = np.zeros((P, TABLE_ROWS))
    for r in range(3):
        spread[r, 32 * r:32 * r + 32] = 1.0
    parts["spread"] = spread
    pick = np.zeros((P, FFN_E))
    for r, partition in enumerate(PARTITIONS_OF_6):
        for c, part in enumerate(partition):
            pick[r, c] = part / 6
    parts["partitions"] = pick
    rows = np.zeros((P, CHUNKS * P))
    for e in range(FFN_E):
        rows[e, e * FFN_F:(e + 1) * FFN_F] = 1.0
    parts["expert_of_row"] = rows
    parts["earlier_part"] = np.tile((np.arange(PARTS)[None, :] < np.arange(PARTS)[:, None])
                                    .reshape(1, -1) * 1.0, (P, 1))
    parts["expert_number"] = np.tile(np.arange(1, MOE_E + 1)[None, :] * 1.0, (P, 1))
    pick3 = np.zeros((P, 3 * P))
    for r in range(3):
        pick3[r, r * P:(r + 1) * P] = 1.0 / (P * ATT_SHIFT)
    parts["bias_pick"] = pick3
    parts["token_number"] = i[:, None] + P * np.arange(nb)[None, :] * 1.0
    parts["tile_number"] = np.tile(np.arange(tiles)[None, :] * 1.0, (P, 1))
    where, at = {}, 0
    for name, a in parts.items():
        where[name] = (at, a.shape[1])
        at += a.shape[1]
    return np.concatenate(list(parts.values()), axis=1).astype(np.float32), where


def wait(eng, sem, n, own=False):
    if isinstance(n, int):
        if n > 0:
            eng.wait_ge(sem, n)
        return
    value = eng.to_reg(n)
    if own:
        eng.wait_ge(sem, 1)
    eng.wait_ge(sem, value)


def at(start, n=1):
    return bass.ds(start, n)


def build(nc, io, out, nb, where):
    tokens, cap, tiles = sizes(nb)
    sorted_rows = tiles * P
    groups = nb // 4
    n_const = sum(w for _, w in where.values())
    ids_rows = nc.dram_tensor("ids_rows", (3, nb, P), F32).ap()
    sorted_x = nc.dram_tensor("sorted_x", (sorted_rows, P + 1), F32).ap()

    with ExitStack() as ctx:
        def sb(name, shape, dt=F32):
            return ctx.enter_context(nc.sbuf_tensor(name, shape, dt))

        def sem(name):
            return ctx.enter_context(nc.semaphore(name))

        bank = [ctx.enter_context(nc.psum_tensor(f"bank{k}", [P, 512], F32)) for k in range(8)]
        A, B, C, D, E = bank[0:2], bank[2:4], bank[4:6], bank[6], bank[7]

        con = sb("con", [P, n_const])

        def const(name, rows=P):
            a, w = where[name]
            return con[0:rows, a:a + w]

        ident = const("ident")
        H = sb("H", [P, nb, P])
        wide = sb("wide", [P, nb * (P + 1)])
        H2 = wide[:, 0:nb * P].rearrange("p (b d) -> p b d", d=P)
        named = wide[:].rearrange("p (b d) -> p b d", d=P + 1)
        neg_half = sb("neg_half", [P, 1])

        w1 = sb("w1", [P, MOE_E, MOE_F])
        w2 = sb("w2", [P, MOE_E, MOE_C, P])
        vec = sb("vec", [P, P])
        vecT = sb("vecT", [P, P])
        empty = sb("empty", [P, P + 1])[:]
        dt_col, skip_col = vecT[:, 0:8], vecT[:, 8:16]
        b1, fb1 = vecT[:, 16:48], vecT[:, 48:64]
        part_w, qkv_b = vecT[:, 64:75], vecT[:, 75:78]
        bq_col, bk_col, bv_col = vecT[:, 75:76], vecT[:, 76:77], vecT[:, 77:78]
        g1_col, be1_col, g2_col, be2_col = (vecT[:, k:k + 1] for k in range(78, 82))
        b2 = sb("b2", [P, MOE_E, P])
        f1 = sb("f1", [P, CHUNKS * P])
        f2 = sb("f2", [P, CHUNKS, P])
        fb2 = sb("fb2", [FFN_E, P])
        rowsP = sb("rowsP", [P, 7, P])
        gamma, beta, bp, bo, ctx_bias, pos = (rowsP[:, k, :] for k in range(6))
        table = rowsP[0:TABLE_ROWS, 6, :]
        small = sb("small", [P, 420])
        taken = [0]

        def piece(n):
            taken[0] += n
            assert taken[0] <= 420
            return small[:, taken[0] - n:taken[0]]

        arena = sb("arena", [P, 12544])
        used = [0]

        def room(*shape):
            n = int(np.prod(shape))
            a = arena[:, used[0]:used[0] + n]
            used[0] += n
            assert used[0] <= 12544, used[0]
            if len(shape) == 2:
                return a.rearrange("p (a b) -> p a b", a=shape[0])
            if len(shape) == 3:
                return a.rearrange("p (a b c) -> p a b c", a=shape[0], b=shape[1])
            return a

        wq, wk, wv, wp = room(HEADS, P), room(HEADS, P), room(HEADS, P), room(HEADS, P)
        gws, xws, prob, pts = room(HEADS, P), room(HEADS, P), room(HEADS, P), room(HEADS, P)
        us = room(2, HEADS, P)
        gs, xs, t0, t1, t2 = room(P), room(P), room(P), room(P), room(P)
        onehot = room(2, P)
        raw = [gws, xws, prob]
        raw_bias = room(1024)
        idrow = H2
        grid_room = us.rearrange("p a h d -> p (a h d)")
        grid = [grid_room[0:nb, 136 * k:136 * k + 129] for k in range(13)]

        mx, negm, rsum, rinv = piece(HEADS), piece(HEADS), piece(HEADS), piece(HEADS)
        st1, mv1, ve1, rs1 = piece(6), piece(2), piece(1), piece(1)
        st2, mv2, ve2, rs2, nb2 = piece(6), piece(2), piece(1), piece(1), piece(1)
        st3, mv3, ve3 = piece(6), piece(2), piece(1)
        amp, rot, walk = piece(4), piece(4), piece(4)
        a_log = piece(STATES)
        spin, turns, waves = piece(8), piece(8), piece(8)
        walk2, walk3, u_re, u_im = piece(4), piece(4), piece(4), piece(4)
        al_re, al_im, be_re, be_im, pr0, pr1 = piece(2), piece(2), piece(2), piece(2), piece(4), piece(4)
        path_w, dt_sum, soft0, soft1 = piece(2), piece(1), piece(HDC), piece(HDC)
        rate = piece(STATES)
        mv4, ve4 = piece(8).rearrange("p (b k) -> p b k", k=2), piece(4)
        st4 = piece(24).rearrange("p (b k) -> p b k", k=6)
        token_sum = sb("token_sum", [P, nb])
        rstd, mrstd = sb("rstd", [P, nb]), sb("mrstd", [P, nb])

        con_in, ids_in, proj_in, table_in, rows_in = (
            sem("con_in"), sem("ids_in"), sem("proj_in"), sem("table_in"), sem("rows_in"))
        wp_in, moe_in, ffn_in = sem("wp_in"), sem("moe_in"), sem("ffn_in")
        ids_out = sem("ids_out")
        zeroed, ids_ready, ids_placed = sem("zeroed"), sem("ids_ready"), sem("ids_placed")
        a_prep_pe, a_prep_dve, a_prep_act = sem("a_prep_pe"), sem("a_prep_dve"), sem("a_prep_act")
        bc_done, oh_ready, em_done, em_evac = (
            sem("bc_done"), sem("oh_ready"), sem("em_done"), sem("em_evac"))
        mv1_ready, rs1_ready, t1_ready, h_ready = (
            sem("mv1_ready"), sem("rs1_ready"), sem("t1_ready"), sem("h_ready"))
        mv2_ready, rs2_ready, xs_ready = sem("mv2_ready"), sem("rs2_ready"), sem("xs_ready")
        g_done, g_evac = sem("g_done"), sem("g_evac")
        xw_done, xw_evac = sem("xw_done"), sem("xw_evac")
        gw_done, gw_evac = sem("gw_done"), sem("gw_evac")
        u_done, u_evac = sem("u_done"), sem("u_evac")
        s_done, negmax, exp_done, p_ready = (
            sem("s_done"), sem("negmax"), sem("exp_done"), sem("p_ready"))
        pt_done, pt_evac = sem("pt_done"), sem("pt_evac")
        o_done, o_added, bp_added, mv3_ready, rs3_ready = (
            sem("o_done"), sem("o_added"), sem("bp_added"), sem("mv3_ready"), sem("rs3_ready"))
        vec_zero, vec_in, late_in = sem("vec_zero"), sem("vec_in"), sem("late_in")
        spin_ready, waves_ready = sem("spin_ready"), sem("waves_ready")
        xn_ready, tb_done, xt_evac = sem("xn_ready"), sem("tb_done"), sem("xt_evac")
        rt_pe, rt_dve, rt_act = sem("rt_pe"), sem("rt_dve"), sem("rt_act")
        up_done, gelu_done, hw_ready, down_done = (
            sem("up_done"), sem("gelu_done"), sem("hw_ready"), sem("down_done"))
        ot_ready, ott_done, ffn_added, mvs_ready, rs4_ready = (
            sem("ot_ready"), sem("ott_done"), sem("ffn_added"), sem("mvs_ready"), sem("rs4_ready"))
        cxn_ready, ct_done, cxt_evac, cz_done, cz_evac, c_added = (
            sem("cxn_ready"), sem("ct_done"), sem("cxt_evac"), sem("cz_done"), sem("cz_evac"), sem("c_added"))
        c_pe, c_dve, c_act = sem("c_pe"), sem("c_dve"), sem("c_act")
        (d_mv1, d_rs1, d_n2, d_qkv, d_qv, d_km0, d_km1, d_pv, d_ctx, d_x2, d_lg, d_mv3, d_rs3, d_hadd, d_n3) = (
            sem(f"d_{n}") for n in ("mv1", "rs1", "n2", "qkv", "qv", "km0", "km1", "pv", "ctx", "x2", "lg", "mv3",
                                    "rs3", "hadd", "n3"))
        d_s, d_neg, d_exp, d_pt, d_pts = (sem(f"d_{n}") for n in ("s", "neg", "exp", "pt", "pts"))
        d_t3, d_ts, d_wl = sem("d_t3"), sem("d_ts"), sem("d_wl")
        dw_in, d_prep_pe, d_prep_dve = sem("dw_in"), sem("d_prep_pe"), sem("d_prep_dve")
        e_dve, e_pe, e_act = sem("e_dve"), sem("e_pe"), sem("e_act")
        empty_ready, emptied, scattered = sem("empty_ready"), sem("emptied"), sem("scattered")
        f_in = [sem(f"f_in{k}") for k in range(4)]
        f_out = [sem(f"f_out{k}") for k in range(4)]
        f_t, f_xt, f_w, f_u, f_g, f_d, f_y = (sem(f"f_{n}") for n in ("t", "xt", "w", "u", "g", "d", "y"))
        phase_done = [sem(f"phase_{c}_done") for c in "ABCDE"]
        stored = sem("stored")

        def half(t, h):
            return t.rearrange("p h d -> p (h d)")[:, 512 * h:512 * h + 512]

        def heads4(b, n=P):
            return b[:, 0:4 * n].rearrange("p (h d) -> p h d", h=4)

        def on(b):
            return not isinstance(b, int) or 0 <= b < nb

        def upto(n, most=nb):
            return min(n, most) if isinstance(n, int) else n

        def run_steps(eng, step, first, last, loop_from, loop_to, unroll):
            trips = (loop_to - loop_from + 1) // unroll
            for j in range(first, loop_from):
                step(j, j % unroll)
            if trips > 0:
                with eng.Fori(0, trips) as i:
                    for k in range(unroll):
                        step(i * unroll + (loop_from + k), (loop_from + k) % unroll)
            for j in range(loop_from + max(trips, 0) * unroll, last + 1):
                step(j, j % unroll)

        def finish(eng, phase):
            eng.drain().then_inc(phase_done[phase], 1)

        def enter(eng, phase):
            eng.wait_ge(phase_done[phase - 1], 3 if phase == 5 else 4)

        A_STEPS = dict(first=-5, last=nb + 1, loop_from=3, loop_to=nb - 6, unroll=2)

        ring = [A[0], A[1], B[0], B[1]]
        used[0] = 0
        w4 = room(CHUNKS, nb)
        xn = room(2, 4, P)
        hid, hidw = room(4, 4, P), room(4, 4, P)
        ot = room(4, P)
        b2w = room(nb)
        pl = room(6 * PARTS * PARTS)
        assert used[0] <= 7568
        used[0] = 7568
        ip_raw, op_raw = room(HDC, P), room(HDC, P)
        bproj, cproj = room(HDC, STATES), room(HDC, STATES)
        low_end = used[0]
        decays = room(STATES, P)
        used[0] = 0
        cxn, cxt = room(2, 4, P), room(2, 4, P)
        used[0] = 2048
        zs, zm = room(STATES, nb), room(STATES, nb)
        used[0] = 4096
        ipT = room(HDC, P)
        ops = room(HDC, P + STATES)
        state_w, mixer, back8 = room(P + STATES), room(P), room(8, P)
        hb = ipT.rearrange("p h d -> p (h d)")[:, 0:STATES * nb].rearrange("p (b n) -> p b n", n=STATES)
        hT = arena[:, 0:1024].rearrange("p (q l) -> p q l", l=P)
        cproj8 = arena[:, 2048:3072].rearrange("p (h d) -> p h d", d=P)

        used[0] = low_end + STATES * P
        aq, ak, av, ao = room(P), room(P), room(P), room(P)
        router_w, router_b = room(MOE_E), room(MOE_E)
        used[0] = 0
        logits = room(nb, MOE_E)
        km, pts2 = room(HEADS, P), room(HEADS, P)
        prob2 = room(2, HEADS, P)
        vals = room(4, HEADS, DK + 1)
        turned = room(3, P)
        qT, n2, x2, n3 = room(2, P), room(2, P), room(2, P), room(2, P)
        kT, ctxs, bv_all, be2_all = (room(P) for _ in range(4))
        assert used[0] <= low_end + STATES * P
        mva, mvc, va2, rs2x, mr2x = piece(2), piece(2), piece(2), piece(2), piece(2)
        rsc, mrc, vc, rctx = piece(1), piece(1), piece(1), piece(HEADS)
        sta, stc = piece(6), piece(6)
        used[0] = 512
        probs, count, cmp = room(nb, MOE_E), room(nb, MOE_E), room(nb, MOE_E)
        chosen, kept, final = room(nb, MOE_E), room(nb, MOE_E), room(nb, MOE_E)
        total, running, rank = room(nb, MOE_E), room(nb, MOE_E), room(nb, MOE_E)
        best, slot, total_p, dropped = room(nb), room(nb), room(nb), room(nb)
        slot_i = room(nb).bitcast(I32)
        by_tile = room(tiles, MOE_E)
        tile_e = room(tiles)
        table_i = room(tiles).bitcast(I32)
        filled, ends, starts, base = piece(8), piece(8), piece(8), piece(8)
        tile_x, tile_y = room(4, P + 1), room(4, P)
        tile_token = room(4).bitcast(I32)
        tile_xT = room(2, P)
        tile_w1 = room(2, MOE_F)
        tile_b1 = room(2, MOE_C)
        tile_h = room(2, MOE_C, P)

        def group_rows(t, g):
            return t[:, at(4 * g, 4), :]

        def run_groups(eng, body, last, peeled=2):
            trips = (last - 2 - peeled) // 2
            for g in range(peeled):
                body(g, g % 2)
            if trips > 0:
                with eng.Fori(0, trips) as i:
                    for k in range(2):
                        body(i * 2 + (peeled + k), k)
            for g in range(peeled + 2 * max(trips, 0), last):
                body(g, g % 2)

        def ongroup(g):
            return not isinstance(g, int) or 0 <= g < groups

        block = ctx.enter_context(nc.Block())

        ffn_b1 = io["L0_ffn_b1"].rearrange("e f -> (e f)")

        D_STEPS = dict(first=-4, last=nb + 6, loop_from=8, loop_to=nb - 5, unroll=4)

        def run_tiles(eng, step):
            full = (tiles - 2) // 4
            for i in range(-1, 2):
                for k in range(4):
                    step(i, k)
            if full > 2:
                with eng.Fori(2, full) as i:
                    for k in range(4):
                        step(i, k)
            for i in range(max(full, 2), -(-(tiles + 2) // 4)):
                for k in range(4):
                    step(i, k)

        def ontile(t):
            return not isinstance(t, int) or 0 <= t < tiles

        @block.sync
        def _(sp):
            sp.dma_start(grid[0].bitcast(I32)[:, 0:P], io["x"]).then_inc(ids_in, 16)
            sp.dma_start(con[:], io["constants"]).then_inc(con_in, 16)
            for k, n in enumerate("qkv"):
                sp.dma_start(raw[k].rearrange("p h d -> p (h d)"), io[f"L0_attn_W{n}"]).then_inc(proj_in, 16)
                sp.dma_start(raw_bias[k:k + 1, :], io[f"L0_attn_b{n}"].unsqueeze(0)).then_inc(proj_in, 16)
            for dst, n in ((amp[:, 0:2], "amplitudes_real"), (amp[:, 2:4], "amplitudes_imag"), (a_log, "a_log")):
                sp.dma_start(dst, io["L1_attn_" + n].partition_broadcast(P)).then_inc(late_in, 16)
            for dst, n in ((rot, "rotation_angles"), (walk, "walk_hamiltonian")):
                sp.dma_start(dst, io["L1_attn_" + n].rearrange("a b -> (a b)").partition_broadcast(P)).then_inc(late_in, 16)
            sp.wait_ge(zeroed, 2)
            sp.dma_start(table[0:VOCAB, :], io["L0_tok_token_table"]).then_inc(table_in, 16)
            sp.dma_start(t1[32:32 + MAX_H, 0:64], io["L0_tok_row_table"]).then_inc(table_in, 16)
            sp.dma_start(t1[64:64 + MAX_W, 64:128], io["L0_tok_col_table"]).then_inc(table_in, 16)
            sp.dma_start(t0, io["L0_tok_w_spatial"]).then_inc(table_in, 16)
            for k, n in enumerate(["L0_tok_ln_gamma", "L0_tok_ln_beta", "L0_attn_bp", "L1_ffn_bo"]):
                sp.dma_start(rowsP[:, k, :], io[n].partition_broadcast(P)).then_inc(rows_in, 16)
            sp.dma_start(pos, io["L0_tok_pos_table"][0:P, :]).then_inc(rows_in, 16)
            sp.dma_start(wp, io["L0_attn_Wp"].rearrange("(h n) d -> n h d", h=HEADS)).then_inc(wp_in, 16)
            for r, a in ((0, io["L1_attn_dt_proj"].rearrange("(c p) -> c p", p=P)),
                         (8, io["L1_attn_skip_proj"].rearrange("(c p) -> c p", p=P)),
                         (16, io["L1_ffn_b1"].rearrange("e (c p) -> (e c) p", p=P)),
                         (48, ffn_b1[0:15 * P].rearrange("(c p) -> c p", p=P)),
                         (64, io["L0_ffn_router_w"]), (75, io["L1_ffn_bq"].unsqueeze(0)),
                         (76, io["L1_ffn_bk"].unsqueeze(0)), (77, io["L1_ffn_bv"].unsqueeze(0)),
                         (78, io["L1_ffn_ln1_g"].unsqueeze(0)), (79, io["L1_ffn_ln1_b"].unsqueeze(0)),
                         (80, io["L1_ffn_ln2_g"].unsqueeze(0)), (81, io["L1_ffn_ln2_b"].unsqueeze(0))):
                sp.dma_start(vec[r:r + a.shape[0], :], a).then_inc(vec_in, 16)
            sp.dma_start(vec[63:64, 0:FFN_ROWS - 15 * P], ffn_b1[15 * P:FFN_ROWS].unsqueeze(0)).then_inc(vec_in, 16)
            sp.wait_ge(ids_ready, 1)
            for k in range(3):
                sp.dma_start(ids_rows[k], grid[k][:, 0:P]).then_inc(ids_out, 16)
            sp.wait_ge(ids_out, 48)
            sp.dma_start(idrow[0:3, :, :], ids_rows).then_inc(ids_placed, 16)
            sp.dma_start(f1[:, 0:FFN_ROWS].rearrange("p (e f) -> p e f", e=FFN_E),
                         io["L0_ffn_W1"].rearrange("e d f -> d e f")).then_inc(ffn_in, 16)
            w2_rows = io["L0_ffn_W2"].rearrange("e f d -> (e f) d")
            sp.dma_start(f2[:, 0:15, :], w2_rows[0:15 * P, :].rearrange("(c p) d -> p c d", p=P)).then_inc(ffn_in, 16)
            sp.dma_start(f2[0:FFN_ROWS - 15 * P, 15, :], w2_rows[15 * P:FFN_ROWS, :]).then_inc(ffn_in, 16)
            sp.dma_start(fb2[:], io["L0_ffn_b2"]).then_inc(ffn_in, 16)
            sp.dma_start(w1[:], io["L1_ffn_w1"].rearrange("e d f -> d e f")).then_inc(moe_in, 16)
            sp.dma_start(w2[:], io["L1_ffn_w2"].rearrange("e (c f) d -> f e c d", c=MOE_C)).then_inc(moe_in, 16)
            sp.dma_start(b2[:], io["L1_ffn_b2"].rearrange("e d -> (e d)").partition_broadcast(P)
                         .rearrange("p (e d) -> p e d", e=MOE_E)).then_inc(moe_in, 16)
            sp.wait_ge(phase_done[0], 4)
            sp.dma_start(ip_raw, io["L1_attn_input_proj"].rearrange("d (c p) -> d c p", p=P)).then_inc(late_in, 16)
            sp.dma_start(op_raw, io["L1_attn_output_proj"].rearrange("(c p) d -> p c d", p=P)).then_inc(late_in, 16)
            sp.dma_start(bproj, io["L1_attn_b_proj"].rearrange("(c p) n -> p c n", p=P)).then_inc(late_in, 16)
            sp.dma_start(cproj, io["L1_attn_c_proj"].rearrange("(c p) n -> p c n", p=P)).then_inc(late_in, 16)
            sp.wait_ge(empty_ready, 1)
            sp.dma_start(sorted_x.rearrange("(p c) d -> p c d", p=P),
                         empty.unsqueeze(1).broadcast_to([P, tiles, P + 1])).then_inc(emptied, 16)
            sp.wait_ge(phase_done[1], 4)
            for dst, n in ((aq, "wq"), (ak, "wk"), (av, "wv"), (ao, "wo"), (router_w, "router_w")):
                sp.dma_start(dst, io["L1_ffn_" + n]).then_inc(dw_in, 16)
            sp.dma_start(router_b, io["L1_ffn_router_b"].partition_broadcast(P)).then_inc(dw_in, 16)
            with sp.Fori(0, groups) as g:
                sp.wait_ge(d_hadd, 4 * g + 4)
                sp.dma_start(out[at(4 * g, 4), :, :].rearrange("b t d -> t b d"),
                             H[:, at(4 * g, 4), :]).then_inc(stored, 16)
            sp.wait_ge(scattered, 16 * nb)

            def tile(i, k):
                t = 4 * i + k
                if ontile(t + 3):
                    wait(sp, f_t, t, own=True)
                    wait(sp, f_w, t)
                    n = (k + 3) % 4
                    sp.dma_start(tile_x[:, n, :], sorted_x[at((t + 3) * P, P), :]).then_inc(f_in[n], 16)

            run_tiles(sp, tile)
            sp.wait_ge(stored, 16 * groups)

        @block.gpsimd
        def _(pool):
            pool.memset(t1, 0.0)
            pool.memset(rowsP[:, 6, :], 0.0)
            pool.memset(vec[:], 0.0)
            pool.memset(empty[:, 0:P], 0.0)
            pool.memset(empty[:, P:P + 1].bitcast(I32), tokens)
            pool.drain().then_inc(empty_ready, 1)
            pool.memset(f1[:, FFN_ROWS:CHUNKS * P], 0.0)
            pool.memset(f2[:, 15, :], 0.0)
            pool.drain().then_inc(zeroed, 2)
            pool.memset(neg_half[:], -0.5)
            pool.drain()
            pool.wait_ge(rows_in, 5 * 16)

            def rsqrt(out, ve, mv):
                pool.tensor_scalar(ve, mv[:, 1:2], LN_EPS, None, ALU.add)
                pool.drain()
                return pool.tensor_tensor(out, ve, neg_half[:], ALU.pow)

            def step(j, par):
                if on(j + 3):
                    wait(pool, t1_ready, j + 4)
                    pool.tensor_tensor(t2, t1, gamma, ALU.mult)
                    pool.drain()
                    pool.tensor_tensor(H[:, at(j + 3), :], t2.unsqueeze(1), beta.unsqueeze(1), ALU.add).then_inc(h_ready, 1)
                if on(j - 1):
                    wait(pool, o_added, j)
                    pool.tensor_tensor(H[:, at(j - 1), :], H[:, at(j - 1), :], bp.unsqueeze(1),
                                       ALU.add).then_inc(bp_added, 1)
                if on(j + 2):
                    wait(pool, xs_ready, j + 2, own=True)
                    wait(pool, mv2_ready, j + 3)
                    rsqrt(rs2, ve2, mv2)
                    pool.drain()
                    pool.tensor_tensor(nb2, mv2[:, 0:1], rs2, ALU.mult)
                    pool.drain()
                    pool.tensor_scalar(nb2, nb2, -1.0, ATT_SHIFT, ALU.mult, ALU.add).then_inc(rs2_ready, 1)
                if on(j + 4):
                    wait(pool, mv1_ready, j + 5, own=True)
                    rsqrt(rs1, ve1, mv1).then_inc(rs1_ready, 1)
                if on(j - 2):
                    wait(pool, mv3_ready, j - 1, own=True)
                    pool.tensor_scalar(ve3, mv3[:, 1:2], LN_EPS, None, ALU.add)
                    pool.drain()
                    pool.tensor_tensor(rstd[:, at(j - 2)], ve3, neg_half[:], ALU.pow)
                    pool.drain()
                    pool.tensor_tensor(mrstd[:, at(j - 2)], mv3[:, 0:1], rstd[:, at(j - 2)], ALU.mult).then_inc(rs3_ready, 1)

            run_steps(pool, step, **A_STEPS)
            finish(pool, 0)

            enter(pool, 1)

            def group(g, par):
                if ongroup(g - 1):
                    wait(pool, mvs_ready, g, own=True)
                    pool.tensor_scalar(ve4, mv4[:, :, 1], LN_EPS, None, ALU.add)
                    pool.drain()
                    pool.tensor_tensor(rstd[:, at(4 * g - 4, 4)], ve4, neg_half[:].broadcast_to([P, 4]), ALU.pow)
                    pool.drain()
                    pool.tensor_tensor(mrstd[:, at(4 * g - 4, 4)], mv4[:, :, 0], rstd[:, at(4 * g - 4, 4)],
                                       ALU.mult).then_inc(rs4_ready, 1)

            run_groups(pool, group, groups + 1)
            finish(pool, 1)
            enter(pool, 2)
            finish(pool, 2)

            enter(pool, 3)
            pool.memset(vals[:, :, :, DK:DK + 1], 1.0)
            pool.drain()

            def attend(j, par):
                if on(j + 4):
                    wait(pool, d_n2, j + 4, own=True)
                    wait(pool, d_mv1, j + 5, own=True)
                    pool.tensor_scalar(va2[:, 0:1], mva[:, 1:2], LN_EPS, None, ALU.add)
                    pool.tensor_scalar(va2[:, 1:2], mva[:, 1:2], 1 + LN_EPS, LN_EPS ** 2, ALU.mult, ALU.add)
                    pool.drain()
                    pool.tensor_tensor(rs2x, va2, neg_half[:].broadcast_to([P, 2]), ALU.pow)
                    pool.drain()
                    pool.tensor_scalar(mr2x, rs2x, mva[:, 0:1], None, ALU.mult)
                    pool.drain().then_inc(d_rs1, 1)
                if on(j + 1):
                    wait(pool, d_s, 2 * j + 2)
                    wait(pool, d_qv, j + 2)
                    pool.tensor_tensor(km[:, 4:8, :], kT.unsqueeze(1).broadcast_to([P, 4, P]),
                                       const("head_of_row")[:, 4:8].unsqueeze(2).broadcast_to([P, 4, P]),
                                       ALU.mult).then_inc(d_km1, 1)
                if on(j - 4):
                    wait(pool, d_x2, j - 3)
                    rows = H[:, at(j - 4), :]
                    pool.tensor_tensor(rows, rows, x2[:, par % 2].unsqueeze(1), ALU.add).then_inc(d_hadd, 1)
                    wait(pool, d_n3, j - 4, own=True)
                    wait(pool, d_mv3, j - 3)
                    rsqrt(rsc, vc, mvc)
                    pool.drain()
                    pool.tensor_scalar(mrc, rsc, mvc[:, 0:1], -1.0, ALU.mult, ALU.mult).then_inc(d_rs3, 1)

            run_steps(pool, attend, **D_STEPS)
            finish(pool, 3)
            pool.wait_ge(e_dve, 4)
            pool.wait_ge(emptied, 16)
            for b in range(nb):
                pool.indirect_dma_start(sorted_x, bass.IndirectOffsetOnAxis(ap=slot_i[:, b:b + 1], axis=0), named[:, b, :],
                                        None, bounds_check=sorted_rows - 1, oob_is_err=False).then_inc(scattered, 16)
            finish(pool, 4)
            pool.wait_ge(stored, 16 * groups)

            def tile(i, k):
                t = 4 * i + k
                if ontile(t - 1):
                    n = (k - 1) % 4
                    wait(pool, f_y, t, own=True)
                    pool.indirect_dma_start(out.rearrange("b t d -> (b t) d"),
                                            bass.IndirectOffsetOnAxis(ap=tile_token[:, n:n + 1], axis=0), tile_y[:, n, :], None,
                                            bounds_check=tokens - 1, oob_is_err=False,
                                            compute_op=ALU.add).then_inc(f_out[n], 16)

            run_tiles(pool, tile)
            for n in range(4):
                pool.wait_ge(f_out[n], 16 * len(range(n, tiles, 4)))

        def quantum_weights(dve):
            m2 = [walk.rearrange("p (i j) -> p i j", j=2), walk2.rearrange("p (i j) -> p i j", j=2),
                  walk3.rearrange("p (i j) -> p i j", j=2)]
            v0, v1 = pr0.rearrange("p (i j) -> p i j", j=2), pr1.rearrange("p (i j) -> p i j", j=2)
            dve.wait_ge(late_in, 5 * 16)
            dve.tensor_copy(spin[:, 0:4], rot)
            dve.tensor_scalar(spin[:, 4:8], rot, math.pi / 2, None, ALU.add)
            dve.drain()
            dve.tensor_scalar(turns, spin, 1.0 / TWO_PI, None, ALU.mult)
            dve.drain()
            dve.tensor_scalar(turns, turns, ROUND, None, ALU.add)
            dve.drain()
            dve.tensor_scalar(turns, turns, -ROUND, None, ALU.add)
            dve.drain()
            dve.scalar_tensor_tensor(spin, turns, -TWO_PI, spin, ALU.mult, ALU.add)
            dve.drain()
            dve.tensor_scalar(spin, spin, 3.1415925, -3.1415925, ALU.min, ALU.max)
            dve.drain().then_inc(spin_ready, 1)
            for n in (0, 1):
                dve.tensor_tensor(v0, m2[n][:, :, 0:1].broadcast_to([P, 2, 2]), m2[0][:, 0:1, :].broadcast_to([P, 2, 2]), ALU.mult)
                dve.tensor_tensor(v1, m2[n][:, :, 1:2].broadcast_to([P, 2, 2]), m2[0][:, 1:2, :].broadcast_to([P, 2, 2]), ALU.mult)
                dve.drain()
                dve.tensor_tensor(m2[n + 1], v0, v1, ALU.add)
                dve.drain()
            dve.tensor_scalar(u_re, walk2, -ENT * ENT / 2, None, ALU.mult)
            dve.tensor_scalar(u_im, walk3, -ENT * ENT * ENT / 6, None, ALU.mult)
            dve.drain()
            dve.scalar_tensor_tensor(u_im, walk, ENT, u_im, ALU.mult, ALU.add)
            dve.tensor_scalar(u_re[:, 0:4:3], u_re[:, 0:4:3], 1.0, None, ALU.add)
            dve.tensor_copy(al_re, amp[:, 0:2])
            dve.tensor_copy(al_im, amp[:, 2:4])
            dve.drain()
            dve.wait_ge(waves_ready, 1)
            ur, ui = u_re.rearrange("p (i j) -> p i j", j=2), u_im.rearrange("p (i j) -> p i j", j=2)
            for depth in range(2):
                sin, cos = waves[:, 2 * depth:2 * depth + 2], waves[:, 4 + 2 * depth:6 + 2 * depth]
                dve.tensor_tensor(pr0[:, 0:2], sin, al_im, ALU.mult)
                dve.tensor_tensor(pr1[:, 0:2], sin, al_re, ALU.mult)
                dve.tensor_tensor(be_re, cos, al_re, ALU.mult)
                dve.tensor_tensor(be_im, cos, al_im, ALU.mult)
                dve.drain()
                dve.tensor_tensor(be_re, be_re, pr0[:, 0:2], ALU.subtract)
                dve.tensor_tensor(be_im, be_im, pr1[:, 0:2], ALU.add)
                dve.drain()
                for a, b, op, dst in ((be_re, be_im, ALU.subtract, al_re), (be_im, be_re, ALU.add, al_im)):
                    dve.tensor_tensor(v0, ur, a.unsqueeze(1).broadcast_to([P, 2, 2]), ALU.mult)
                    dve.tensor_tensor(v1, ui, b.unsqueeze(1).broadcast_to([P, 2, 2]), ALU.mult)
                    dve.drain()
                    dve.tensor_tensor(v0, v0, v1, op)
                    dve.drain()
                    dve.tensor_reduce(dst, v0, X, ALU.add)
                    dve.drain()
            dve.tensor_tensor(be_re, al_re, al_re, ALU.mult)
            dve.tensor_tensor(be_im, al_im, al_im, ALU.mult)
            dve.drain()
            dve.tensor_tensor(be_re, be_re, be_im, ALU.add)
            dve.drain()
            dve.tensor_reduce(be_im[:, 0:1], be_re, X, ALU.add)
            dve.drain()
            dve.reciprocal(be_im[:, 1:2], be_im[:, 0:1])
            dve.drain()
            dve.tensor_scalar(path_w, be_re, be_im[:, 1:2], None, ALU.mult)
            dve.drain()

        def routing(dve):

            def over_experts(t):
                return t.unsqueeze(2).broadcast_to([P, nb, MOE_E])

            dve.tensor_reduce(best, logits, X, ALU.max)
            dve.drain()
            dve.tensor_tensor(logits, logits, over_experts(best), ALU.subtract)
            dve.memset(count, 0.0)
            dve.drain().then_inc(e_dve, 1)
            dve.wait_ge(e_act, 1)
            dve.tensor_reduce(slot, probs, X, ALU.add)
            dve.drain()
            dve.reciprocal(total_p, slot)
            dve.drain()
            dve.tensor_tensor(probs, probs, over_experts(total_p), ALU.mult)
            dve.drain()
            for e in range(MOE_E):
                this = probs[:, :, e:e + 1]
                if e:
                    dve.tensor_tensor(cmp[:, :, 0:e], this.broadcast_to([P, nb, e]), probs[:, :, 0:e], ALU.is_gt)
                dve.memset(cmp[:, :, e:e + 1], 0.0)
                if e + 1 < MOE_E:
                    dve.tensor_tensor(cmp[:, :, e + 1:], this.broadcast_to([P, nb, MOE_E - 1 - e]), probs[:, :, e + 1:], ALU.is_ge)
                dve.drain()
                dve.tensor_tensor(count, count, cmp, ALU.add)
                dve.drain()
            dve.tensor_scalar(chosen, count, 1.5, None, ALU.is_lt)
            dve.drain().then_inc(e_dve, 1)

            def places(banks):
                dve.tensor_copy(total, banks[1][:, 0:nb * MOE_E].rearrange("p (b e) -> p b e", e=MOE_E))
                dve.drain()
                for e in range(MOE_E):
                    dve.tensor_tensor_scan(running[:, :, e], const("ones")[:, 0:nb], total[:, :, e], 0.0, ALU.mult, ALU.add)
                dve.drain()
                dve.tensor_tensor(rank, running, total, ALU.subtract)
                dve.drain()
                dve.tensor_tensor(rank, rank, banks[0][:, 0:nb * MOE_E].rearrange("p (b e) -> p b e", e=MOE_E), ALU.add)
                dve.drain()

            dve.wait_ge(e_pe, 1)
            places(A)
            dve.scalar_tensor_tensor(kept, rank, float(cap), chosen, ALU.is_lt, ALU.mult)
            dve.drain()
            dve.tensor_tensor(cmp, kept, const("expert_number").unsqueeze(1).broadcast_to([P, nb, MOE_E]), ALU.mult)
            dve.drain()
            dve.tensor_reduce(best, cmp, X, ALU.max)
            dve.drain()
            dve.tensor_tensor(final, cmp, over_experts(best), ALU.is_equal)
            dve.drain()
            dve.tensor_tensor(final, final, kept, ALU.mult)
            dve.drain().then_inc(e_dve, 1)
            dve.wait_ge(e_pe, 2)
            places(B)
            dve.tensor_scalar(filled, running[:, nb - 1, :], 1.0 / P, 127.0 / 256.0, ALU.mult, ALU.add)
            dve.drain()
            dve.tensor_scalar(filled, filled, ROUND, None, ALU.add)
            dve.drain()
            dve.tensor_scalar(filled, filled, -ROUND, None, ALU.add)
            dve.drain()
            dve.tensor_tensor_scan(ends, const("ones")[:, 0:MOE_E], filled, 0.0, ALU.mult, ALU.add)
            dve.drain()
            dve.tensor_tensor(starts, ends, filled, ALU.subtract)
            dve.drain()
            dve.tensor_scalar(base, starts, float(P), None, ALU.mult)
            dve.drain()
            dve.tensor_tensor(rank, rank, base.unsqueeze(1).broadcast_to([P, nb, MOE_E]), ALU.add)
            dve.tensor_reduce(dropped, final, X, ALU.add)
            dve.drain()
            dve.tensor_tensor(rank, rank, final, ALU.mult)
            dve.tensor_scalar(dropped, dropped, -float(sorted_rows), float(sorted_rows), ALU.mult, ALU.add)
            dve.drain()
            dve.tensor_reduce(slot, rank, X, ALU.add)
            dve.drain()
            dve.tensor_tensor(slot_i, slot, dropped, ALU.add)
            dve.drain().then_inc(e_dve, 1)
            def over_tiles(t):
                return t.unsqueeze(1).broadcast_to([P, tiles, MOE_E])

            numbers = const("tile_number")
            dve.tensor_tensor(by_tile, over_tiles(ends), numbers.unsqueeze(2).broadcast_to([P, tiles, MOE_E]), ALU.is_le)
            dve.drain()
            dve.tensor_reduce(tile_e, by_tile, X, ALU.add)
            dve.drain()
            dve.tensor_scalar(table_i, tile_e, MOE_E - 1.0, None, ALU.min)
            dve.drain().then_inc(e_dve, 1)

        def router0(dve):
            lg, pr, sel = pl[0:nb, 0:11], pl[0:nb, 11:22], pl[0:nb, 22:33]
            m, s, r = pl[0:nb, 33:34], pl[0:nb, 34:35], pl[0:nb, 35:36]
            gt = pl[0:nb, 121:242].rearrange("p (i j) -> p i j", j=PARTS)
            eq = pl[0:nb, 242:363].rearrange("p (i j) -> p i j", j=PARTS)
            dve.drain().then_inc(rt_dve, 1)
            dve.wait_ge(rt_pe, 1)
            dve.tensor_scalar(lg, E[0:nb, 0:PARTS], 1.0 / P, None, ALU.mult)
            dve.drain()
            dve.tensor_reduce(m, lg, X, ALU.max)
            dve.drain()
            dve.tensor_scalar(lg, lg, m, None, ALU.subtract)
            dve.drain().then_inc(rt_dve, 1)
            dve.wait_ge(rt_act, 1)
            dve.reciprocal(r, s)
            dve.drain()
            dve.tensor_scalar(pr, pr, r, None, ALU.mult)
            dve.drain()
            of_i, of_j = pr.unsqueeze(2).broadcast_to([nb, PARTS, PARTS]), pr.unsqueeze(1).broadcast_to([nb, PARTS, PARTS])
            dve.tensor_tensor(gt, of_j, of_i, ALU.is_gt)
            dve.tensor_tensor(eq, of_j, of_i, ALU.is_equal)
            dve.drain()
            dve.tensor_tensor(eq, eq, const("earlier_part", nb).rearrange("p (i j) -> p i j", j=PARTS), ALU.mult)
            dve.drain()
            dve.tensor_tensor(gt, gt, eq, ALU.add)
            dve.drain()
            dve.tensor_reduce(sel, gt, X, ALU.add)
            dve.drain()
            dve.tensor_scalar(sel, sel, 1.5, None, ALU.is_lt)
            dve.drain()
            dve.tensor_tensor(sel, sel, pr, ALU.mult)
            dve.drain()
            dve.tensor_reduce(m, sel, X, ALU.add)
            dve.drain()
            dve.reciprocal(r, m)
            dve.drain()
            dve.tensor_scalar(sel, sel, r, None, ALU.mult)
            dve.drain().then_inc(rt_dve, 1)
            dve.wait_ge(rt_pe, 2)
            dve.tensor_copy(pl[0:PARTS, 400:400 + nb], D[0:PARTS, 0:nb])
            dve.drain().then_inc(rt_dve, 1)
            dve.wait_ge(rt_pe, 3)
            dve.tensor_scalar(pl[0:FFN_E, 500:500 + nb], E[0:FFN_E, 0:nb], 1e-6, None, ALU.is_gt)
            dve.drain()
            dve.tensor_tensor(pl[0:FFN_E, 500:500 + nb], pl[0:FFN_E, 500:500 + nb], E[0:FFN_E, 0:nb], ALU.mult)
            dve.drain().then_inc(rt_dve, 1)
            dve.wait_ge(rt_pe, 4)
            for h in range(2):
                dve.tensor_copy(w4[:, 8 * h:8 * h + 8, :], A[h][:, 0:8 * nb].rearrange("p (c b) -> p c b", c=8))
            dve.tensor_copy(b2w, B[0][:, 0:nb])
            dve.drain().then_inc(rt_dve, 1)

        def state_space_weights(dve):
            dve.tensor_scalar(soft0, dt_col, -1.0, None, ALU.mult)
            dve.drain()
            dve.tensor_tensor(soft0, soft0, dt_col, ALU.max)
            dve.drain().then_inc(c_dve, 1)
            dve.wait_ge(late_in, 9 * 16)
            dve.wait_ge(c_act, 1)
            dve.tensor_scalar(soft0, dt_col, 0.0, None, ALU.max)
            dve.drain()
            dve.tensor_tensor(soft0, soft0, soft1, ALU.add)
            dve.drain()
            dve.tensor_reduce(dt_sum, soft0, X, ALU.add)
            dve.tensor_tensor(ops[:, :, 0:P], op_raw, skip_col.unsqueeze(2).broadcast_to([P, HDC, P]), ALU.mult)
            dve.tensor_tensor(ops[:, :, P:P + STATES], bproj, soft0.unsqueeze(2).broadcast_to([P, HDC, STATES]), ALU.mult)
            dve.tensor_copy(cproj8.rearrange("p c (r n) -> p c r n", n=STATES), cproj.unsqueeze(2).broadcast_to([P, HDC, 8, STATES]))
            dve.drain().then_inc(c_dve, 1)
            dve.wait_ge(c_pe, 2)
            dve.tensor_scalar(soft1[:, 0:1], D[:, 0:1], -1.0 / HD, None, ALU.mult)
            dve.drain()
            dve.tensor_scalar(rate, rate, soft1[:, 0:1], None, ALU.mult)
            dve.drain().then_inc(c_dve, 1)
            dve.tensor_scalar(mixer, const("low_band"), path_w[:, 0:1], None, ALU.mult)
            dve.drain()
            dve.scalar_tensor_tensor(mixer, const("high_band"), path_w[:, 1:2], mixer, ALU.mult, ALU.add)
            dve.wait_ge(c_pe, 3)
            dve.tensor_copy(state_w, E[:, 0:P + STATES])
            dve.wait_ge(c_pe, 4)
            dve.tensor_tensor(back8, D[:, P:2 * P].unsqueeze(1).broadcast_to([P, 8, P]),
                              const("octet_of_row").unsqueeze(2).broadcast_to([P, 8, P]), ALU.mult)
            dve.wait_ge(c_act, 2)
            dve.tensor_tensor(decays, decays, const("causal").unsqueeze(1).broadcast_to([P, STATES, P]), ALU.mult)
            dve.drain().then_inc(c_dve, 1)

        @block.vector
        def _(dve):
            dve.wait_ge(ids_in, 16)
            (tok, row, col, bos, sep, rw, end, color, keep, inside, rowc, colc, g) = grid
            n = P
            dve.tensor_copy(g[:, 0:n], tok[:, 0:n].bitcast(I32))
            dve.drain()
            for dst, code in ((bos, BOS), (sep, SEP), (rw, ROW), (end, EOS), (keep, PAD)):
                dve.tensor_scalar(dst[:, 0:n], g[:, 0:n], float(code), None, ALU.is_equal)
            dve.tensor_scalar(color[:, 0:n], g[:, 0:n], 9.5, None, ALU.is_lt)
            dve.tensor_scalar(col[:, 0:n], g[:, 0:n], -0.5, None, ALU.is_gt)
            dve.tensor_copy(tok[:, 0:n], g[:, 0:n])
            for t in (inside, rowc, colc):
                dve.memset(t[:, 0:1], 0.0)
            dve.drain()
            dve.tensor_tensor(color[:, 0:n], color[:, 0:n], col[:, 0:n], ALU.mult)
            dve.tensor_tensor(end[:, 0:n], end[:, 0:n], keep[:, 0:n], ALU.add)
            dve.drain()
            dve.tensor_tensor(end[:, 0:n], end[:, 0:n], bos[:, 0:n], ALU.add)
            dve.tensor_tensor(sep[:, 0:n], sep[:, 0:n], bos[:, 0:n], ALU.add)
            dve.drain()
            dve.tensor_scalar(keep[:, 0:n], end[:, 0:n], -1.0, 1.0, ALU.mult, ALU.add)
            dve.tensor_scalar(g[:, 0:n], sep[:, 0:n], -1.0, 1.0, ALU.mult, ALU.add)
            dve.drain()
            dve.tensor_tensor_scan(inside[:, 1:n + 1], keep[:, 0:n], bos[:, 0:n], 0.0, ALU.mult, ALU.add)
            dve.tensor_tensor_scan(rowc[:, 1:n + 1], g[:, 0:n], rw[:, 0:n], 0.0, ALU.mult, ALU.add)
            dve.drain()
            dve.tensor_tensor(inside[:, 0:n], inside[:, 0:n], color[:, 0:n], ALU.mult)
            dve.tensor_tensor(g[:, 0:n], g[:, 0:n], rw[:, 0:n], ALU.subtract)
            dve.drain()
            dve.tensor_tensor_scan(colc[:, 1:n + 1], g[:, 0:n], inside[:, 0:n], 0.0, ALU.mult, ALU.add)
            dve.tensor_scalar(color[:, 0:n], color[:, 0:n], -NO_CELL, NO_CELL, ALU.mult, ALU.add)
            dve.drain()
            for dst, src, most in ((row, rowc, MAX_H - 1), (col, colc, MAX_W - 1)):
                dve.tensor_tensor(dst[:, 0:n], src[:, 0:n], inside[:, 0:n], ALU.mult)
                dve.drain()
                dve.tensor_scalar(dst[:, 0:n], dst[:, 0:n], float(most), None, ALU.min)
                dve.drain()
                dve.tensor_tensor(dst[:, 0:n], dst[:, 0:n], color[:, 0:n], ALU.add)
            dve.drain().then_inc(ids_ready, 1)
            quantum_weights(dve)
            dve.wait_ge(a_prep_pe, 1)
            for h in range(2):
                last = dve.tensor_copy(wq[:, :, 64 * h:64 * h + 64].rearrange("p h e -> p e h"),
                                       A[h][:].rearrange("p (e h) -> p e h", h=HEADS))
            dve.wait_ge(a_prep_pe, 4)
            dve.tensor_copy(vecT[:], D[:, 256:384])
            dve.tensor_copy(gs, D[:, 0:P])
            dve.tensor_copy(t2[:, 0:TABLE_ROWS], D[:, P:P + TABLE_ROWS])
            dve.drain().then_inc(a_prep_dve, 1)
            dve.wait_ge(a_prep_pe, 5)
            dve.wait_ge(table_in, 64)
            dve.tensor_tensor(table, table, E[0:TABLE_ROWS, 0:P], ALU.add)
            dve.drain().then_inc(a_prep_dve, 1)
            dve.wait_ge(con_in, 16)
            dve.wait_ge(rows_in, 5 * 16)

            def stats(st, mv, src):
                dve.bn_stats(st, src)
                dve.drain()
                return dve.bn_aggr(mv, st)

            def step(j, par):
                if on(j):
                    for h in range(2):
                        m = slice(4 * h, 4 * h + 4)
                        wait(dve, s_done, 2 * j + h + 1)
                        dve.tensor_reduce(mx[:, m], heads4(C[h]), X, ALU.max)
                        dve.drain()
                        wait(dve, exp_done, 2 * j + h - 1)
                        dve.tensor_scalar(negm[:, m], mx[:, m], -SCALE, None, ALU.mult).then_inc(negmax, 1)
                if on(j + 5):
                    wait(dve, bc_done, j + 6)
                    wait(dve, em_done, j + 4)
                    dve.tensor_scalar(onehot[0:TABLE_ROWS, (par + 1) % 2, :], D[0:TABLE_ROWS, P:2 * P],
                                      const("key", TABLE_ROWS), None, ALU.is_equal).then_inc(oh_ready, 1)
                if on(j + 3):
                    wait(dve, rs1_ready, j + 4)
                    wait(dve, h_ready, j + 3)
                    dve.tensor_scalar(t1, t0, mv1[:, 0:1], rs1, ALU.subtract, ALU.mult).then_inc(t1_ready, 1)
                if on(j - 1):
                    wait(dve, o_done, j)
                    dve.tensor_tensor(H[:, at(j - 1), :], H[:, at(j - 1), :], E[:, 0:P].unsqueeze(1),
                                      ALU.add).then_inc(o_added, 1)
                if on(j + 1):
                    wait(dve, g_done, j + 2)
                    wait(dve, gw_done, 2 * j + 2)
                    dve.tensor_copy(gs, D[:, 0:P]).then_inc(g_evac, 1)
                if on(j + 2):
                    wait(dve, rs2_ready, j + 2, own=True)
                    wait(dve, h_ready, j + 3)
                    stats(st2, mv2, H[:, at(j + 2), :]).then_inc(mv2_ready, 1)
                if on(j + 1):
                    wait(dve, u_done, 2 * j + 2)
                    for h in range(2):
                        wait(dve, xw_done, 2 * j + h + 3)
                        dve.tensor_copy(half(xws, h), A[h][:]).then_inc(xw_evac, 1)
                if on(j + 4):
                    wait(dve, t1_ready, j + 4)
                    wait(dve, em_done, j + 5)
                    dve.tensor_tensor(t0, E[:, P:2 * P], pos, ALU.add).then_inc(em_evac, 1)
                    dve.drain()
                    wait(dve, rs1_ready, j + 4, own=True)
                    stats(st1, mv1, t0).then_inc(mv1_ready, 1)
                if on(j - 2):
                    wait(dve, rs3_ready, j - 2, own=True)
                    wait(dve, bp_added, j - 1)
                    stats(st3, mv3, H[:, at(j - 2), :]).then_inc(mv3_ready, 1)
                if on(j):
                    for h in range(2):
                        wait(dve, exp_done, 2 * j + h + 1)
                        dve.reciprocal(rinv[:, 4 * h:4 * h + 4], rsum[:, 4 * h:4 * h + 4])
                        dve.drain()
                        p4 = prob[:, 4 * h:4 * h + 4, :]
                        dve.tensor_tensor(p4, p4, rinv[:, 4 * h:4 * h + 4].unsqueeze(2).broadcast_to([P, 4, P]),
                                          ALU.mult).then_inc(p_ready, 1)
                if on(j + 1):
                    wait(dve, o_done, j)
                    for h in range(2):
                        wait(dve, u_done, 2 * j + h + 3)
                        dve.tensor_copy(half(us[:, (par + 1) % 2], h), A[h][:]).then_inc(u_evac, 1)
                if on(j + 2):
                    wait(dve, xw_done, upto(2 * j + 4, 2 * nb))
                    wait(dve, rs2_ready, j + 3)
                    dve.tensor_scalar(xs.unsqueeze(1), H[:, at(j + 2), :], rs2, nb2, ALU.mult, ALU.add).then_inc(xs_ready, 1)

            run_steps(dve, step, **A_STEPS)
            finish(dve, 0)

            enter(dve, 1)

            def normalize(g, par, dst, evacuated):
                wait(dve, evacuated, g - 1)
                for k in range(4):
                    b = 4 * g + k
                    last = dve.tensor_scalar(dst[:, par, k, :].unsqueeze(1), H[:, at(b), :], rstd[:, at(b)],
                                             mrstd[:, at(b)], ALU.mult, ALU.subtract)
                return last

            def to_columns(g, par):
                if ongroup(g):
                    normalize(g, par, xn, tb_done).then_inc(xn_ready, 1)
                if ongroup(g - 1):
                    wait(dve, xt_evac, g, own=True)
                    dve.tensor_reduce(token_sum[:, at(4 * g - 4, 4)], group_rows(H2, g - 1), X, ALU.add)

            run_groups(dve, to_columns, groups + 1)
            router0(dve)

            def group(g, par):
                for c in range(CHUNKS):
                    n = 16 * g + c
                    if ongroup(g):
                        wait(dve, gelu_done, n + 1)
                        wait(dve, down_done, n - 3)
                        dve.tensor_tensor(hidw[:, c % 4], hid[:, c % 4],
                                          w4[:, c, at(4 * g, 4)].unsqueeze(2).broadcast_to([P, 4, P]),
                                          ALU.mult).then_inc(hw_ready, 1)
                    if c == 8 and ongroup(g - 1):
                        wait(dve, ott_done, g)
                        rows = group_rows(H, g - 1)
                        dve.tensor_tensor(rows, rows, E[:].rearrange("p (b d) -> p b d", b=4), ALU.add).then_inc(ffn_added, 1)
                        dve.drain()
                        wait(dve, rs4_ready, g - 1, own=True)
                        for k in range(4):
                            dve.bn_stats(st4[:, k, :], H[:, at(4 * g - 4 + k), :])
                        dve.drain()
                        for k in range(4):
                            last = dve.bn_aggr(mv4[:, k, :], st4[:, k, :])
                        last.then_inc(mvs_ready, 1)
                if ongroup(g):
                    wait(dve, ott_done, g)
                    wait(dve, down_done, 16 * g + 16)
                    dve.tensor_tensor(ot, D[:].rearrange("p (b d) -> p b d", b=4),
                                      b2w[:, at(4 * g, 4)].unsqueeze(2).broadcast_to([P, 4, P]), ALU.add).then_inc(ot_ready, 1)

            run_groups(dve, group, groups + 1)
            finish(dve, 1)

            enter(dve, 2)
            state_space_weights(dve)

            def states(g, par):
                if ongroup(g):
                    normalize(g, par, cxn, ct_done).then_inc(cxn_ready, 1)
                if ongroup(g - 1):
                    wait(dve, cz_done, g)
                    z = (B, C)[(par + 1) % 2]
                    for k in range(2):
                        rows = H[:, at(4 * g - 4 + 2 * k, 2), :]
                        last = dve.tensor_tensor(rows, rows, z[k][:, 0:288].rearrange("p (b n) -> p b n", b=2)[:, :, 0:P], ALU.add)
                    last.then_inc(c_added, 1)

            run_groups(dve, states, groups + 1, peeled=4)
            nh = 8 * nb
            for h in range(2):
                dve.wait_ge(c_pe, 5 + h)
                dve.tensor_copy(zm.rearrange("p n b -> p (n b)")[:, nh * h:nh * h + nh], A[h][:, 0:nh])
            dve.drain().then_inc(c_dve, 1)
            for h in range(2):
                dve.wait_ge(c_pe, 7 + h)
                dve.tensor_copy(hb[:, :, 8 * h:8 * h + 8].rearrange("p b n -> p n b"), B[h][:, 0:nh].rearrange("p (n b) -> p n b", b=nb))
            dve.drain().then_inc(c_dve, 1)
            for q in range(nb // 8):
                for h in range(2):
                    dve.wait_ge(c_pe, 10 + 2 * q + h)
                    rows = H[:, 8 * q + 4 * h:8 * q + 4 * h + 4, :]
                    dve.tensor_tensor(rows, rows, (A, B)[q % 2][h][:].rearrange("p (b d) -> p b d", b=4), ALU.add).then_inc(c_added, 1)
            finish(dve, 2)

            enter(dve, 3)
            dve.tensor_copy(named[:, :, P].bitcast(I32), const("token_number"))
            dve.tensor_copy(be2_all, be2_col.broadcast_to([P, P]))
            dve.drain().then_inc(d_prep_dve, 1)
            dve.wait_ge(d_prep_pe, 1)
            dve.tensor_tensor(qkv_b, qkv_b, D[:, 0:3], ALU.add)
            dve.tensor_tensor(router_b, router_b, D[:, 8:16], ALU.add)
            dve.tensor_tensor(b1, b1, D[:, 16:48], ALU.add)
            for w, scale in ((aq, g1_col), (ak, g1_col), (av, g1_col), (router_w, g2_col)):
                dve.tensor_scalar(w, w, scale, None, ALU.mult)
            dve.drain()
            dve.tensor_copy(bv_all, bv_col.broadcast_to([P, P]))
            dve.drain().then_inc(d_prep_dve, 1)
            dve.wait_ge(d_prep_pe, 2)
            dve.tensor_tensor(ctx_bias, D[:, 64:64 + P], bo, ALU.add)
            dve.drain().then_inc(d_prep_dve, 1)

            def attend(j, par):
                def largest(h):
                    m = slice(4 * h, 4 * h + 4)
                    wait(dve, d_s, 2 * j + h + 1)
                    dve.tensor_reduce(mx[:, m], heads4(C[h]), X, ALU.max)
                    dve.drain()
                    wait(dve, d_exp, 2 * j + h - 1)
                    dve.tensor_scalar(negm[:, m], mx[:, m], -DK ** -0.5, None, ALU.mult).then_inc(d_neg, 1)

                if on(j + 3):
                    wait(dve, d_rs1, j + 4)
                    wait(dve, d_t3, j + 2)
                    dve.tensor_scalar(n2[:, (par + 1) % 2].unsqueeze(1), H[:, at(j + 3), :], rs2x[:, 1:2], mr2x[:, 1:2],
                                      ALU.mult, ALU.subtract)
                    dve.tensor_scalar(named[:, at(j + 3), 0:P], H[:, at(j + 3), :], rs2x[:, 0:1], mr2x[:, 0:1],
                                      ALU.mult, ALU.subtract)
                    dve.drain().then_inc(d_n2, 1)
                if on(j + 4):
                    wait(dve, d_rs1, j + 4, own=True)
                    stats(sta, mva, H[:, at(j + 4), :]).then_inc(d_mv1, 1)
                if on(j):
                    largest(0)
                if on(j + 1):
                    wait(dve, d_s, 2 * j + 1)
                    wait(dve, d_qv, j + 2)
                    dve.tensor_tensor(km[:, 0:4, :], kT.unsqueeze(1).broadcast_to([P, 4, P]),
                                      const("head_of_row")[:, 0:4].unsqueeze(2).broadcast_to([P, 4, P]),
                                      ALU.mult).then_inc(d_km0, 1)
                if on(j):
                    largest(1)
                if on(j - 7):
                    wait(dve, d_wl, j - 3)
                    dve.tensor_tensor(logits[:, at(j - 7), :], E[:, P:P + MOE_E].unsqueeze(1), router_b.unsqueeze(1),
                                      ALU.add).then_inc(d_lg, 1)
                if on(j - 4):
                    wait(dve, d_wl, j - 3)
                    wait(dve, d_n3, j - 5)
                    wait(dve, d_hadd, j - 5)
                    dve.tensor_tensor(x2[:, par % 2].unsqueeze(1), E[:, 0:P].unsqueeze(1), named[:, at(j - 4), 0:P],
                                      ALU.add).then_inc(d_x2, 1)
                    dve.drain()
                    wait(dve, d_rs3, j - 4, own=True)
                    stats(stc, mvc, x2[:, par % 2]).then_inc(d_mv3, 1)
                if on(j - 2):
                    wait(dve, d_pv, j - 1)
                    c4 = D[:, 0:HEADS * (DK + 1)].rearrange("p (h n) -> p h n", h=HEADS)
                    dve.reciprocal(rctx.unsqueeze(2), c4[:, :, DK:DK + 1])
                    dve.drain()
                    wait(dve, d_t3, j + 3)
                    dve.tensor_tensor(ctxs.rearrange("p (h n) -> p h n", h=HEADS), c4[:, :, 0:DK],
                                      rctx.unsqueeze(2).broadcast_to([P, HEADS, DK]), ALU.mult).then_inc(d_ctx, 1)

            run_steps(dve, attend, **D_STEPS)
            finish(dve, 3)
            enter(dve, 4)
            routing(dve)
            finish(dve, 4)

            dve.wait_ge(e_act, 2)

            def tile(i, k):
                t = 4 * i + k
                if ontile(t + 1):
                    n = (k + 1) % 2
                    e = dve.value_load(table_i[0:1, at(t + 1)], min_val=0, max_val=MOE_E - 1)
                    wait(dve, f_g, t)
                    dve.tensor_copy(tile_w1[:, n, :].unsqueeze(1), w1[:, at(e), :])
                    dve.tensor_copy(tile_b1[:, n, :], b1[:, at(e * MOE_C, MOE_C)])
                    m = (k + 1) % 4
                    wait(dve, f_out[m], 16 * (i + (k + 1) // 4))
                    wait(dve, f_in[m], 16 * (i + (k + 1) // 4) + 16)
                    dve.tensor_copy(tile_token[:, m:m + 1], tile_x[:, m, P:P + 1].bitcast(I32))
                    dve.drain().then_inc(f_w, 1)
                if ontile(t - 1):
                    e = dve.value_load(table_i[0:1, at(t - 1)], min_val=0, max_val=MOE_E - 1)
                    n = (k - 1) % 4
                    wait(dve, f_out[n], 16 * (i + (k - 1) // 4))
                    wait(dve, f_d, t)
                    dve.tensor_tensor(tile_y[:, n, :].unsqueeze(1), C[(k - 1) % 2][:, 0:P].unsqueeze(1), b2[:, at(e), :],
                                      ALU.add)
                    dve.drain().then_inc(f_y, 1)

            run_tiles(dve, tile)

        @block.scalar
        def _(act):
            act.wait_ge(spin_ready, 1)
            act.activation(waves, spin, ACT.Sin).then_inc(waves_ready, 1)
            for k, (w, src) in enumerate(((wk, B), (wv, C))):
                act.wait_ge(a_prep_pe, k + 2)
                for h in range(2):
                    act.activation(w[:, :, 64 * h:64 * h + 64].rearrange("p h e -> p e h"),
                                   src[h][:].rearrange("p (e h) -> p e h", h=HEADS), ACT.Copy)
            act.drain().then_inc(a_prep_act, 1)
            act.preload_act_table(ACT.Exp)

            def step(j, par):
                if on(j - 1):
                    wait(act, o_done, j - 1)
                    for h in range(2):
                        wait(act, pt_done, 2 * j + h - 1)
                        act.activation(half(pts, h), B[h][:], ACT.Copy).then_inc(pt_evac, 1)
                if on(j):
                    wait(act, p_ready, 2 * j)
                    for h in range(2):
                        wait(act, negmax, 2 * j + h + 1)
                        for k in range(4):
                            c = 4 * h + k
                            last = act.activation(prob[:, c, :], C[h][:, k * P:k * P + P], ACT.Exp, bias=negm[:, c:c + 1],
                                                  scale=SCALE, accum_out=rsum[:, c:c + 1])
                        last.then_inc(exp_done, 1)
                if on(j + 1):
                    wait(act, s_done, 2 * j + 2)
                    for h in range(2):
                        wait(act, gw_done, 2 * j + h + 3)
                        act.activation(half(gws, h), B[h][:], ACT.Copy).then_inc(gw_evac, 1)

            run_steps(act, step, **A_STEPS)
            finish(act, 0)

            enter(act, 1)

            def columns_out(g, par):
                wait(act, tb_done, g + 1, own=True)
                act.activation(group_rows(H2, g), A[par][:].rearrange("p (b d) -> p b d", b=4), ACT.Copy).then_inc(xt_evac, 1)

            run_groups(act, columns_out, groups)
            act.wait_ge(rt_dve, 2)
            act.activation(pl[0:nb, 11:22], pl[0:nb, 0:11], ACT.Exp, accum_out=pl[0:nb, 34:35]).then_inc(rt_act, 1)
            act.preload_act_table(ACT.Gelu)

            def group(g, par):
                for c in range(CHUNKS):
                    n = 16 * g + c
                    wait(act, up_done, n + 1)
                    wait(act, hw_ready, n - 3)
                    act.activation(hid[:, c % 4].rearrange("p b d -> p (b d)"), ring[c % 4][:], ACT.Gelu,
                                   bias=fb1[:, c:c + 1]).then_inc(gelu_done, 1)

            run_groups(act, group, groups)
            finish(act, 1)

            enter(act, 2)
            act.wait_ge(c_dve, 1)
            act.activation(soft1, soft0, ACT.Exp, scale=-1.0)
            act.activation(rate, a_log, ACT.Exp)
            act.drain()
            act.activation(soft1, soft1, ACT.Ln, bias=1.0)
            act.drain().then_inc(c_act, 1)
            act.wait_ge(c_pe, 1)
            for h in range(2):
                act.activation(half(ipT, h), C[h][:], ACT.Copy)
            act.wait_ge(c_dve, 3)
            for n in range(STATES):
                act.activation(decays[:, n, :], const("age"), ACT.Exp, scale=rate[:, n:n + 1])
            act.drain().then_inc(c_act, 1)

            def states(g, par):
                if ongroup(g):
                    wait(act, cz_done, g - 1)
                    wait(act, ct_done, g + 1)
                    act.activation(cxt[:, par].rearrange("p b d -> p (b d)"), A[par][:], ACT.Copy).then_inc(cxt_evac, 1)
                if ongroup(g - 1):
                    wait(act, c_added, g, own=True)
                    z = (B, C)[(par + 1) % 2]
                    for k in range(2):
                        last = act.activation(zs[:, :, at(4 * g - 4 + 2 * k, 2)].rearrange("p n b -> p b n"),
                                              z[k][:, 0:288].rearrange("p (b n) -> p b n", b=2)[:, :, P:P + STATES], ACT.Copy)
                    last.then_inc(cz_evac, 1)

            run_groups(act, states, groups + 1, peeled=4)
            act.wait_ge(c_pe, 9)
            for h in range(-(-nb // 32)):
                k = min(4, nb // 8 - 4 * h)
                act.activation(hT[:, 4 * h:4 * h + k, :], C[h][:, 0:k * P].rearrange("p (q l) -> p q l", l=P), ACT.Copy)
            act.drain().then_inc(c_act, 1)
            finish(act, 2)

            enter(act, 3)
            act.preload_act_table(ACT.Exp)

            def attend(j, par):
                def exponentials(h):
                    wait(act, d_neg, 2 * j + h + 1)
                    for k in range(4):
                        c = 4 * h + k
                        last = act.activation(prob2[:, par % 2, c, :], C[h][:, k * P:k * P + P], ACT.Exp, bias=negm[:, c:c + 1],
                                              scale=DK ** -0.5)
                    last.then_inc(d_exp, 1)

                if on(j - 2):
                    wait(act, d_pv, j - 2)
                    for h in range(2):
                        wait(act, d_pt, 2 * j + h - 3)
                        act.activation(half(pts2, h), B[h][:], ACT.Copy).then_inc(d_pts, 1)
                if on(j + 1):
                    wait(act, d_s, 2 * j)
                    wait(act, d_km0, j + 1)
                    wait(act, d_km1, j + 1)
                    wait(act, d_pv, j - 2)
                    wait(act, d_qkv, j + 2)
                    act.activation(kT, A[1][:, P:2 * P], ACT.Identity, bias=bk_col)
                    act.activation(qT[:, (par + 1) % 2], A[1][:, 0:P], ACT.Identity, bias=bq_col)
                    act.activation(vals[:, (par + 1) % 4, :, 0:DK], A[1][:, 2 * P:3 * P].rearrange("p (h n) -> p h n", h=HEADS),
                                   ACT.Copy)
                    act.drain().then_inc(d_qv, 1)
                if on(j - 5):
                    wait(act, d_t3, upto(j + 2, nb + 8), own=True)
                    wait(act, d_rs3, j - 4, own=True)
                    act.activation(n3[:, (par + 1) % 2], x2[:, (par - 1) % 2], ACT.Identity, bias=mrc, scale=rsc)
                    act.activation(named[:, at(j - 5), 0:P], x2[:, (par - 1) % 2].unsqueeze(1), ACT.Identity, bias=mrc, scale=rsc)
                    act.drain().then_inc(d_n3, 1)
                if on(j):
                    wait(act, d_pt, 2 * j - 2)
                    exponentials(0)
                if on(j + 2) or on(j - 3) or on(j - 6):
                    wait(act, d_t3, j + 3)
                    wait(act, d_qkv, upto(j + 2))
                    wait(act, d_wl, j - 3)
                    parts = [k for k, o in enumerate((2, -3, -6)) if on(j + o)]
                    a, b = min(parts), max(parts) + 1
                    if b - a != len(parts):
                        for k in parts:
                            act.activation(turned[:, k, :], A[0][:, k * P:k * P + P], ACT.Copy)
                    else:
                        act.activation(turned[:, a:b, :].rearrange("p a b -> p (a b)"), A[0][:, a * P:b * P], ACT.Copy)
                    act.drain().then_inc(d_ts, 1)
                if on(j):
                    exponentials(1)

            run_steps(act, attend, **D_STEPS)
            finish(act, 3)
            act.wait_ge(e_dve, 1)
            act.activation(probs, logits, ACT.Exp).then_inc(e_act, 1)
            act.preload_act_table(ACT.Gelu)
            for e in range(MOE_E):
                act.activation(w1[:, e, :], w1[:, e, :], ACT.Copy, scale=g2_col)
            act.drain().then_inc(e_act, 1)
            finish(act, 4)

            def tile(i, k):
                t = 4 * i + k
                if ontile(t + 1):
                    wait(act, f_u, t)
                    wait(act, f_t, t + 2)
                    act.activation(tile_xT[:, (k + 1) % 2, :], A[(k + 1) % 2][:, 0:P], ACT.Copy).then_inc(f_xt, 1)
                if ontile(t):
                    wait(act, f_d, t - 1)
                    wait(act, f_u, t + 1)
                    for c in range(MOE_C):
                        last = act.activation(tile_h[:, k % 2, c, :], B[k % 2][:, c * P:c * P + P], ACT.Gelu,
                                              bias=tile_b1[:, k % 2, c:c + 1])
                    last.then_inc(f_g, 1)

            run_tiles(act, tile)

        @block.tensor
        def _(pe):
            pe.wait_ge(con_in, 16)
            pe.wait_ge(proj_in, 96)
            for r, dst in enumerate((A, B, C)):
                for h in range(2):
                    pe.matmul(dst[h][:], const("centre"), half(raw[r], h), start=True, stop=False)
                    last = pe.matmul(dst[h][:], const("bias_pick", 3)[:, r * P:(r + 1) * P], raw_bias[0:3, 512 * h:512 * h + 512],
                                     start=False, stop=True)
                last.then_inc(a_prep_pe, 1)
            pe.wait_ge(table_in, 64)
            pe.transpose(D[:, 0:P], t0, ident)
            pe.wait_ge(vec_in, 13 * 16)
            pe.transpose(D[:, 256:384], vec[:], ident)
            pe.transpose(D[:, P:P + TABLE_ROWS], t1[0:TABLE_ROWS, :], ident[0:TABLE_ROWS, 0:TABLE_ROWS]).then_inc(a_prep_pe, 1)
            pe.wait_ge(a_prep_dve, 1)
            pe.matmul(E[0:TABLE_ROWS, 0:P], t2[:, 0:TABLE_ROWS], gs, start=True, stop=True).then_inc(a_prep_pe, 1)
            pe.wait_ge(a_prep_dve, 2)
            pe.wait_ge(a_prep_act, 1)
            pe.wait_ge(wp_in, 16)
            pe.wait_ge(ids_placed, 16)

            def step(j, par):
                if on(j):
                    for h in range(2):
                        wait(pe, exp_done, 2 * j + h - 1)
                        wait(pe, gw_evac, 2 * j + h + 1)
                        for k in range(4):
                            c = 4 * h + k
                            last = pe.matmul(C[h][:, k * P:k * P + P], wq[:, c, :], gws[:, c, :], start=True, stop=True)
                        last.then_inc(s_done, 1)
                if on(j + 5):
                    wait(pe, oh_ready, j + 5)
                    wait(pe, g_evac, upto(j + 1))
                    pe.matmul(D[0:TABLE_ROWS, P:2 * P], const("spread", 3), idrow[0:3, at(j + 5), :],
                              start=True, stop=True).then_inc(bc_done, 1)
                if on(j - 1):
                    wait(pe, em_evac, upto(j + 4))
                    wait(pe, o_added, j - 1)
                    wait(pe, pt_evac, 2 * j)
                    wait(pe, u_evac, 2 * j)
                    for c in range(HEADS):
                        last = pe.matmul(E[:, 0:P], pts[:, c, :], us[:, (par + 1) % 2, c, :], start=c == 0, stop=c == HEADS - 1)
                    last.then_inc(o_done, 1)
                if on(j + 1):
                    wait(pe, oh_ready, upto(j + 6))
                    wait(pe, xs_ready, j + 2)
                    pe.matmul(D[:, 0:P], xs, xs, start=True, stop=True).then_inc(g_done, 1)
                    for h in range(2):
                        wait(pe, u_evac, 2 * j + h + 1)
                        pe.matmul(A[h][:], xs, half(wp, h), start=True, stop=True).then_inc(xw_done, 1)
                if on(j + 4):
                    wait(pe, oh_ready, j + 5)
                    wait(pe, em_evac, j + 4)
                    wait(pe, o_added, j)
                    pe.matmul(E[:, P:2 * P], onehot[0:TABLE_ROWS, par, :], table, start=True, stop=True).then_inc(em_done, 1)
                if on(j + 1):
                    for h in range(2):
                        wait(pe, pt_evac, 2 * j + h - 1)
                        wait(pe, g_evac, j + 2)
                        pe.matmul(B[h][:], gs, half(wk, h), start=True, stop=True).then_inc(gw_done, 1)
                    for h in range(2):
                        wait(pe, xw_evac, 2 * j + h + 3)
                        for k in range(4):
                            c = 4 * h + k
                            last = pe.matmul(A[h][:, k * P:k * P + P], wv[:, c, :], xws[:, c, :], start=True, stop=True)
                        last.then_inc(u_done, 1)
                if on(j):
                    for h in range(2):
                        wait(pe, p_ready, 2 * j + h + 1)
                        wait(pe, pt_evac, 2 * j + h - 1)
                        wait(pe, gw_evac, upto(2 * j + h + 3, 2 * nb))
                        for k in range(4):
                            last = pe.transpose(B[h][:, k * P:k * P + P], prob[:, 4 * h + k, :], ident)
                        last.then_inc(pt_done, 1)

            run_steps(pe, step, **A_STEPS)
            finish(pe, 0)

            enter(pe, 1)

            def turn(g, par, src, ready, evacuated, done):
                wait(pe, evacuated, g - 1)
                wait(pe, ready, g + 1)
                for k in range(4):
                    last = pe.transpose(A[par][:, k * P:k * P + P], src[:, par, k, :], ident)
                last.then_inc(done, 1)

            run_groups(pe, lambda g, par: turn(g, par, xn, xn_ready, xt_evac, tb_done), groups)
            pe.wait_ge(rt_dve, 1)
            pe.matmul(E[0:nb, 0:PARTS], token_sum[:], part_w, start=True, stop=True).then_inc(rt_pe, 1)
            pe.wait_ge(rt_dve, 3)
            pe.transpose(D[0:PARTS, 0:nb], pl[0:nb, 22:33], ident[0:nb, 0:nb]).then_inc(rt_pe, 1)
            pe.wait_ge(rt_dve, 4)
            pe.matmul(E[0:FFN_E, 0:nb], const("partitions", PARTS), pl[0:PARTS, 400:400 + nb], start=True, stop=True).then_inc(rt_pe, 1)
            pe.wait_ge(rt_dve, 5)
            pe.wait_ge(ffn_in, 64)
            pe.wait_ge(xt_evac, groups)
            for c in range(CHUNKS):
                pe.matmul(A[c // 8][:, (c % 8) * nb:(c % 8) * nb + nb], const("expert_of_row", FFN_E)[:, c * P:c * P + P],
                          pl[0:FFN_E, 500:500 + nb], start=True, stop=True)
            pe.matmul(B[0][:, 0:nb], fb2[:], pl[0:FFN_E, 500:500 + nb], start=True, stop=True).then_inc(rt_pe, 1)
            pe.wait_ge(rt_dve, 6)

            def up(g, c):
                n = 16 * g + c
                wait(pe, gelu_done, n - 3)
                pe.matmul(ring[c % 4][:], f1[:, c * P:c * P + P], group_rows(H2, g), start=True, stop=True).then_inc(up_done, 1)

            def group(g, par):
                if ongroup(g) and isinstance(g, int) and g == 0:
                    for c in range(3):
                        up(g, c)
                for c in range(CHUNKS):
                    if ongroup(g):
                        if c == 0:
                            wait(pe, ot_ready, g)
                        wait(pe, hw_ready, 16 * g + c + 1)
                        pe.matmul(D[:], f2[:, c, :], hidw[:, c % 4].rearrange("p b d -> p (b d)"), start=c == 0,
                                  stop=c == CHUNKS - 1).then_inc(down_done, 1)
                        if c + 3 < CHUNKS:
                            up(g, c + 3)
                        elif ongroup(g + 1):
                            up(g + 1, c + 3 - CHUNKS)
                    if c == 3 and ongroup(g - 1):
                        wait(pe, ffn_added, g - 1)
                        wait(pe, ot_ready, g)
                        for k in range(4):
                            last = pe.transpose(E[:, k * P:k * P + P], ot[:, k, :], ident)
                        last.then_inc(ott_done, 1)

            run_groups(pe, group, groups + 1)
            finish(pe, 1)

            enter(pe, 2)
            pe.wait_ge(late_in, 9 * 16)
            for c in range(HDC):
                last = pe.transpose(C[c // 4][:, (c % 4) * P:(c % 4) * P + P], ip_raw[:, c, :], ident)
            last.then_inc(c_pe, 1)
            pe.wait_ge(c_dve, 2)
            pe.matmul(D[:, 0:1], const("ones"), dt_sum, start=True, stop=True).then_inc(c_pe, 1)
            pe.wait_ge(c_act, 2)
            for c in range(HDC):
                last = pe.matmul(E[:, 0:P + STATES], ipT[:, c, :], ops[:, c, :], start=c == 0, stop=c == HDC - 1)
            last.then_inc(c_pe, 1)
            pe.wait_ge(c_dve, 3)
            for c in range(HDC):
                last = pe.matmul(D[:, P:2 * P], cproj8[:, c, :], op_raw[:, c, :], start=c == 0, stop=c == HDC - 1)
            last.then_inc(c_pe, 1)
            pe.wait_ge(c_dve, 4)

            def states(g, par):
                if ongroup(g):
                    turn(g, par, cxn, cxn_ready, cxt_evac, ct_done)
                if ongroup(g - 1):
                    o = (par + 1) % 2
                    wait(pe, cz_evac, g - 2)
                    wait(pe, cxt_evac, g)
                    for k in range(4):
                        last = pe.matmul((B, C)[o][k // 2][:, 144 * (k % 2):144 * (k % 2) + 144], cxt[:, o, k, :], state_w,
                                         start=True, stop=True)
                    last.then_inc(cz_done, 1)

            run_groups(pe, states, groups + 1, peeled=4)
            nh = 8 * nb
            pe.wait_ge(cz_evac, groups)
            for h in range(2):
                pe.matmul(A[h][:, 0:nh], mixer, zs.rearrange("p n b -> p (n b)")[:, nh * h:nh * h + nh], start=True,
                          stop=True).then_inc(c_pe, 1)
            pe.wait_ge(c_dve, 5)
            for n in range(STATES):
                last = pe.matmul(B[n // 8][:, (n % 8) * nb:(n % 8) * nb + nb], decays[:, n, :], zm[:, n, :], start=True, stop=True)
                if n % 8 == 7:
                    last.then_inc(c_pe, 1)
            pe.wait_ge(c_dve, 6)
            for q in range(nb // 8):
                last = pe.transpose(C[q // 4][:, (q % 4) * P:(q % 4) * P + P], hb[:, 8 * q:8 * q + 8, :].rearrange("p b n -> p (b n)"), ident)
            last.then_inc(c_pe, 1)
            pe.wait_ge(c_act, 3)
            for q in range(nb // 8):
                for h in range(2):
                    if q >= 2:
                        pe.wait_ge(c_added, groups + 2 * (q - 2) + h + 1)
                    pe.matmul((A, B)[q % 2][h][:], hT[:, q, :], back8.rearrange("p b d -> p (b d)")[:, 512 * h:512 * h + 512],
                              start=True, stop=True).then_inc(c_pe, 1)
            finish(pe, 2)

            enter(pe, 3)
            pe.wait_ge(dw_in, 6 * 16)
            pe.wait_ge(d_prep_dve, 1)
            for k, w in enumerate((aq, ak, av)):
                pe.matmul(D[:, k:k + 1], w, be1_col, start=True, stop=True)
            pe.matmul(D[:, 8:8 + MOE_E], be2_all, router_w, start=True, stop=True)
            pe.wait_ge(moe_in, 48)
            for e in range(MOE_E):
                for c in range(MOE_C):
                    k = 16 + e * MOE_C + c
                    last = pe.matmul(D[:, k:k + 1], w1[:, e, c * P:c * P + P], be2_col, start=True, stop=True)
            last.then_inc(d_prep_pe, 1)
            pe.wait_ge(d_prep_dve, 2)
            pe.matmul(D[:, 64:64 + P], bv_all, ao, start=True, stop=True).then_inc(d_prep_pe, 1)
            pe.wait_ge(d_prep_dve, 3)

            def attend(j, par):
                if on(j + 1):
                    wait(pe, d_qv, j + 1)
                    wait(pe, d_ts, j + 2)
                    pe.matmul(A[1][:, 0:P], aq, turned[:, 0, :], start=True, stop=True)
                    pe.matmul(A[1][:, P:2 * P], ak, turned[:, 0, :], start=True, stop=True)
                    pe.matmul(A[1][:, 2 * P:3 * P], turned[:, 0, :], av, start=True, stop=True).then_inc(d_qkv, 1)
                if on(j):
                    wait(pe, d_qv, j + 1)
                    for h, ready in enumerate((d_km0, d_km1)):
                        wait(pe, ready, j + 1)
                        wait(pe, d_exp, 2 * j + h - 1)
                        pe.matmul(C[h][:], qT[:, par % 2], half(km, h), start=True, stop=True).then_inc(d_s, 1)
                if on(j - 4) or on(j - 7):
                    wait(pe, d_ts, j + 2)
                    wait(pe, d_x2, upto(j - 4))
                    wait(pe, d_lg, j - 7)
                    if on(j - 4):
                        pe.matmul(E[:, 0:P], ident, ctx_bias, start=True, stop=False)
                        last = pe.matmul(E[:, 0:P], turned[:, 1, :], ao, start=False, stop=True)
                    if on(j - 7):
                        last = pe.matmul(E[:, P:P + MOE_E], turned[:, 2, :], router_w, start=True, stop=True)
                    last.then_inc(d_wl, 1)
                if on(j + 2) or on(j - 3) or on(j - 6):
                    wait(pe, d_ts, j + 2)
                    for k, (o, src, ready) in enumerate(((2, n2[:, par % 2], d_n2), (-3, ctxs, d_ctx), (-6, n3[:, par % 2], d_n3))):
                        if on(j + o):
                            wait(pe, ready, j + o + 1)
                            last = pe.transpose(A[0][:, k * P:k * P + P], src, ident)
                    last.then_inc(d_t3, 1)
                if on(j - 2):
                    wait(pe, d_ctx, j - 2)
                    wait(pe, d_pts, 2 * j - 2)
                    for h in range(HEADS):
                        last = pe.matmul(D[:, h * (DK + 1):(h + 1) * (DK + 1)], pts2[:, h, :], vals[:, (par - 2) % 4, h, :],
                                         start=True, stop=True)
                    last.then_inc(d_pv, 1)
                if on(j - 1):
                    for h in range(2):
                        wait(pe, d_pts, 2 * j + h - 3)
                        wait(pe, d_exp, 2 * j + h - 1)
                        for k in range(4):
                            last = pe.transpose(B[h][:, k * P:k * P + P], prob2[:, (par + 1) % 2, 4 * h + k, :], ident)
                        last.then_inc(d_pt, 1)

            run_steps(pe, attend, **D_STEPS)
            finish(pe, 3)

            enter(pe, 4)
            n8 = nb * MOE_E
            for src, banks, ready in ((chosen, A, 2), (final, B, 3)):
                pe.wait_ge(e_dve, ready)
                flat = src.rearrange("p b e -> p (b e)")
                pe.matmul(banks[0][:, 0:n8], const("before"), flat, start=True, stop=True)
                pe.matmul(banks[1][:, 0:n8], const("ones"), flat, start=True, stop=True).then_inc(e_pe, 1)
            pe.wait_ge(moe_in, 48)
            enter(pe, 5)

            def tile(i, k):
                t = 4 * i + k
                if ontile(t + 1):
                    n = (k + 1) % 4
                    wait(pe, f_xt, t)
                    wait(pe, f_in[n], 16 * (i + (k + 1) // 4) + 16)
                    pe.transpose(A[n % 2][:, 0:P], tile_x[:, n, 0:P], ident).then_inc(f_t, 1)
                if ontile(t):
                    wait(pe, f_g, t - 1)
                    wait(pe, f_w, t + 1)
                    wait(pe, f_xt, t + 1)
                    for c in range(MOE_C):
                        last = pe.matmul(B[k % 2][:, c * P:c * P + P], tile_w1[:, k % 2, c * P:c * P + P], tile_xT[:, k % 2, :],
                                         start=True, stop=True)
                    last.then_inc(f_u, 1)
                if ontile(t - 1):
                    n = (k - 1) % 2
                    e = pe.value_load(table_i[0:1, at(t - 1)], min_val=0, max_val=MOE_E - 1)
                    wait(pe, f_y, t - 2)
                    wait(pe, f_g, t)
                    for c in range(MOE_C):
                        last = pe.matmul(C[n][:, 0:P], tile_h[:, n, c, :], w2[:, at(e), c, :], start=c == 0,
                                         stop=c == MOE_C - 1)
                    last.then_inc(f_d, 1)

            run_tiles(pe, tile)


INPUTS = ["x", "L0_tok_token_table", "L0_tok_pos_table", "L0_tok_row_table", "L0_tok_col_table", "L0_tok_w_spatial",
          "L0_tok_ln_gamma", "L0_tok_ln_beta", "L0_attn_Wq", "L0_attn_bq", "L0_attn_Wk", "L0_attn_bk", "L0_attn_Wv",
          "L0_attn_bv", "L0_attn_Wp", "L0_attn_bp", "L0_ffn_router_w", "L0_ffn_W1", "L0_ffn_b1", "L0_ffn_W2",
          "L0_ffn_b2", "L1_attn_input_proj", "L1_attn_output_proj", "L1_attn_a_log", "L1_attn_b_proj",
          "L1_attn_c_proj", "L1_attn_dt_proj", "L1_attn_skip_proj", "L1_attn_amplitudes_real",
          "L1_attn_amplitudes_imag", "L1_attn_rotation_angles", "L1_attn_walk_hamiltonian", "L1_ffn_ln1_g",
          "L1_ffn_ln1_b", "L1_ffn_ln2_g", "L1_ffn_ln2_b", "L1_ffn_wq", "L1_ffn_bq", "L1_ffn_wk", "L1_ffn_bk",
          "L1_ffn_wv", "L1_ffn_bv", "L1_ffn_wo", "L1_ffn_bo", "L1_ffn_router_w", "L1_ffn_router_b", "L1_ffn_w1",
          "L1_ffn_b1", "L1_ffn_w2", "L1_ffn_b2"]


def kernel(**inputs):
    import concourse.bacc as bacc
    from concourse.bass_utils import run_bass_kernel_spmd

    nb = inputs["x"].shape[0]
    blob, where = constants(nb)
    nc = bacc.Bacc("TRN2", target_bir_lowering=False, num_devices=1)
    arrays, io = {}, {}
    for name in INPUTS + ["constants"]:
        a = blob if name == "constants" else np.ascontiguousarray(inputs[name])
        arrays[f"in_{name}"] = a
        io[name] = nc.dram_tensor(f"in_{name}", a.shape, mybir.dt.from_np(a.dtype), kind="ExternalInput").ap()
    out = nc.dram_tensor("out_0", (nb, P, P), F32, kind="ExternalOutput").ap()
    build(nc, io, out, nb, where)
    r = run_bass_kernel_spmd(nc, [arrays], core_ids=[0])
    return r.results[0]["out_0"]
```

```python
import math
from contextlib import ExitStack

import numpy as np

import concourse.bass as bass
from concourse import mybir

F32 = mybir.dt.float32
I32 = mybir.dt.int32
F32R = mybir.dt.float32r
ALU = mybir.AluOpType
ACT = mybir.ActivationFunctionType
X = mybir.AxisListType.X

P = 128
LN_EPS = 1e-5
BOS, EOS, PAD, ROW, SEP = 11, 12, 10, 13, 14
VOCAB, MAX_H, MAX_W = 15, 30, 30
NO_CELL = 99.0
HEADS = 8
PARTS_ROOM = 14336
ATT_SHIFT = 0.125
FFN_E, FFN_F, PARTS = 6, 341, 11
FFN_ROWS = FFN_E * FFN_F
CHUNKS = -(-FFN_ROWS // P)
STATES = 16
HD = 1024
HDC = HD // P
ENT = 0.3
DK = P // HEADS
MOE_E, MOE_F = 8, 512
MOE_C = MOE_F // P
TABLE_ROWS = 96
SCALE = 1.0 / math.sqrt(P)
TWO_PI = 2.0 * math.pi
ROUND = 1.5 * 2.0 ** 23
PARTITIONS_OF_6 = [(6,), (5, 1), (4, 2), (4, 1, 1), (3, 3), (3, 2, 1), (3, 1, 1, 1), (2, 2, 2),
                   (2, 2, 1, 1), (2, 1, 1, 1, 1), (1, 1, 1, 1, 1, 1)]


def sizes(nb):
    tokens = nb * P
    cap = int(np.ceil(tokens * 1.6 / MOE_E))
    tiles = tokens // P + MOE_E - 1
    return tokens, cap, tiles


def constants(nb):
    tokens, cap, tiles = sizes(nb)
    i = np.arange(P)
    f = np.arange(P // 2 + 1)
    band0 = (f * 2 // len(f)) == 0
    weight = np.where((f == 0) | (f == P // 2), 1.0, 2.0)
    wave = np.cos(2 * np.pi * f[None, None, :] * (i[:, None, None] - i[None, :, None]) / P) * weight / P
    parts = {
        "ident": np.eye(P),
        "centre": np.eye(P) - 1.0 / P,
        "low_band": wave[:, :, band0].sum(-1),
        "high_band": wave[:, :, ~band0].sum(-1),
        "before": (i[:, None] < i[None, :]) * 1.0,
        "ones": np.ones((P, P)),
        "age": np.maximum(i[None, :] - i[:, None], 0) * 1.0,
        "causal": (i[None, :] >= i[:, None]) * 1.0,
        "head_of_row": (i[:, None] // DK == np.arange(HEADS)[None, :]) * 1.0,
        "octet_of_row": (i[:, None] // STATES == np.arange(8)[None, :]) * 1.0,
    }
    key = np.full((P, 1), -7.0)
    key[:VOCAB, 0] = np.arange(VOCAB)
    key[32:32 + MAX_H, 0] = np.arange(MAX_H)
    key[64:64 + MAX_W, 0] = np.arange(MAX_W)
    parts["key"] = key
    spread = np.zeros((P, TABLE_ROWS))
    for r in range(3):
        spread[r, 32 * r:32 * r + 32] = 1.0
    parts["spread"] = spread
    pick = np.zeros((P, FFN_E))
    for r, partition in enumerate(PARTITIONS_OF_6):
        for c, part in enumerate(partition):
            pick[r, c] = part / 6
    parts["partitions"] = pick
    rows = np.zeros((P, CHUNKS * P))
    for e in range(FFN_E):
        rows[e, e * FFN_F:(e + 1) * FFN_F] = 1.0
    parts["expert_of_row"] = rows
    parts["earlier_part"] = np.tile((np.arange(PARTS)[None, :] < np.arange(PARTS)[:, None])
                                    .reshape(1, -1) * 1.0, (P, 1))
    parts["earliness"] = np.tile(np.arange(MOE_E, 0, -1)[None, :] * 1.0, (P, 1))
    parts["expert_number"] = np.tile(np.arange(1, MOE_E + 1)[None, :] * 1.0, (P, 1))
    parts["token_number"] = i[:, None] + P * np.arange(nb)[None, :] * 1.0
    parts["tile_number"] = np.tile(np.arange(tiles)[None, :] * 1.0, (P, 1))
    where, at = {}, 0
    for name, a in parts.items():
        where[name] = (at, a.shape[1])
        at += a.shape[1]
    return np.concatenate(list(parts.values()), axis=1).astype(np.float32), where


def wait(eng, sem, n, own=False):
    if isinstance(n, int):
        if n > 0:
            eng.wait_ge(sem, n)
        return
    value = eng.to_reg(n)
    if own:
        eng.wait_ge(sem, 1)
    eng.wait_ge(sem, value)


def at(start, n=1):
    return bass.ds(start, n)


def build(nc, io, out, nb, where):
    tokens, cap, tiles = sizes(nb)
    sorted_rows = tiles * P
    groups = nb // 4
    n_const = sum(w for _, w in where.values())
    ids_rows = nc.dram_tensor("ids_rows", (3, nb, P), F32).ap()
    sorted_x = nc.dram_tensor("sorted_x", (sorted_rows, P + 1), F32).ap()

    with ExitStack() as ctx:
        def sb(name, shape, dt=F32):
            return ctx.enter_context(nc.sbuf_tensor(name, shape, dt))

        def sem(name):
            return ctx.enter_context(nc.semaphore(name))

        bank = [ctx.enter_context(nc.psum_tensor(f"bank{k}", [P, 512], F32)) for k in range(8)]
        A, B, C, D, E = bank[0:2], bank[2:4], bank[4:6], bank[6], bank[7]

        con = sb("con", [P, n_const])

        def const(name, rows=P):
            a, w = where[name]
            return con[0:rows, a:a + w]

        ident = const("ident")
        moe_size = MOE_E * MOE_F
        big = sb("big", [P, max(nb * P, 2 * moe_size)])
        H = big[:, 0:nb * P].rearrange("p (b d) -> p b d", d=P)
        w1 = big[:, 0:moe_size].rearrange("p (e f) -> p e f", f=MOE_F)
        w2 = big[:, moe_size:2 * moe_size].rearrange("p (e c d) -> p e c d", c=MOE_C, d=P)
        wide = sb("wide", [P, nb * (P + 1)])
        H2 = wide[:, 0:nb * P].rearrange("p (b d) -> p b d", d=P)
        named = wide[:].rearrange("p (b d) -> p b d", d=P + 1)
        neg_half = sb("neg_half", [P, 1])

        parts = sb("parts", [P, PARTS_ROOM])

        def part(start, *shape):
            a = parts[:, start:start + int(np.prod(shape))].bitcast(F32R)
            return a if len(shape) == 1 else a.rearrange("p (a b) -> p a b", a=shape[0])

        vec = sb("vec", [P, P])
        vecT = sb("vecT", [P, P])
        empty = sb("empty", [P, P + 1])[:]
        dt_col, skip_col = vecT[:, 0:8], vecT[:, 8:16]
        b1, fb1 = vecT[:, 16:48], vecT[:, 48:64]
        part_w, qkv_b = vecT[:, 64:75], vecT[:, 75:78]
        bq_col, bk_col, bv_col = vecT[:, 75:76], vecT[:, 76:77], vecT[:, 77:78]
        g1_col, be1_col, g2_col, be2_col = (vecT[:, k:k + 1] for k in range(78, 82))
        b2 = sb("b2", [P, MOE_E, P])
        fb2 = sb("fb2", [FFN_E, P])
        rowsP = sb("rowsP", [P, 7, P])
        gamma, beta, bp, bo, ctx_bias, pos = (rowsP[:, k, :] for k in range(6))
        table = rowsP[0:TABLE_ROWS, 6, :]
        small = sb("small", [P, 420])
        taken = [0]

        def piece(n):
            taken[0] += n
            assert taken[0] <= 420
            return small[:, taken[0] - n:taken[0]]

        arena = sb("arena", [P, 12544])
        used = [0]

        def room(*shape):
            n = int(np.prod(shape))
            a = arena[:, used[0]:used[0] + n]
            used[0] += n
            assert used[0] <= 12544, used[0]
            if len(shape) == 2:
                return a.rearrange("p (a b) -> p a b", a=shape[0])
            if len(shape) == 3:
                return a.rearrange("p (a b c) -> p a b c", a=shape[0], b=shape[1])
            return a

        wq, wk, wv, wp = room(HEADS, P), room(HEADS, P), room(HEADS, P), room(HEADS, P)
        gws, xws, prob, pts = room(HEADS, P), room(HEADS, P), room(HEADS, P), room(HEADS, P)
        us = room(2, HEADS, P)
        gs, xs, t0, t1, t2 = room(P), room(P), room(P), room(P), room(P)
        onehot = room(2, P)
        (wk_hi, wk_lo), (wp_hi, wp_lo) = ((part(2048 * k, HEADS, P), part(2048 * k + 1024, HEADS, P)) for k in range(2))
        xs_hi, xs_lo, gs_hi, gs_lo = (part(4096 + P * k, P) for k in range(4))
        raw = [gws, xws, prob]
        bias_rows = big[:, 0:3 * HD].rearrange("p (r n) -> p r n", r=3)
        idrow = H2
        grid_room = us.rearrange("p a h d -> p (a h d)")
        grid = [grid_room[0:nb, 136 * k:136 * k + 129] for k in range(13)]

        mx, negm, rsum, rinv = piece(HEADS), piece(HEADS), piece(HEADS), piece(HEADS)
        st1, mv1, ve1, rs1 = piece(6), piece(2), piece(1), piece(1)
        st2, mv2, ve2, rs2, nb2 = piece(6), piece(2), piece(1), piece(1), piece(1)
        st3, mv3, ve3 = piece(6), piece(2), piece(1)
        amp, rot, walk = piece(4), piece(4), piece(4)
        a_log = piece(STATES)
        spin, turns, waves = piece(8), piece(8), piece(8)
        walk2, walk3, u_re, u_im = piece(4), piece(4), piece(4), piece(4)
        al_re, al_im, be_re, be_im, pr0, pr1 = piece(2), piece(2), piece(2), piece(2), piece(4), piece(4)
        path_w, dt_sum, soft0, soft1 = piece(2), piece(1), piece(HDC), piece(HDC)
        rate = piece(STATES)
        mv4 = piece(8).rearrange("p (b k) -> p b k", k=2)
        mv_all = sb("mv_all", [P, nb, 2])
        st4 = piece(24).rearrange("p (b k) -> p b k", k=6)
        token_sum = sb("token_sum", [P, nb])
        rstd, mrstd = sb("rstd", [P, nb]), sb("mrstd", [P, nb])

        con_in, ids_in, proj_in, table_in, rows_in = (
            sem("con_in"), sem("ids_in"), sem("proj_in"), sem("table_in"), sem("rows_in"))
        wp_in, moe_in, ffn_in = sem("wp_in"), sem("moe_in"), sem("ffn_in")
        bias_in, ids_out = sem("bias_in"), sem("ids_out")
        zeroed, ids_ready, ids_placed = sem("zeroed"), sem("ids_ready"), sem("ids_placed")
        a_prep_pe, a_prep_dve = sem("a_prep_pe"), sem("a_prep_dve")
        bc_done, oh_ready, em_done, em_evac = (
            sem("bc_done"), sem("oh_ready"), sem("em_done"), sem("em_evac"))
        mv1_ready, rs1_ready, t1_ready, h_ready = (
            sem("mv1_ready"), sem("rs1_ready"), sem("t1_ready"), sem("h_ready"))
        mv2_ready, rs2_ready, xs_ready = sem("mv2_ready"), sem("rs2_ready"), sem("xs_ready")
        xl_ready, a_split_dve, a_split_pool = sem("xl_ready"), sem("a_split_dve"), sem("a_split_pool")
        g_done, g_evac = sem("g_done"), sem("g_evac")
        xw_done, xw_evac = sem("xw_done"), sem("xw_evac")
        gw_done, gw_evac = sem("gw_done"), sem("gw_evac")
        u_done, u_evac = sem("u_done"), sem("u_evac")
        s_done, negmax, exp_done, p_ready = (
            sem("s_done"), sem("negmax"), sem("exp_done"), sem("p_ready"))
        pt_done, pt_evac = sem("pt_done"), sem("pt_evac")
        o_done, o_added, bp_added, mv3_ready, rs3_ready = (
            sem("o_done"), sem("o_added"), sem("bp_added"), sem("mv3_ready"), sem("rs3_ready"))
        vec_in, late_in = sem("vec_in"), sem("late_in")
        spin_ready, waves_ready = sem("spin_ready"), sem("waves_ready")
        xn_ready, tb_done, xt_evac = sem("xn_ready"), sem("tb_done"), sem("xt_evac")
        rt_pe, rt_dve, rt_act = sem("rt_pe"), sem("rt_dve"), sem("rt_act")
        up_done, gelu_done, down_done = (
            sem("up_done"), sem("gelu_done"), sem("down_done"))
        hi_ready, lo_ready, w_split, x_split = sem("hi_ready"), sem("lo_ready"), sem("w_split"), sem("x_split")
        x_hi_ready = sem("x_hi_ready")
        f_zeroed = sem("f_zeroed")
        ot_ready, ott_done, ffn_added, mvs_ready, mv_kept = (
            sem("ot_ready"), sem("ott_done"), sem("ffn_added"), sem("mvs_ready"), sem("mv_kept"))
        cxn_ready, ct_done, cxt_evac, cz_done, cz_evac, c_added = (
            sem("cxn_ready"), sem("ct_done"), sem("cxt_evac"), sem("cz_done"), sem("cz_evac"), sem("c_added"))
        c_pe, c_dve, c_act, c_factors = sem("c_pe"), sem("c_dve"), sem("c_act"), sem("c_factors")
        (d_mv1, d_rs1, d_n2, d_qkv, d_qv, d_km0, d_km1, d_pv, d_ctx, d_x2, d_lg, d_mv3, d_rs3, d_hadd, d_n3) = (
            sem(f"d_{n}") for n in ("mv1", "rs1", "n2", "qkv", "qv", "km0", "km1", "pv", "ctx", "x2", "lg", "mv3",
                                    "rs3", "hadd", "n3"))
        d_s, d_neg, d_exp, d_pt, d_pts = (sem(f"d_{n}") for n in ("s", "neg", "exp", "pt", "pts"))
        d_t3, d_ts, d_wl = sem("d_t3"), sem("d_ts"), sem("d_wl")
        dw_in, d_prep_pe, d_prep_dve = sem("dw_in"), sem("d_prep_pe"), sem("d_prep_dve")
        d_based = sem("d_based")
        e_dve, e_pe, e_act = sem("e_dve"), sem("e_pe"), sem("e_act")
        empty_ready, emptied, scattered = sem("empty_ready"), sem("emptied"), sem("scattered")
        f_in = [sem(f"f_in{k}") for k in range(4)]
        f_out = [sem(f"f_out{k}") for k in range(4)]
        f_tok, f_t, f_xt, f_w, f_u, f_g, f_d, f_y = (sem(f"f_{n}") for n in ("tok", "t", "xt", "w", "u", "g", "d", "y"))
        phase_done = [sem(f"phase_{c}_done") for c in "ABCDE"]
        stored = sem("stored")

        def product(eng, dst, lhs, rhs, start=True, stop=True):
            for k, (a, b) in enumerate(((0, 0), (0, 1), (1, 0))):
                last = eng.matmul(dst, lhs[a], rhs[b], start=start and k == 0, stop=stop and k == 2)
            return last

        def half(t, h):
            return t.rearrange("p h d -> p (h d)")[:, 512 * h:512 * h + 512]

        def heads4(b, n=P):
            return b[:, 0:4 * n].rearrange("p (h d) -> p h d", h=4)

        def on(b):
            return not isinstance(b, int) or 0 <= b < nb

        def upto(n, most=nb):
            return min(n, most) if isinstance(n, int) else n

        def run_steps(eng, step, first, last, loop_from, loop_to, unroll):
            trips = (loop_to - loop_from + 1) // unroll
            for j in range(first, loop_from):
                step(j, j % unroll)
            if trips > 0:
                with eng.Fori(0, trips) as i:
                    for k in range(unroll):
                        step(i * unroll + (loop_from + k), (loop_from + k) % unroll)
            for j in range(loop_from + max(trips, 0) * unroll, last + 1):
                step(j, j % unroll)

        def finish(eng, phase):
            eng.drain().then_inc(phase_done[phase], 1)

        def enter(eng, phase):
            eng.wait_ge(phase_done[phase - 1], 3 if phase == 5 else 4)

        A_STEPS = dict(first=-5, last=nb + 1, loop_from=3, loop_to=nb - 6, unroll=2)

        ring = [A[0], A[1], B[0], B[1]]
        used[0] = 0
        w4 = room(CHUNKS, nb)
        xn = room(2, 4, P)
        hid = room(4, 4 * P)
        f1_hi, f1_lo, f2_hi, f2_lo = (part(2048 * k, CHUNKS, P) for k in range(4))
        x_hi, x_lo = part(8192, 2, 4 * P), part(9216, 2, 4 * P)
        hid_hi, hid_lo = part(10240, 4, 4 * P), part(12288, 4, 4 * P)
        ot = room(4, P)
        b2w = room(nb)
        pl = room(6 * PARTS * PARTS)
        f1, f2 = room(CHUNKS, P), room(CHUNKS, P)
        low_end = 7568
        used[0] = max(used[0], low_end + STATES * P)
        ip_raw, op_raw = room(HDC, P), room(HDC, P)
        bproj, cproj = room(HDC, STATES), room(HDC, STATES)
        raw_end = used[0]
        used[0] = low_end
        decays = room(STATES, P)
        used[0] = 0
        cxn, cxt = room(2, 4, P), room(2, 4, P)
        used[0] = 2048
        zs, zm = room(STATES, nb), room(STATES, nb)
        used[0] = 4096
        ipT = room(HDC, P)
        ops = room(HDC, P + STATES)
        state_w, mixer, back8 = room(P + STATES), room(P), room(8, P)
        hb = ipT.rearrange("p h d -> p (h d)")[:, 0:STATES * nb].rearrange("p (b n) -> p b n", n=STATES)
        hT = arena[:, 0:1024].rearrange("p (q l) -> p q l", l=P)
        cproj8 = arena[:, 2048:3072].rearrange("p (h d) -> p h d", d=P)

        used[0] = raw_end
        aq, ak, av, ao = room(P), room(P), room(P), room(P)
        router_w, router_b = room(MOE_E), room(MOE_E)
        used[0] = 0
        logits = room(nb, MOE_E)
        km, pts2 = room(HEADS, P), room(HEADS, P)
        prob2 = room(2, HEADS, P)
        vals = room(4, HEADS, DK + 1)
        turned = room(3, P)
        qT, n2, x2, n3 = room(2, P), room(2, P), room(2, P), room(2, P)
        kT, ctxs, bv_all, be2_all = (room(P) for _ in range(4))
        assert used[0] <= raw_end
        mva, mvc, va2, rs2x, mr2x = piece(2), piece(2), piece(2), piece(2), piece(2)
        rsc, mrc, vc, rctx = piece(1), piece(1), piece(1), piece(HEADS)
        sta, stc = piece(6), piece(6)
        used[0] = 512
        probs, first, cmp = room(nb, MOE_E), room(nb, MOE_E), room(nb, MOE_E)
        chosen, kept, final = room(nb, MOE_E), room(nb, MOE_E), room(nb, MOE_E)
        total, running, rank = room(nb, MOE_E), room(nb, MOE_E), room(nb, MOE_E)
        best, slot, total_p, dropped = room(nb), room(nb), room(nb), room(nb)
        slot_i = room(nb).bitcast(I32)
        by_tile = room(tiles, MOE_E)
        tile_e = room(tiles)
        table_i = room(tiles).bitcast(I32)
        filled, ends, starts, base = piece(8), piece(8), piece(8), piece(8)
        tile_x, tile_y = room(4, P + 1), room(4, P)
        tile_token = room(4).bitcast(I32)
        tile_xT = room(2, P)
        tile_w1 = room(4, MOE_F)
        tile_b1, tile_b2 = room(4, MOE_C), room(4, P)
        tile_h = room(2, MOE_C, P)

        def group_rows(t, g):
            return t[:, at(4 * g, 4), :]

        def run_groups(eng, body, last, peeled=2):
            trips = (last - 2 - peeled) // 2
            for g in range(peeled):
                body(g, g % 2)
            if trips > 0:
                with eng.Fori(0, trips) as i:
                    for k in range(2):
                        body(i * 2 + (peeled + k), k)
            for g in range(peeled + 2 * max(trips, 0), last):
                body(g, g % 2)

        def ongroup(g):
            return not isinstance(g, int) or 0 <= g < groups

        block = ctx.enter_context(nc.Block())

        ffn_b1 = io["L0_ffn_b1"].rearrange("e f -> (e f)")

        D_STEPS = dict(first=-4, last=nb + 6, loop_from=8, loop_to=nb - 5, unroll=4)

        def run_tiles(eng, step):
            full = (tiles - 2) // 4
            for i in range(-1, 2):
                for k in range(4):
                    step(i, k)
            if full > 2:
                with eng.Fori(2, full) as i:
                    for k in range(4):
                        step(i, k)
            for i in range(max(full, 2), -(-(tiles + 2) // 4)):
                for k in range(4):
                    step(i, k)

        def ontile(t):
            return not isinstance(t, int) or 0 <= t < tiles

        @block.sync
        def _(sp):
            sp.dma_start(grid[0].bitcast(I32)[:, 0:P], io["x"]).then_inc(ids_in, 16)
            for dst, n in ((amp[:, 0:2], "amplitudes_real"), (amp[:, 2:4], "amplitudes_imag"), (a_log, "a_log")):
                sp.dma_start(dst, io["L1_attn_" + n].partition_broadcast(P)).then_inc(late_in, 16)
            for dst, n in ((rot, "rotation_angles"), (walk, "walk_hamiltonian")):
                sp.dma_start(dst, io["L1_attn_" + n].rearrange("a b -> (a b)").partition_broadcast(P)).then_inc(late_in, 16)
            sp.dma_start(con[:], io["constants"]).then_inc(con_in, 16)
            for k, n in enumerate("qkv"):
                sp.dma_start(raw[k].rearrange("p h d -> p (h d)"), io[f"L0_attn_W{n}"]).then_inc(proj_in, 16)
            for k, n in enumerate("qkv"):
                sp.dma_start(bias_rows[:, k, :], io[f"L0_attn_b{n}"].partition_broadcast(P)).then_inc(bias_in, 16)
            sp.wait_ge(zeroed, 2)
            sp.dma_start(table[0:VOCAB, :], io["L0_tok_token_table"]).then_inc(table_in, 16)
            sp.dma_start(t1[32:32 + MAX_H, 0:64], io["L0_tok_row_table"]).then_inc(table_in, 16)
            sp.dma_start(t1[64:64 + MAX_W, 64:128], io["L0_tok_col_table"]).then_inc(table_in, 16)
            sp.dma_start(t0, io["L0_tok_w_spatial"]).then_inc(table_in, 16)
            for k, n in enumerate(["L0_tok_ln_gamma", "L0_tok_ln_beta", "L0_attn_bp", "L1_ffn_bo"]):
                sp.dma_start(rowsP[:, k, :], io[n].partition_broadcast(P)).then_inc(rows_in, 16)
            sp.dma_start(pos, io["L0_tok_pos_table"][0:P, :]).then_inc(rows_in, 16)
            sp.dma_start(wp, io["L0_attn_Wp"].rearrange("(h n) d -> n h d", h=HEADS)).then_inc(wp_in, 16)
            for r, a in ((0, io["L1_attn_dt_proj"].rearrange("(c p) -> c p", p=P)),
                         (8, io["L1_attn_skip_proj"].rearrange("(c p) -> c p", p=P)),
                         (16, io["L1_ffn_b1"].rearrange("e (c p) -> (e c) p", p=P)),
                         (48, ffn_b1[0:15 * P].rearrange("(c p) -> c p", p=P)),
                         (64, io["L0_ffn_router_w"]), (75, io["L1_ffn_bq"].unsqueeze(0)),
                         (76, io["L1_ffn_bk"].unsqueeze(0)), (77, io["L1_ffn_bv"].unsqueeze(0)),
                         (78, io["L1_ffn_ln1_g"].unsqueeze(0)), (79, io["L1_ffn_ln1_b"].unsqueeze(0)),
                         (80, io["L1_ffn_ln2_g"].unsqueeze(0)), (81, io["L1_ffn_ln2_b"].unsqueeze(0))):
                sp.dma_start(vec[r:r + a.shape[0], :], a).then_inc(vec_in, 16)
            sp.dma_start(vec[63:64, 0:FFN_ROWS - 15 * P], ffn_b1[15 * P:FFN_ROWS].unsqueeze(0)).then_inc(vec_in, 16)
            sp.wait_ge(ids_ready, 1)
            for k in range(3):
                sp.dma_start(ids_rows[k], grid[k][:, 0:P]).then_inc(ids_out, 16)
            sp.wait_ge(ids_out, 48)
            sp.dma_start(idrow[0:3, :, :], ids_rows).then_inc(ids_placed, 16)
            sp.dma_start(fb2[:], io["L0_ffn_b2"]).then_inc(ffn_in, 16)
            sp.dma_start(b2[:], io["L1_ffn_b2"].rearrange("e d -> (e d)").partition_broadcast(P)
                         .rearrange("p (e d) -> p e d", e=MOE_E)).then_inc(moe_in, 16)
            sp.wait_ge(f_zeroed, 1)
            sp.dma_start(f1.rearrange("p c d -> p (c d)")[:, 0:FFN_ROWS].rearrange("p (e f) -> p e f", e=FFN_E),
                         io["L0_ffn_W1"].rearrange("e d f -> d e f")).then_inc(ffn_in, 16)
            w2_rows = io["L0_ffn_W2"].rearrange("e f d -> (e f) d")
            sp.dma_start(f2[:, 0:15, :], w2_rows[0:15 * P, :].rearrange("(c p) d -> p c d", p=P)).then_inc(ffn_in, 16)
            sp.dma_start(f2[0:FFN_ROWS - 15 * P, 15, :], w2_rows[15 * P:FFN_ROWS, :]).then_inc(ffn_in, 16)
            sp.dma_start(ip_raw, io["L1_attn_input_proj"].rearrange("d (c p) -> d c p", p=P)).then_inc(late_in, 16)
            sp.dma_start(op_raw, io["L1_attn_output_proj"].rearrange("(c p) d -> p c d", p=P)).then_inc(late_in, 16)
            sp.dma_start(bproj, io["L1_attn_b_proj"].rearrange("(c p) n -> p c n", p=P)).then_inc(late_in, 16)
            sp.dma_start(cproj, io["L1_attn_c_proj"].rearrange("(c p) n -> p c n", p=P)).then_inc(late_in, 16)
            sp.wait_ge(empty_ready, 1)
            sp.dma_start(sorted_x.rearrange("(p c) d -> p c d", p=P),
                         empty.unsqueeze(1).broadcast_to([P, tiles, P + 1])).then_inc(emptied, 16)
            sp.wait_ge(phase_done[1], 4)
            for dst, n in ((aq, "wq"), (ak, "wk"), (av, "wv"), (ao, "wo"), (router_w, "router_w")):
                sp.dma_start(dst, io["L1_ffn_" + n]).then_inc(dw_in, 16)
            sp.dma_start(router_b, io["L1_ffn_router_b"].partition_broadcast(P)).then_inc(dw_in, 16)
            with sp.Fori(0, groups) as g:
                sp.wait_ge(d_hadd, 4 * g + 4)
                sp.dma_start(out[at(4 * g, 4), :, :].rearrange("b t d -> t b d"),
                             H[:, at(4 * g, 4), :]).then_inc(stored, 16)
            sp.wait_ge(phase_done[3], 4)
            sp.wait_ge(stored, 16 * groups)
            sp.dma_start(w1, io["L1_ffn_w1"].rearrange("e d f -> d e f")).then_inc(moe_in, 16)
            sp.dma_start(w2, io["L1_ffn_w2"].rearrange("e (c f) d -> f e c d", c=MOE_C)).then_inc(moe_in, 16)
            sp.wait_ge(scattered, 16 * nb)

            def tile(i, k):
                t = 4 * i + k
                if ontile(t + 3):
                    wait(sp, f_t, t, own=True)
                    wait(sp, f_tok, t)
                    n = (k + 3) % 4
                    sp.dma_start(tile_x[:, n, :], sorted_x[at((t + 3) * P, P), :]).then_inc(f_in[n], 16)

            run_tiles(sp, tile)
            sp.wait_ge(stored, 16 * groups)

        @block.gpsimd
        def _(pool):
            pool.memset(t1, 0.0)
            pool.memset(rowsP[:, 6, :], 0.0)
            pool.memset(vec[:], 0.0)
            pool.memset(empty[:, 0:P], 0.0)
            pool.memset(empty[:, P:P + 1].bitcast(I32), tokens)
            pool.drain().then_inc(empty_ready, 1)
            pool.drain().then_inc(zeroed, 2)
            pool.memset(neg_half[:], -0.5)
            pool.drain()
            pool.wait_ge(rows_in, 5 * 16)

            def rsqrt(out, ve, mv):
                pool.tensor_scalar(ve, mv[:, 1:2], LN_EPS, None, ALU.add)
                pool.drain()
                return pool.tensor_tensor(out, ve, neg_half[:], ALU.pow)

            pool.wait_ge(wp_in, 16)
            pool.tensor_copy(wp_hi, wp)
            pool.drain()
            pool.tensor_tensor(wp_lo, wp, wp_hi.bitcast(F32), ALU.subtract).then_inc(a_split_pool, 1)

            def step(j, par):
                if on(j + 1):
                    wait(pool, xw_done, 2 * j + 2)
                    wait(pool, xs_ready, j + 2)
                    pool.tensor_tensor(xs_lo, xs, xs_hi.bitcast(F32), ALU.subtract).then_inc(xl_ready, 1)
                if on(j + 3):
                    wait(pool, t1_ready, j + 4)
                    pool.tensor_tensor(t2, t1, gamma, ALU.mult)
                    pool.drain()
                    pool.tensor_tensor(H[:, at(j + 3), :], t2.unsqueeze(1), beta.unsqueeze(1), ALU.add).then_inc(h_ready, 1)
                if on(j - 1):
                    wait(pool, o_added, j)
                    pool.tensor_tensor(H[:, at(j - 1), :], H[:, at(j - 1), :], bp.unsqueeze(1),
                                       ALU.add).then_inc(bp_added, 1)
                if on(j + 2):
                    wait(pool, xs_ready, j + 2, own=True)
                    wait(pool, mv2_ready, j + 3)
                    rsqrt(rs2, ve2, mv2)
                    pool.drain()
                    pool.tensor_tensor(nb2, mv2[:, 0:1], rs2, ALU.mult)
                    pool.drain()
                    pool.tensor_scalar(nb2, nb2, -1.0, ATT_SHIFT, ALU.mult, ALU.add).then_inc(rs2_ready, 1)
                if on(j + 4):
                    wait(pool, mv1_ready, j + 5, own=True)
                    rsqrt(rs1, ve1, mv1).then_inc(rs1_ready, 1)
                if on(j - 2):
                    wait(pool, mv3_ready, j - 1, own=True)
                    pool.tensor_scalar(ve3, mv3[:, 1:2], LN_EPS, None, ALU.add)
                    pool.drain()
                    pool.tensor_tensor(rstd[:, at(j - 2)], ve3, neg_half[:], ALU.pow)
                    pool.drain()
                    pool.tensor_tensor(mrstd[:, at(j - 2)], mv3[:, 0:1], rstd[:, at(j - 2)], ALU.mult).then_inc(rs3_ready, 1)

            run_steps(pool, step, **A_STEPS)
            finish(pool, 0)

            enter(pool, 1)
            f1_rows = f1.rearrange("p c d -> p (c d)")
            pool.memset(f1_rows[:, FFN_ROWS:CHUNKS * P], 0.0)
            pool.memset(f2[:, 15, :], 0.0)
            pool.drain().then_inc(f_zeroed, 1)
            pool.wait_ge(ffn_in, 64)
            for w, hi in ((f1, f1_hi), (f2, f2_hi)):
                pool.tensor_copy(hi, w)
            pool.drain()
            for w, hi, lo in ((f1, f1_hi, f1_lo), (f2, f2_hi, f2_lo)):
                pool.tensor_tensor(lo, w, hi.bitcast(F32), ALU.subtract)
            pool.drain().then_inc(w_split, 1)

            def group(g, par):
                for c in range(CHUNKS):
                    n = 16 * g + c
                    if ongroup(g):
                        wait(pool, down_done, n - 3)
                        wait(pool, hi_ready, n + 1)
                        pool.tensor_tensor(hid_lo[:, c % 4], hid[:, c % 4], hid_hi[:, c % 4].bitcast(F32),
                                           ALU.subtract).then_inc(lo_ready, 1)

            run_groups(pool, group, groups)
            finish(pool, 1)
            enter(pool, 2)
            pool.tensor_scalar(rstd[:], mv_all[:, :, 1], LN_EPS, None, ALU.add)
            pool.drain()
            pool.tensor_tensor(rstd[:], rstd[:], neg_half[:].broadcast_to([P, nb]), ALU.pow)
            pool.drain()
            pool.tensor_tensor(mrstd[:], mv_all[:, :, 0], rstd[:], ALU.mult).then_inc(c_factors, 1)
            finish(pool, 2)

            enter(pool, 3)
            pool.wait_ge(d_prep_dve, 3)
            pool.memset(vals[:, :, :, DK:DK + 1], 1.0)
            pool.drain()

            def attend(j, par):
                if on(j + 4):
                    wait(pool, d_n2, j + 4, own=True)
                    wait(pool, d_mv1, j + 5, own=True)
                    pool.tensor_scalar(va2[:, 0:1], mva[:, 1:2], LN_EPS, None, ALU.add)
                    pool.tensor_scalar(va2[:, 1:2], mva[:, 1:2], 1 + LN_EPS, LN_EPS ** 2, ALU.mult, ALU.add)
                    pool.drain()
                    pool.tensor_tensor(rs2x, va2, neg_half[:].broadcast_to([P, 2]), ALU.pow)
                    pool.drain()
                    pool.tensor_scalar(mr2x, rs2x, mva[:, 0:1], None, ALU.mult)
                    pool.drain().then_inc(d_rs1, 1)
                if on(j + 1):
                    wait(pool, d_s, 2 * j + 2)
                    wait(pool, d_qv, j + 2)
                    pool.tensor_tensor(km[:, 4:8, :], kT.unsqueeze(1).broadcast_to([P, 4, P]),
                                       const("head_of_row")[:, 4:8].unsqueeze(2).broadcast_to([P, 4, P]),
                                       ALU.mult).then_inc(d_km1, 1)
                if on(j + 2):
                    wait(pool, d_n2, j + 3)
                    row = named[:, at(j + 2), 0:P]
                    pool.tensor_tensor(row, row, ctx_bias.unsqueeze(1), ALU.add).then_inc(d_based, 1)
                if on(j - 4):
                    wait(pool, d_x2, j - 3)
                    rows = H[:, at(j - 4), :]
                    pool.tensor_tensor(rows, rows, x2[:, par % 2].unsqueeze(1), ALU.add).then_inc(d_hadd, 1)
                    wait(pool, d_n3, j - 4, own=True)
                    wait(pool, d_mv3, j - 3)
                    rsqrt(rsc, vc, mvc)
                    pool.drain()
                    pool.tensor_scalar(mrc, rsc, mvc[:, 0:1], -1.0, ALU.mult, ALU.mult).then_inc(d_rs3, 1)

            run_steps(pool, attend, **D_STEPS)
            finish(pool, 3)
            pool.wait_ge(e_dve, 4)
            pool.wait_ge(emptied, 16)
            for b in range(nb):
                pool.indirect_dma_start(sorted_x, bass.IndirectOffsetOnAxis(ap=slot_i[:, b:b + 1], axis=0), named[:, b, :],
                                        None, bounds_check=sorted_rows - 1, oob_is_err=False).then_inc(scattered, 16)
            finish(pool, 4)
            pool.wait_ge(stored, 16 * groups)

            def tile(i, k):
                t = 4 * i + k
                if ontile(t - 1):
                    n = (k - 1) % 4
                    wait(pool, f_tok, t, own=True)
                    wait(pool, f_y, t, own=True)
                    pool.indirect_dma_start(out.rearrange("b t d -> (b t) d"),
                                            bass.IndirectOffsetOnAxis(ap=tile_token[:, n:n + 1], axis=0), tile_y[:, n, :], None,
                                            bounds_check=tokens - 1, oob_is_err=False,
                                            compute_op=ALU.add).then_inc(f_out[n], 16)

            run_tiles(pool, tile)
            for n in range(4):
                pool.wait_ge(f_out[n], 16 * len(range(n, tiles, 4)))

        def quantum_weights(dve):
            m2 = [walk.rearrange("p (i j) -> p i j", j=2), walk2.rearrange("p (i j) -> p i j", j=2),
                  walk3.rearrange("p (i j) -> p i j", j=2)]
            v0, v1 = pr0.rearrange("p (i j) -> p i j", j=2), pr1.rearrange("p (i j) -> p i j", j=2)
            dve.wait_ge(late_in, 5 * 16)
            dve.tensor_copy(spin[:, 0:4], rot)
            dve.tensor_scalar(spin[:, 4:8], rot, math.pi / 2, None, ALU.add)
            dve.drain()
            dve.tensor_scalar(turns, spin, 1.0 / TWO_PI, None, ALU.mult)
            dve.drain()
            dve.tensor_scalar(turns, turns, ROUND, None, ALU.add)
            dve.drain()
            dve.tensor_scalar(turns, turns, -ROUND, None, ALU.add)
            dve.drain()
            dve.scalar_tensor_tensor(spin, turns, -TWO_PI, spin, ALU.mult, ALU.add)
            dve.drain()
            dve.tensor_scalar(spin, spin, 3.1415925, -3.1415925, ALU.min, ALU.max)
            dve.drain().then_inc(spin_ready, 1)
            for n in (0, 1):
                dve.tensor_tensor(v0, m2[n][:, :, 0:1].broadcast_to([P, 2, 2]), m2[0][:, 0:1, :].broadcast_to([P, 2, 2]), ALU.mult)
                dve.tensor_tensor(v1, m2[n][:, :, 1:2].broadcast_to([P, 2, 2]), m2[0][:, 1:2, :].broadcast_to([P, 2, 2]), ALU.mult)
                dve.drain()
                dve.tensor_tensor(m2[n + 1], v0, v1, ALU.add)
                dve.drain()
            dve.tensor_scalar(u_re, walk2, -ENT * ENT / 2, None, ALU.mult)
            dve.tensor_scalar(u_im, walk3, -ENT * ENT * ENT / 6, None, ALU.mult)
            dve.drain()
            dve.scalar_tensor_tensor(u_im, walk, ENT, u_im, ALU.mult, ALU.add)
            dve.tensor_scalar(u_re[:, 0:4:3], u_re[:, 0:4:3], 1.0, None, ALU.add)
            dve.tensor_copy(al_re, amp[:, 0:2])
            dve.tensor_copy(al_im, amp[:, 2:4])
            dve.drain()
            dve.wait_ge(waves_ready, 1)
            ur, ui = u_re.rearrange("p (i j) -> p i j", j=2), u_im.rearrange("p (i j) -> p i j", j=2)
            for depth in range(2):
                sin, cos = waves[:, 2 * depth:2 * depth + 2], waves[:, 4 + 2 * depth:6 + 2 * depth]
                dve.tensor_tensor(pr0[:, 0:2], sin, al_im, ALU.mult)
                dve.tensor_tensor(pr1[:, 0:2], sin, al_re, ALU.mult)
                dve.tensor_tensor(be_re, cos, al_re, ALU.mult)
                dve.tensor_tensor(be_im, cos, al_im, ALU.mult)
                dve.drain()
                dve.tensor_tensor(be_re, be_re, pr0[:, 0:2], ALU.subtract)
                dve.tensor_tensor(be_im, be_im, pr1[:, 0:2], ALU.add)
                dve.drain()
                for a, b, op, dst in ((be_re, be_im, ALU.subtract, al_re), (be_im, be_re, ALU.add, al_im)):
                    dve.tensor_tensor(v0, ur, a.unsqueeze(1).broadcast_to([P, 2, 2]), ALU.mult)
                    dve.tensor_tensor(v1, ui, b.unsqueeze(1).broadcast_to([P, 2, 2]), ALU.mult)
                    dve.drain()
                    dve.tensor_tensor(v0, v0, v1, op)
                    dve.drain()
                    dve.tensor_reduce(dst, v0, X, ALU.add)
                    dve.drain()
            dve.tensor_tensor(be_re, al_re, al_re, ALU.mult)
            dve.tensor_tensor(be_im, al_im, al_im, ALU.mult)
            dve.drain()
            dve.tensor_tensor(be_re, be_re, be_im, ALU.add)
            dve.drain()
            dve.tensor_reduce(be_im[:, 0:1], be_re, X, ALU.add)
            dve.drain()
            dve.reciprocal(be_im[:, 1:2], be_im[:, 0:1])
            dve.drain()
            dve.tensor_scalar(path_w, be_re, be_im[:, 1:2], None, ALU.mult)
            dve.drain()

        def routing(dve):

            def over_experts(t):
                return t.unsqueeze(2).broadcast_to([P, nb, MOE_E])

            dve.tensor_reduce(best, logits, X, ALU.max)
            dve.drain()
            dve.tensor_tensor(logits, logits, over_experts(best), ALU.subtract)
            dve.drain().then_inc(e_dve, 1)
            dve.wait_ge(e_act, 1)
            dve.tensor_reduce(slot, probs, X, ALU.add)
            dve.drain()
            dve.reciprocal(total_p, slot)
            dve.drain()
            dve.tensor_tensor(probs, probs, over_experts(total_p), ALU.mult)
            dve.drain()
            early = const("earliness").unsqueeze(1).broadcast_to([P, nb, MOE_E])
            for k, pick in enumerate((first, chosen)):
                dve.tensor_reduce(best, probs, X, ALU.max)
                dve.drain()
                dve.tensor_tensor(cmp, probs, over_experts(best), ALU.is_equal)
                dve.drain()
                dve.tensor_tensor(cmp, cmp, early, ALU.mult)
                dve.drain()
                dve.tensor_reduce(best, cmp, X, ALU.max)
                dve.drain()
                dve.tensor_tensor(pick, cmp, over_experts(best), ALU.is_equal)
                dve.drain()
                if k == 0:
                    dve.scalar_tensor_tensor(probs, pick, -2.0, probs, ALU.mult, ALU.add)
                    dve.drain()
            dve.tensor_tensor(chosen, chosen, first, ALU.add)
            dve.drain().then_inc(e_dve, 1)

            def places(banks):
                dve.tensor_copy(total, banks[1][:, 0:nb * MOE_E].rearrange("p (b e) -> p b e", e=MOE_E))
                dve.drain()
                for e in range(MOE_E):
                    dve.tensor_tensor_scan(running[:, :, e], const("ones")[:, 0:nb], total[:, :, e], 0.0, ALU.mult, ALU.add)
                dve.drain()
                dve.tensor_tensor(rank, running, total, ALU.subtract)
                dve.drain()
                dve.tensor_tensor(rank, rank, banks[0][:, 0:nb * MOE_E].rearrange("p (b e) -> p b e", e=MOE_E), ALU.add)
                dve.drain()

            dve.wait_ge(e_pe, 1)
            places(A)
            dve.scalar_tensor_tensor(kept, rank, float(cap), chosen, ALU.is_lt, ALU.mult)
            dve.drain()
            dve.tensor_tensor(cmp, kept, const("expert_number").unsqueeze(1).broadcast_to([P, nb, MOE_E]), ALU.mult)
            dve.drain()
            dve.tensor_reduce(best, cmp, X, ALU.max)
            dve.drain()
            dve.tensor_tensor(final, cmp, over_experts(best), ALU.is_equal)
            dve.drain()
            dve.tensor_tensor(final, final, kept, ALU.mult)
            dve.drain().then_inc(e_dve, 1)
            dve.wait_ge(e_pe, 2)
            places(B)
            dve.tensor_scalar(filled, running[:, nb - 1, :], 1.0 / P, 127.0 / 256.0, ALU.mult, ALU.add)
            dve.drain()
            dve.tensor_scalar(filled, filled, ROUND, None, ALU.add)
            dve.drain()
            dve.tensor_scalar(filled, filled, -ROUND, None, ALU.add)
            dve.drain()
            dve.tensor_tensor_scan(ends, const("ones")[:, 0:MOE_E], filled, 0.0, ALU.mult, ALU.add)
            dve.drain()
            dve.tensor_tensor(starts, ends, filled, ALU.subtract)
            dve.drain()
            dve.tensor_scalar(base, starts, float(P), None, ALU.mult)
            dve.drain()
            dve.tensor_tensor(rank, rank, base.unsqueeze(1).broadcast_to([P, nb, MOE_E]), ALU.add)
            dve.tensor_reduce(dropped, final, X, ALU.add)
            dve.drain()
            dve.tensor_tensor(rank, rank, final, ALU.mult)
            dve.tensor_scalar(dropped, dropped, -float(sorted_rows), float(sorted_rows), ALU.mult, ALU.add)
            dve.drain()
            dve.tensor_reduce(slot, rank, X, ALU.add)
            dve.drain()
            dve.tensor_tensor(slot_i, slot, dropped, ALU.add)
            dve.drain().then_inc(e_dve, 1)
            dve.wait_ge(e_pe, 3)
            dve.tensor_tensor(b1, b1, D[:, 0:MOE_E * MOE_C], ALU.add)
            def over_tiles(t):
                return t.unsqueeze(1).broadcast_to([P, tiles, MOE_E])

            numbers = const("tile_number")
            dve.tensor_tensor(by_tile, over_tiles(ends), numbers.unsqueeze(2).broadcast_to([P, tiles, MOE_E]), ALU.is_le)
            dve.drain()
            dve.tensor_reduce(tile_e, by_tile, X, ALU.add)
            dve.drain()
            dve.tensor_scalar(table_i, tile_e, MOE_E - 1.0, None, ALU.min)
            dve.drain().then_inc(e_dve, 1)

        def router0(dve):
            lg, pr, sel = pl[0:nb, 0:11], pl[0:nb, 11:22], pl[0:nb, 22:33]
            m, s, r = pl[0:nb, 33:34], pl[0:nb, 34:35], pl[0:nb, 35:36]
            gt = pl[0:nb, 121:242].rearrange("p (i j) -> p i j", j=PARTS)
            eq = pl[0:nb, 242:363].rearrange("p (i j) -> p i j", j=PARTS)
            dve.drain().then_inc(rt_dve, 1)
            dve.wait_ge(rt_pe, 1)
            dve.tensor_scalar(lg, E[0:nb, 0:PARTS], 1.0 / P, None, ALU.mult)
            dve.drain()
            dve.tensor_reduce(m, lg, X, ALU.max)
            dve.drain()
            dve.tensor_scalar(lg, lg, m, None, ALU.subtract)
            dve.drain().then_inc(rt_dve, 1)
            dve.wait_ge(rt_act, 1)
            dve.reciprocal(r, s)
            dve.drain()
            dve.tensor_scalar(pr, pr, r, None, ALU.mult)
            dve.drain()
            of_i, of_j = pr.unsqueeze(2).broadcast_to([nb, PARTS, PARTS]), pr.unsqueeze(1).broadcast_to([nb, PARTS, PARTS])
            dve.tensor_tensor(gt, of_j, of_i, ALU.is_gt)
            dve.tensor_tensor(eq, of_j, of_i, ALU.is_equal)
            dve.drain()
            dve.tensor_tensor(eq, eq, const("earlier_part", nb).rearrange("p (i j) -> p i j", j=PARTS), ALU.mult)
            dve.drain()
            dve.tensor_tensor(gt, gt, eq, ALU.add)
            dve.drain()
            dve.tensor_reduce(sel, gt, X, ALU.add)
            dve.drain()
            dve.tensor_scalar(sel, sel, 1.5, None, ALU.is_lt)
            dve.drain()
            dve.tensor_tensor(sel, sel, pr, ALU.mult)
            dve.drain()
            dve.tensor_reduce(m, sel, X, ALU.add)
            dve.drain()
            dve.reciprocal(r, m)
            dve.drain()
            dve.tensor_scalar(sel, sel, r, None, ALU.mult)
            dve.drain().then_inc(rt_dve, 1)
            dve.wait_ge(rt_pe, 2)
            dve.tensor_copy(pl[0:PARTS, 400:400 + nb], D[0:PARTS, 0:nb])
            dve.drain().then_inc(rt_dve, 1)
            dve.wait_ge(rt_pe, 3)
            dve.tensor_scalar(pl[0:FFN_E, 500:500 + nb], E[0:FFN_E, 0:nb], 1e-6, None, ALU.is_gt)
            dve.drain()
            dve.tensor_tensor(pl[0:FFN_E, 500:500 + nb], pl[0:FFN_E, 500:500 + nb], E[0:FFN_E, 0:nb], ALU.mult)
            dve.drain().then_inc(rt_dve, 1)
            dve.wait_ge(rt_pe, 4)
            for h in range(2):
                dve.tensor_copy(w4[:, 8 * h:8 * h + 8, :], A[h][:, 0:8 * nb].rearrange("p (c b) -> p c b", c=8))
            dve.tensor_copy(b2w, B[0][:, 0:nb])
            dve.drain().then_inc(rt_dve, 1)

        def state_space_weights(dve):
            dve.tensor_scalar(soft0, dt_col, -1.0, None, ALU.mult)
            dve.drain()
            dve.tensor_tensor(soft0, soft0, dt_col, ALU.max)
            dve.drain().then_inc(c_dve, 1)
            dve.wait_ge(late_in, 9 * 16)
            dve.wait_ge(c_act, 1)
            dve.tensor_scalar(soft0, dt_col, 0.0, None, ALU.max)
            dve.drain()
            dve.tensor_tensor(soft0, soft0, soft1, ALU.add)
            dve.drain()
            dve.tensor_reduce(dt_sum, soft0, X, ALU.add)
            dve.tensor_tensor(ops[:, :, 0:P], op_raw, skip_col.unsqueeze(2).broadcast_to([P, HDC, P]), ALU.mult)
            dve.tensor_tensor(ops[:, :, P:P + STATES], bproj, soft0.unsqueeze(2).broadcast_to([P, HDC, STATES]), ALU.mult)
            dve.tensor_copy(cproj8.rearrange("p c (r n) -> p c r n", n=STATES), cproj.unsqueeze(2).broadcast_to([P, HDC, 8, STATES]))
            dve.drain().then_inc(c_dve, 1)
            dve.wait_ge(c_pe, 2)
            dve.tensor_scalar(soft1[:, 0:1], D[:, 0:1], -1.0 / HD, None, ALU.mult)
            dve.drain()
            dve.tensor_scalar(rate, rate, soft1[:, 0:1], None, ALU.mult)
            dve.drain().then_inc(c_dve, 1)
            dve.tensor_scalar(mixer, const("low_band"), path_w[:, 0:1], None, ALU.mult)
            dve.drain()
            dve.scalar_tensor_tensor(mixer, const("high_band"), path_w[:, 1:2], mixer, ALU.mult, ALU.add)
            dve.wait_ge(c_pe, 3)
            dve.tensor_copy(state_w, E[:, 0:P + STATES])
            dve.wait_ge(c_pe, 4)
            dve.tensor_tensor(back8, D[:, P:2 * P].unsqueeze(1).broadcast_to([P, 8, P]),
                              const("octet_of_row").unsqueeze(2).broadcast_to([P, 8, P]), ALU.mult)
            dve.wait_ge(c_act, 2)
            dve.tensor_tensor(decays, decays, const("causal").unsqueeze(1).broadcast_to([P, STATES, P]), ALU.mult)
            dve.drain().then_inc(c_dve, 1)

        @block.vector
        def _(dve):
            dve.wait_ge(ids_in, 16)
            (tok, row, col, bos, sep, rw, end, color, keep, inside, rowc, colc, g) = grid
            n = P
            dve.tensor_copy(g[:, 0:n], tok[:, 0:n].bitcast(I32))
            dve.drain()
            for dst, code in ((bos, BOS), (sep, SEP), (rw, ROW), (end, EOS), (keep, PAD)):
                dve.tensor_scalar(dst[:, 0:n], g[:, 0:n], float(code), None, ALU.is_equal)
            dve.tensor_scalar(color[:, 0:n], g[:, 0:n], 9.5, None, ALU.is_lt)
            dve.tensor_scalar(col[:, 0:n], g[:, 0:n], -0.5, None, ALU.is_gt)
            dve.tensor_copy(tok[:, 0:n], g[:, 0:n])
            for t in (inside, rowc, colc):
                dve.memset(t[:, 0:1], 0.0)
            dve.drain()
            dve.tensor_tensor(color[:, 0:n], color[:, 0:n], col[:, 0:n], ALU.mult)
            dve.tensor_tensor(end[:, 0:n], end[:, 0:n], keep[:, 0:n], ALU.add)
            dve.drain()
            dve.tensor_tensor(end[:, 0:n], end[:, 0:n], bos[:, 0:n], ALU.add)
            dve.tensor_tensor(sep[:, 0:n], sep[:, 0:n], bos[:, 0:n], ALU.add)
            dve.drain()
            dve.tensor_scalar(keep[:, 0:n], end[:, 0:n], -1.0, 1.0, ALU.mult, ALU.add)
            dve.tensor_scalar(g[:, 0:n], sep[:, 0:n], -1.0, 1.0, ALU.mult, ALU.add)
            dve.drain()
            dve.tensor_tensor_scan(inside[:, 1:n + 1], keep[:, 0:n], bos[:, 0:n], 0.0, ALU.mult, ALU.add)
            dve.tensor_tensor_scan(rowc[:, 1:n + 1], g[:, 0:n], rw[:, 0:n], 0.0, ALU.mult, ALU.add)
            dve.drain()
            dve.tensor_tensor(inside[:, 0:n], inside[:, 0:n], color[:, 0:n], ALU.mult)
            dve.tensor_tensor(g[:, 0:n], g[:, 0:n], rw[:, 0:n], ALU.subtract)
            dve.drain()
            dve.tensor_tensor_scan(colc[:, 1:n + 1], g[:, 0:n], inside[:, 0:n], 0.0, ALU.mult, ALU.add)
            dve.tensor_scalar(color[:, 0:n], color[:, 0:n], -NO_CELL, NO_CELL, ALU.mult, ALU.add)
            dve.drain()
            for dst, src, most in ((row, rowc, MAX_H - 1), (col, colc, MAX_W - 1)):
                dve.tensor_tensor(dst[:, 0:n], src[:, 0:n], inside[:, 0:n], ALU.mult)
                dve.drain()
                dve.tensor_scalar(dst[:, 0:n], dst[:, 0:n], float(most), None, ALU.min)
                dve.drain()
                dve.tensor_tensor(dst[:, 0:n], dst[:, 0:n], color[:, 0:n], ALU.add)
            dve.drain().then_inc(ids_ready, 1)
            quantum_weights(dve)
            dve.wait_ge(bias_in, 48)
            for r, (w, banks) in enumerate(((wq, A), (wk, B), (wv, C))):
                dve.wait_ge(a_prep_pe, r + 1)
                for h in range(2):
                    dve.scalar_tensor_tensor(w[:, :, 64 * h:64 * h + 64].rearrange("p h e -> p e h"),
                                             bias_rows[:, r, 512 * h:512 * h + 512].rearrange("p (e h) -> p e h", h=HEADS),
                                             1.0 / (P * ATT_SHIFT), banks[h][:].rearrange("p (e h) -> p e h", h=HEADS),
                                             ALU.mult, ALU.add)
            dve.wait_ge(a_prep_pe, 4)
            dve.tensor_copy(vecT[:], D[:, 256:384])
            dve.tensor_copy(gs, D[:, 0:P])
            dve.tensor_copy(t2[:, 0:TABLE_ROWS], D[:, P:P + TABLE_ROWS])
            dve.drain().then_inc(a_prep_dve, 1)
            dve.wait_ge(a_prep_pe, 5)
            dve.wait_ge(table_in, 64)
            dve.tensor_tensor(table, table, E[0:TABLE_ROWS, 0:P], ALU.add)
            dve.drain().then_inc(a_prep_dve, 1)
            dve.wait_ge(con_in, 16)
            dve.wait_ge(rows_in, 5 * 16)

            def stats(st, mv, src):
                dve.bn_stats(st, src)
                dve.drain()
                return dve.bn_aggr(mv, st)

            dve.tensor_copy(wk_hi, wk)
            dve.drain()
            dve.tensor_tensor(wk_lo, wk, wk_hi.bitcast(F32), ALU.subtract)
            dve.drain().then_inc(a_split_dve, 1)

            def step(j, par):
                if on(j):
                    for h in range(2):
                        m = slice(4 * h, 4 * h + 4)
                        wait(dve, s_done, 2 * j + h + 1)
                        dve.tensor_reduce(mx[:, m], heads4(C[h]), X, ALU.max)
                        dve.drain()
                        wait(dve, exp_done, 2 * j + h - 1)
                        dve.tensor_scalar(negm[:, m], mx[:, m], -SCALE, None, ALU.mult).then_inc(negmax, 1)
                if on(j + 5):
                    wait(dve, bc_done, j + 6)
                    wait(dve, em_done, j + 4)
                    dve.tensor_scalar(onehot[0:TABLE_ROWS, (par + 1) % 2, :], D[0:TABLE_ROWS, P:2 * P],
                                      const("key", TABLE_ROWS), None, ALU.is_equal).then_inc(oh_ready, 1)
                if on(j + 3):
                    wait(dve, rs1_ready, j + 4)
                    wait(dve, h_ready, j + 3)
                    dve.tensor_scalar(t1, t0, mv1[:, 0:1], rs1, ALU.subtract, ALU.mult).then_inc(t1_ready, 1)
                if on(j - 1):
                    wait(dve, o_done, j)
                    dve.tensor_tensor(H[:, at(j - 1), :], H[:, at(j - 1), :], E[:, 0:P].unsqueeze(1),
                                      ALU.add).then_inc(o_added, 1)
                if on(j + 1):
                    wait(dve, g_done, j + 2)
                    wait(dve, gw_done, 2 * j + 2)
                    dve.tensor_copy(gs_hi, D[:, 0:P])
                    dve.drain()
                    dve.tensor_tensor(gs_lo, D[:, 0:P], gs_hi.bitcast(F32), ALU.subtract).then_inc(g_evac, 1)
                if on(j + 2):
                    wait(dve, rs2_ready, j + 2, own=True)
                    wait(dve, h_ready, j + 3)
                    stats(st2, mv2, H[:, at(j + 2), :]).then_inc(mv2_ready, 1)
                if on(j + 1):
                    wait(dve, u_done, 2 * j + 2)
                    for h in range(2):
                        wait(dve, xw_done, 2 * j + h + 3)
                        dve.tensor_copy(half(xws, h), A[h][:]).then_inc(xw_evac, 1)
                if on(j):
                    for h in range(2):
                        wait(dve, exp_done, 2 * j + h + 1)
                        dve.reciprocal(rinv[:, 4 * h:4 * h + 4], rsum[:, 4 * h:4 * h + 4])
                        dve.drain()
                        p4 = prob[:, 4 * h:4 * h + 4, :]
                        dve.tensor_tensor(p4, p4, rinv[:, 4 * h:4 * h + 4].unsqueeze(2).broadcast_to([P, 4, P]),
                                          ALU.mult).then_inc(p_ready, 1)
                if on(j + 4):
                    wait(dve, t1_ready, j + 4)
                    wait(dve, em_done, j + 5)
                    dve.tensor_tensor(t0, E[:, P:2 * P], pos, ALU.add).then_inc(em_evac, 1)
                    dve.drain()
                    wait(dve, rs1_ready, j + 4, own=True)
                    stats(st1, mv1, t0).then_inc(mv1_ready, 1)
                if on(j - 2):
                    wait(dve, rs3_ready, j - 2, own=True)
                    wait(dve, bp_added, j - 1)
                    stats(st3, mv3, H[:, at(j - 2), :]).then_inc(mv3_ready, 1)
                if on(j + 2):
                    wait(dve, xw_done, upto(2 * j + 4, 2 * nb))
                    wait(dve, rs2_ready, j + 3)
                    for x in (xs, xs_hi):
                        last = dve.tensor_scalar(x.unsqueeze(1), H[:, at(j + 2), :], rs2, nb2, ALU.mult, ALU.add)
                    dve.drain().then_inc(xs_ready, 1)

            run_steps(dve, step, **A_STEPS)
            finish(dve, 0)

            enter(dve, 1)

            def normalize(g, par, dst, evacuated):
                wait(dve, evacuated, g - 1)
                for k in range(4):
                    b = 4 * g + k
                    last = dve.tensor_scalar(dst[:, par, k, :].unsqueeze(1), H[:, at(b), :], rstd[:, at(b)],
                                             mrstd[:, at(b)], ALU.mult, ALU.subtract)
                return last

            def to_columns(g, par):
                if ongroup(g):
                    normalize(g, par, xn, tb_done).then_inc(xn_ready, 1)
                if ongroup(g - 2):
                    wait(dve, xt_evac, g - 1, own=True)
                    dve.tensor_reduce(token_sum[:, at(4 * g - 8, 4)], group_rows(H2, g - 2), X, ALU.add)

            run_groups(dve, to_columns, groups + 2, peeled=4)
            router0(dve)

            def x_low(g, xpar):
                hi, lo = (x[:, xpar].rearrange("p (b d) -> p b d", b=4) for x in (x_hi, x_lo))
                wait(dve, x_hi_ready, g + 1)
                wait(dve, up_done, 16 * g - 16)
                dve.tensor_tensor(lo, group_rows(H2, g), hi.bitcast(F32), ALU.subtract).then_inc(x_split, 1)

            x_low(0, 0)

            def group(g, par):
                for c in range(CHUNKS):
                    n = 16 * g + c
                    if ongroup(g):
                        wait(dve, gelu_done, n + 1)
                        h4 = hid[:, c % 4].rearrange("p (b d) -> p b d", b=4)
                        dve.tensor_tensor(h4, h4,
                                          w4[:, c, at(4 * g, 4)].unsqueeze(2).broadcast_to([P, 4, P]), ALU.mult)
                        dve.drain()
                        wait(dve, down_done, n - 3, own=True)
                        dve.tensor_copy(hid_hi[:, c % 4], hid[:, c % 4]).then_inc(hi_ready, 1)
                    if c == 10 and ongroup(g + 1):
                        x_low(g + 1, (par + 1) % 2)
                    if c == 11 and ongroup(g - 1):
                        wait(dve, ott_done, g)
                        rows = group_rows(H, g - 1)
                        dve.tensor_tensor(rows, rows, E[:].rearrange("p (b d) -> p b d", b=4), ALU.add)
                        dve.drain().then_inc(ffn_added, 1)
                    if c in (12, 13) and ongroup(g - 1):
                        for k in (2 * c - 24, 2 * c - 23):
                            dve.bn_stats(st4[:, k, :], H[:, at(4 * g - 4 + k), :])
                    if c == 14 and ongroup(g - 1):
                        dve.drain()
                        wait(dve, mv_kept, g - 1, own=True)
                        for k in range(4):
                            last = dve.bn_aggr(mv4[:, k, :], st4[:, k, :])
                        last.then_inc(mvs_ready, 1)

            run_groups(dve, group, groups + 1)
            finish(dve, 1)

            enter(dve, 2)
            state_space_weights(dve)

            dve.wait_ge(c_factors, 1)
            normalize(0, 0, cxn, ct_done).then_inc(cxn_ready, 1)

            def states(g, par):
                if ongroup(g + 1):
                    normalize(g + 1, (par + 1) % 2, cxn, ct_done).then_inc(cxn_ready, 1)
                if ongroup(g - 1):
                    wait(dve, cz_done, g)
                    z = (B, C)[(par + 1) % 2]
                    for k in range(2):
                        rows = H[:, at(4 * g - 4 + 2 * k, 2), :]
                        last = dve.tensor_tensor(rows, rows, z[k][:, 0:288].rearrange("p (b n) -> p b n", b=2)[:, :, 0:P], ALU.add)
                    last.then_inc(c_added, 1)

            run_groups(dve, states, groups + 1, peeled=4)
            nh = 8 * nb
            for h in range(2):
                dve.wait_ge(c_pe, 5 + h)
                dve.tensor_copy(zm.rearrange("p n b -> p (n b)")[:, nh * h:nh * h + nh], A[h][:, 0:nh])
            dve.drain().then_inc(c_dve, 1)
            for h in range(2):
                dve.wait_ge(c_pe, 7 + h)
                dve.tensor_copy(hb[:, :, 8 * h:8 * h + 8].rearrange("p b n -> p n b"), B[h][:, 0:nh].rearrange("p (n b) -> p n b", b=nb))
            dve.drain().then_inc(c_dve, 1)
            for q in range(nb // 8):
                for h in range(2):
                    dve.wait_ge(c_pe, 10 + 2 * q + h)
                    rows = H[:, 8 * q + 4 * h:8 * q + 4 * h + 4, :]
                    dve.tensor_tensor(rows, rows, (A, B)[q % 2][h][:].rearrange("p (b d) -> p b d", b=4), ALU.add).then_inc(c_added, 1)
            finish(dve, 2)

            enter(dve, 3)
            dve.tensor_copy(named[:, :, P].bitcast(I32), const("token_number"))
            dve.tensor_copy(be2_all, be2_col.broadcast_to([P, P]))
            dve.drain().then_inc(d_prep_dve, 1)
            dve.wait_ge(d_prep_pe, 1)
            dve.tensor_tensor(qkv_b, qkv_b, D[:, 0:3], ALU.add)
            dve.tensor_tensor(router_b, router_b, D[:, 8:16], ALU.add)
            for w, scale in ((aq, g1_col), (ak, g1_col), (av, g1_col), (router_w, g2_col)):
                dve.tensor_scalar(w, w, scale, None, ALU.mult)
            dve.drain()
            dve.tensor_copy(bv_all, bv_col.broadcast_to([P, P]))
            dve.drain().then_inc(d_prep_dve, 1)
            dve.wait_ge(d_prep_pe, 2)
            dve.tensor_tensor(ctx_bias, D[:, 64:64 + P], bo, ALU.add)
            dve.drain().then_inc(d_prep_dve, 1)

            def attend(j, par):
                def largest(h):
                    m = slice(4 * h, 4 * h + 4)
                    wait(dve, d_s, 2 * j + h + 1)
                    dve.tensor_reduce(mx[:, m], heads4(C[h]), X, ALU.max)
                    dve.drain()
                    wait(dve, d_exp, 2 * j + h - 1)
                    dve.tensor_scalar(negm[:, m], mx[:, m], -DK ** -0.5, None, ALU.mult).then_inc(d_neg, 1)

                if on(j + 3):
                    wait(dve, d_rs1, j + 4)
                    wait(dve, d_t3, j + 2)
                    dve.tensor_scalar(n2[:, (par + 1) % 2].unsqueeze(1), H[:, at(j + 3), :], rs2x[:, 1:2], mr2x[:, 1:2],
                                      ALU.mult, ALU.subtract)
                    dve.tensor_scalar(named[:, at(j + 3), 0:P], H[:, at(j + 3), :], rs2x[:, 0:1], mr2x[:, 0:1],
                                      ALU.mult, ALU.subtract)
                    dve.drain().then_inc(d_n2, 1)
                if on(j + 4):
                    wait(dve, d_rs1, j + 4, own=True)
                    stats(sta, mva, H[:, at(j + 4), :]).then_inc(d_mv1, 1)
                if on(j):
                    largest(0)
                if on(j + 1):
                    wait(dve, d_s, 2 * j + 1)
                    wait(dve, d_qv, j + 2)
                    dve.tensor_tensor(km[:, 0:4, :], kT.unsqueeze(1).broadcast_to([P, 4, P]),
                                      const("head_of_row")[:, 0:4].unsqueeze(2).broadcast_to([P, 4, P]),
                                      ALU.mult).then_inc(d_km0, 1)
                if on(j):
                    largest(1)
                if on(j - 7):
                    wait(dve, d_wl, j - 3)
                    dve.tensor_tensor(logits[:, at(j - 7), :], E[:, P:P + MOE_E].unsqueeze(1), router_b.unsqueeze(1),
                                      ALU.add).then_inc(d_lg, 1)
                if on(j - 4):
                    wait(dve, d_wl, j - 3)
                    wait(dve, d_based, j - 3)
                    wait(dve, d_n3, j - 5)
                    wait(dve, d_hadd, j - 5)
                    dve.tensor_tensor(x2[:, par % 2].unsqueeze(1), E[:, 0:P].unsqueeze(1), named[:, at(j - 4), 0:P],
                                      ALU.add).then_inc(d_x2, 1)
                    dve.drain()
                    wait(dve, d_rs3, j - 4, own=True)
                    stats(stc, mvc, x2[:, par % 2]).then_inc(d_mv3, 1)
                if on(j - 2):
                    wait(dve, d_pv, j - 1)
                    c4 = D[:, 0:HEADS * (DK + 1)].rearrange("p (h n) -> p h n", h=HEADS)
                    dve.reciprocal(rctx.unsqueeze(2), c4[:, :, DK:DK + 1])
                    dve.drain()
                    wait(dve, d_t3, j + 3)
                    dve.tensor_tensor(ctxs.rearrange("p (h n) -> p h n", h=HEADS), c4[:, :, 0:DK],
                                      rctx.unsqueeze(2).broadcast_to([P, HEADS, DK]), ALU.mult).then_inc(d_ctx, 1)

            run_steps(dve, attend, **D_STEPS)
            finish(dve, 3)
            enter(dve, 4)
            routing(dve)
            finish(dve, 4)

            dve.wait_ge(e_act, 2)

            def tile(i, k):
                t = 4 * i + k
                if ontile(t + 1):
                    m = (k + 1) % 4
                    e = dve.value_load(table_i[0:1, at(t + 1)], min_val=0, max_val=MOE_E - 1)
                    wait(dve, f_g, t - 2)
                    dve.tensor_copy(tile_w1[:, m, :].unsqueeze(1), w1[:, at(e), :])
                    dve.tensor_copy(tile_b1[:, m, :], b1[:, at(e * MOE_C, MOE_C)])
                    dve.tensor_copy(tile_b2[:, m, :].unsqueeze(1), b2[:, at(e), :])
                    dve.drain().then_inc(f_w, 1)
                if ontile(t - 1):
                    n = (k - 1) % 4
                    wait(dve, f_out[n], 16 * (i + (k - 1) // 4))
                    wait(dve, f_d, t)
                    dve.tensor_tensor(tile_y[:, n, :], C[(k - 1) % 2][:, 0:P], tile_b2[:, n, :], ALU.add)
                    dve.drain().then_inc(f_y, 1)
                if ontile(t + 1):
                    m = (k + 1) % 4
                    wait(dve, f_out[m], 16 * (i + (k + 1) // 4))
                    wait(dve, f_in[m], 16 * (i + (k + 1) // 4) + 16)
                    dve.tensor_copy(tile_token[:, m:m + 1], tile_x[:, m, P:P + 1].bitcast(I32)).then_inc(f_tok, 1)

            run_tiles(dve, tile)

        @block.scalar
        def _(act):
            act.wait_ge(spin_ready, 1)
            act.activation(waves, spin, ACT.Sin).then_inc(waves_ready, 1)
            act.preload_act_table(ACT.Exp)

            def step(j, par):
                if on(j - 1):
                    wait(act, o_done, j - 1)
                    for h in range(2):
                        wait(act, pt_done, 2 * j + h - 1)
                        act.activation(half(pts, h), B[h][:], ACT.Copy).then_inc(pt_evac, 1)
                if on(j):
                    wait(act, p_ready, 2 * j)
                    for h in range(2):
                        wait(act, negmax, 2 * j + h + 1)
                        for k in range(4):
                            c = 4 * h + k
                            last = act.activation(prob[:, c, :], C[h][:, k * P:k * P + P], ACT.Exp, bias=negm[:, c:c + 1],
                                                  scale=SCALE, accum_out=rsum[:, c:c + 1])
                        last.then_inc(exp_done, 1)
                if on(j + 1):
                    wait(act, s_done, 2 * j + 2)
                    for h in range(2):
                        wait(act, gw_done, 2 * j + h + 3)
                        act.activation(half(gws, h), B[h][:], ACT.Copy).then_inc(gw_evac, 1)
                    wait(act, o_done, j)
                    for h in range(2):
                        wait(act, u_done, 2 * j + h + 3)
                        act.activation(half(us[:, (par + 1) % 2], h), A[h][:], ACT.Copy).then_inc(u_evac, 1)

            run_steps(act, step, **A_STEPS)
            finish(act, 0)

            enter(act, 1)

            def columns_out(g, par):
                wait(act, tb_done, g + 1, own=True)
                act.activation(group_rows(H2, g), A[par][:].rearrange("p (b d) -> p b d", b=4), ACT.Copy).then_inc(xt_evac, 1)

            run_groups(act, columns_out, groups)
            act.wait_ge(rt_dve, 2)
            act.activation(pl[0:nb, 11:22], pl[0:nb, 0:11], ACT.Exp, accum_out=pl[0:nb, 34:35]).then_inc(rt_act, 1)
            act.preload_act_table(ACT.Gelu)

            def x_high(g, xpar):
                wait(act, up_done, 16 * g - 16, own=True)
                act.activation(x_hi[:, xpar].rearrange("p (b d) -> p b d", b=4), group_rows(H2, g),
                               ACT.Copy).then_inc(x_hi_ready, 1)

            x_high(0, 0)

            def group(g, par):
                for c in range(CHUNKS):
                    n = 16 * g + c
                    if ongroup(g):
                        wait(act, lo_ready, n - 3)
                        wait(act, up_done, n + 1)
                        act.activation(hid[:, c % 4], ring[c % 4][:], ACT.Gelu, bias=fb1[:, c:c + 1]).then_inc(gelu_done, 1)
                    if c in (5, 6, 7, 8) and ongroup(g - 1):
                        k = c - 5
                        wait(act, ott_done, g - 1, own=True)
                        wait(act, down_done, 16 * g)
                        last = act.activation(ot[:, k, :], C[(par + 1) % 2][:, k * P:k * P + P], ACT.Identity,
                                              bias=b2w[:, at(4 * g - 4 + k)])
                        if k == 3:
                            last.then_inc(ot_ready, 1)
                    if c == 15 and ongroup(g - 1):
                        wait(act, mvs_ready, g, own=True)
                        act.activation(mv_all[:, at(4 * g - 4, 4), :], mv4, ACT.Copy).then_inc(mv_kept, 1)
                    if c == 9 and ongroup(g + 1):
                        x_high(g + 1, (par + 1) % 2)

            run_groups(act, group, groups + 1, peeled=4)
            finish(act, 1)

            enter(act, 2)
            act.wait_ge(c_dve, 1)
            act.activation(soft1, soft0, ACT.Exp, scale=-1.0)
            act.activation(rate, a_log, ACT.Exp)
            act.drain()
            act.activation(soft1, soft1, ACT.Ln, bias=1.0)
            act.drain().then_inc(c_act, 1)
            act.wait_ge(c_pe, 1)
            for h in range(2):
                act.activation(half(ipT, h), C[h][:], ACT.Copy)
            act.wait_ge(c_dve, 3)
            for n in range(STATES):
                act.activation(decays[:, n, :], const("age"), ACT.Exp, scale=rate[:, n:n + 1])
            act.drain().then_inc(c_act, 1)

            def states(g, par):
                if ongroup(g):
                    wait(act, cz_done, g - 1)
                    wait(act, ct_done, g + 1)
                    act.activation(cxt[:, par].rearrange("p b d -> p (b d)"), A[par][:], ACT.Copy).then_inc(cxt_evac, 1)
                if ongroup(g - 1):
                    wait(act, c_added, g, own=True)
                    z = (B, C)[(par + 1) % 2]
                    for k in range(2):
                        last = act.activation(zs[:, :, at(4 * g - 4 + 2 * k, 2)].rearrange("p n b -> p b n"),
                                              z[k][:, 0:288].rearrange("p (b n) -> p b n", b=2)[:, :, P:P + STATES], ACT.Copy)
                    last.then_inc(cz_evac, 1)

            run_groups(act, states, groups + 1, peeled=4)
            act.wait_ge(c_pe, 9)
            for h in range(-(-nb // 32)):
                k = min(4, nb // 8 - 4 * h)
                act.activation(hT[:, 4 * h:4 * h + k, :], C[h][:, 0:k * P].rearrange("p (q l) -> p q l", l=P), ACT.Copy)
            act.drain().then_inc(c_act, 1)
            finish(act, 2)

            enter(act, 3)
            act.preload_act_table(ACT.Exp)

            def attend(j, par):
                def exponentials(h):
                    wait(act, d_neg, 2 * j + h + 1)
                    for k in range(4):
                        c = 4 * h + k
                        last = act.activation(prob2[:, par % 2, c, :], C[h][:, k * P:k * P + P], ACT.Exp, bias=negm[:, c:c + 1],
                                              scale=DK ** -0.5)
                    last.then_inc(d_exp, 1)

                if on(j - 2):
                    wait(act, d_pv, j - 2)
                    for h in range(2):
                        wait(act, d_pt, 2 * j + h - 3)
                        act.activation(half(pts2, h), B[h][:], ACT.Copy).then_inc(d_pts, 1)
                if on(j + 1):
                    wait(act, d_s, 2 * j)
                    wait(act, d_km0, j + 1)
                    wait(act, d_km1, j + 1)
                    wait(act, d_pv, j - 2)
                    wait(act, d_qkv, j + 2)
                    act.activation(kT, A[1][:, P:2 * P], ACT.Identity, bias=bk_col)
                    act.activation(qT[:, (par + 1) % 2], A[1][:, 0:P], ACT.Identity, bias=bq_col)
                    act.activation(vals[:, (par + 1) % 4, :, 0:DK], A[1][:, 2 * P:3 * P].rearrange("p (h n) -> p h n", h=HEADS),
                                   ACT.Copy)
                    act.drain().then_inc(d_qv, 1)
                if on(j - 5):
                    wait(act, d_t3, upto(j + 2, nb + 8), own=True)
                    wait(act, d_rs3, j - 4, own=True)
                    act.activation(n3[:, (par + 1) % 2], x2[:, (par - 1) % 2], ACT.Identity, bias=mrc, scale=rsc)
                    act.activation(named[:, at(j - 5), 0:P], x2[:, (par - 1) % 2].unsqueeze(1), ACT.Identity, bias=mrc, scale=rsc)
                    act.drain().then_inc(d_n3, 1)
                if on(j):
                    wait(act, d_pt, 2 * j - 2)
                    exponentials(0)
                if on(j + 2) or on(j - 3) or on(j - 6):
                    wait(act, d_t3, j + 3)
                    wait(act, d_qkv, upto(j + 2))
                    wait(act, d_wl, j - 3)
                    parts = [k for k, o in enumerate((2, -3, -6)) if on(j + o)]
                    a, b = min(parts), max(parts) + 1
                    if b - a != len(parts):
                        for k in parts:
                            act.activation(turned[:, k, :], A[0][:, k * P:k * P + P], ACT.Copy)
                    else:
                        act.activation(turned[:, a:b, :].rearrange("p a b -> p (a b)"), A[0][:, a * P:b * P], ACT.Copy)
                    act.drain().then_inc(d_ts, 1)
                if on(j):
                    exponentials(1)

            run_steps(act, attend, **D_STEPS)
            finish(act, 3)
            act.wait_ge(e_dve, 1)
            act.activation(probs, logits, ACT.Exp).then_inc(e_act, 1)
            act.preload_act_table(ACT.Gelu)
            act.wait_ge(e_pe, 3)
            for e in range(MOE_E):
                act.activation(w1[:, e, :], w1[:, e, :], ACT.Copy, scale=g2_col)
            act.drain().then_inc(e_act, 1)
            finish(act, 4)

            def tile(i, k):
                t = 4 * i + k
                if ontile(t + 1):
                    wait(act, f_u, t)
                    wait(act, f_t, t + 2)
                    act.activation(tile_xT[:, (k + 1) % 2, :], A[(k + 1) % 2][:, 0:P], ACT.Copy).then_inc(f_xt, 1)
                if ontile(t):
                    wait(act, f_d, t - 1)
                    wait(act, f_u, t + 1)
                    for c in range(MOE_C):
                        last = act.activation(tile_h[:, k % 2, c, :], B[k % 2][:, c * P:c * P + P], ACT.Gelu,
                                              bias=tile_b1[:, k, c:c + 1])
                    last.then_inc(f_g, 1)

            run_tiles(act, tile)

        @block.tensor
        def _(pe):
            pe.wait_ge(con_in, 16)
            pe.wait_ge(proj_in, 48)
            for r, dst in enumerate((A, B, C)):
                for h in range(2):
                    last = pe.matmul(dst[h][:], const("centre"), half(raw[r], h), start=True, stop=True)
                last.then_inc(a_prep_pe, 1)
            pe.wait_ge(table_in, 64)
            pe.transpose(D[:, 0:P], t0, ident)
            pe.wait_ge(vec_in, 13 * 16)
            pe.transpose(D[:, 256:384], vec[:], ident)
            pe.transpose(D[:, P:P + TABLE_ROWS], t1[0:TABLE_ROWS, :], ident[0:TABLE_ROWS, 0:TABLE_ROWS]).then_inc(a_prep_pe, 1)
            pe.wait_ge(a_prep_dve, 1)
            pe.matmul(E[0:TABLE_ROWS, 0:P], t2[:, 0:TABLE_ROWS], gs, start=True, stop=True).then_inc(a_prep_pe, 1)
            pe.wait_ge(a_prep_dve, 2)
            pe.wait_ge(a_split_dve, 1)
            pe.wait_ge(a_split_pool, 1)
            pe.wait_ge(ids_placed, 16)

            def step(j, par):
                if on(j):
                    for h in range(2):
                        wait(pe, exp_done, 2 * j + h - 1)
                        wait(pe, gw_evac, 2 * j + h + 1)
                        for k in range(4):
                            c = 4 * h + k
                            last = pe.matmul(C[h][:, k * P:k * P + P], wq[:, c, :], gws[:, c, :], start=True, stop=True)
                        last.then_inc(s_done, 1)
                if on(j + 5):
                    wait(pe, oh_ready, j + 5)
                    wait(pe, g_evac, upto(j + 1))
                    pe.matmul(D[0:TABLE_ROWS, P:2 * P], const("spread", 3), idrow[0:3, at(j + 5), :],
                              start=True, stop=True).then_inc(bc_done, 1)
                if on(j - 1):
                    wait(pe, em_evac, upto(j + 4))
                    wait(pe, o_added, j - 1)
                    wait(pe, pt_evac, 2 * j)
                    wait(pe, u_evac, 2 * j)
                    for c in range(HEADS):
                        last = pe.matmul(E[:, 0:P], pts[:, c, :], us[:, (par + 1) % 2, c, :], start=c == 0, stop=c == HEADS - 1)
                    last.then_inc(o_done, 1)
                if on(j + 1):
                    wait(pe, oh_ready, upto(j + 6))
                    wait(pe, xs_ready, j + 2)
                    pe.matmul(D[:, 0:P], xs, xs, start=True, stop=True).then_inc(g_done, 1)
                    wait(pe, xl_ready, j + 2)
                    for h in range(2):
                        wait(pe, u_evac, 2 * j + h + 1)
                        product(pe, A[h][:], (xs_hi, xs_lo), (half(wp_hi, h), half(wp_lo, h))).then_inc(xw_done, 1)
                if on(j + 4):
                    wait(pe, oh_ready, j + 5)
                    wait(pe, em_evac, j + 4)
                    wait(pe, o_added, j)
                    pe.matmul(E[:, P:2 * P], onehot[0:TABLE_ROWS, par, :], table, start=True, stop=True).then_inc(em_done, 1)
                if on(j + 1):
                    for h in range(2):
                        wait(pe, pt_evac, 2 * j + h - 1)
                        wait(pe, g_evac, j + 2)
                        product(pe, B[h][:], (gs_hi, gs_lo), (half(wk_hi, h), half(wk_lo, h))).then_inc(gw_done, 1)
                    for h in range(2):
                        wait(pe, xw_evac, 2 * j + h + 3)
                        for k in range(4):
                            c = 4 * h + k
                            last = pe.matmul(A[h][:, k * P:k * P + P], wv[:, c, :], xws[:, c, :], start=True, stop=True)
                        last.then_inc(u_done, 1)
                if on(j):
                    for h in range(2):
                        wait(pe, p_ready, 2 * j + h + 1)
                        wait(pe, pt_evac, 2 * j + h - 1)
                        wait(pe, gw_evac, upto(2 * j + h + 3, 2 * nb))
                        for k in range(4):
                            last = pe.transpose(B[h][:, k * P:k * P + P], prob[:, 4 * h + k, :], ident)
                        last.then_inc(pt_done, 1)

            run_steps(pe, step, **A_STEPS)
            finish(pe, 0)

            enter(pe, 1)

            def turn(g, par, src, ready, evacuated, done):
                wait(pe, evacuated, g - 1)
                wait(pe, ready, g + 1)
                for k in range(4):
                    last = pe.transpose(A[par][:, k * P:k * P + P], src[:, par, k, :], ident)
                last.then_inc(done, 1)

            run_groups(pe, lambda g, par: turn(g, par, xn, xn_ready, xt_evac, tb_done), groups)
            pe.wait_ge(rt_dve, 1)
            pe.matmul(E[0:nb, 0:PARTS], token_sum[:], part_w, start=True, stop=True).then_inc(rt_pe, 1)
            pe.wait_ge(rt_dve, 3)
            pe.transpose(D[0:PARTS, 0:nb], pl[0:nb, 22:33], ident[0:nb, 0:nb]).then_inc(rt_pe, 1)
            pe.wait_ge(rt_dve, 4)
            pe.matmul(E[0:FFN_E, 0:nb], const("partitions", PARTS), pl[0:PARTS, 400:400 + nb], start=True, stop=True).then_inc(rt_pe, 1)
            pe.wait_ge(rt_dve, 5)
            pe.wait_ge(ffn_in, 64)
            pe.wait_ge(xt_evac, groups)
            for c in range(CHUNKS):
                pe.matmul(A[c // 8][:, (c % 8) * nb:(c % 8) * nb + nb], const("expert_of_row", FFN_E)[:, c * P:c * P + P],
                          pl[0:FFN_E, 500:500 + nb], start=True, stop=True)
            pe.matmul(B[0][:, 0:nb], fb2[:], pl[0:FFN_E, 500:500 + nb], start=True, stop=True).then_inc(rt_pe, 1)
            pe.wait_ge(rt_dve, 6)

            def up(g, c, gpar):
                n = 16 * g + c
                if c == 0:
                    wait(pe, x_split, g + 1)
                wait(pe, gelu_done, n - 3)
                product(pe, ring[c % 4][:], (f1_hi[:, c], f1_lo[:, c]), (x_hi[:, gpar], x_lo[:, gpar])).then_inc(up_done, 1)

            def group(g, par):
                if ongroup(g) and isinstance(g, int) and g == 0:
                    pe.wait_ge(w_split, 1)
                    for c in range(4):
                        up(g, c, 0)
                for c in range(CHUNKS):
                    if ongroup(g):
                        if c == 0:
                            wait(pe, ot_ready, g - 1)
                        wait(pe, lo_ready, 16 * g + c + 1)
                        product(pe, C[par][:], (f2_hi[:, c], f2_lo[:, c]), (hid_hi[:, c % 4], hid_lo[:, c % 4]), c == 0,
                                c == CHUNKS - 1).then_inc(down_done, 1)
                        if c + 4 < CHUNKS:
                            up(g, c + 4, par)
                        elif ongroup(g + 1):
                            up(g + 1, c + 4 - CHUNKS, (par + 1) % 2)
                    if c == 6 and ongroup(g - 1):
                        wait(pe, ffn_added, g - 1)
                        wait(pe, ot_ready, g)
                        for k in range(4):
                            last = pe.transpose(E[:, k * P:k * P + P], ot[:, k, :], ident)
                        last.then_inc(ott_done, 1)

            run_groups(pe, group, groups + 1)
            finish(pe, 1)

            enter(pe, 2)
            pe.wait_ge(late_in, 9 * 16)
            for c in range(HDC):
                last = pe.transpose(C[c // 4][:, (c % 4) * P:(c % 4) * P + P], ip_raw[:, c, :], ident)
            last.then_inc(c_pe, 1)
            pe.wait_ge(c_dve, 2)
            pe.matmul(D[:, 0:1], const("ones"), dt_sum, start=True, stop=True).then_inc(c_pe, 1)
            pe.wait_ge(c_act, 2)
            for c in range(HDC):
                last = pe.matmul(E[:, 0:P + STATES], ipT[:, c, :], ops[:, c, :], start=c == 0, stop=c == HDC - 1)
            last.then_inc(c_pe, 1)
            pe.wait_ge(c_dve, 3)
            for c in range(HDC):
                last = pe.matmul(D[:, P:2 * P], cproj8[:, c, :], op_raw[:, c, :], start=c == 0, stop=c == HDC - 1)
            last.then_inc(c_pe, 1)
            pe.wait_ge(c_dve, 4)

            def states(g, par):
                if ongroup(g):
                    turn(g, par, cxn, cxn_ready, cxt_evac, ct_done)
                if ongroup(g - 1):
                    o = (par + 1) % 2
                    wait(pe, cz_evac, g - 2)
                    wait(pe, cxt_evac, g)
                    for k in range(4):
                        last = pe.matmul((B, C)[o][k // 2][:, 144 * (k % 2):144 * (k % 2) + 144], cxt[:, o, k, :], state_w,
                                         start=True, stop=True)
                    last.then_inc(cz_done, 1)

            run_groups(pe, states, groups + 1, peeled=4)
            nh = 8 * nb
            pe.wait_ge(cz_evac, groups)
            for h in range(2):
                pe.matmul(A[h][:, 0:nh], mixer, zs.rearrange("p n b -> p (n b)")[:, nh * h:nh * h + nh], start=True,
                          stop=True).then_inc(c_pe, 1)
            pe.wait_ge(c_dve, 5)
            for n in range(STATES):
                last = pe.matmul(B[n // 8][:, (n % 8) * nb:(n % 8) * nb + nb], decays[:, n, :], zm[:, n, :], start=True, stop=True)
                if n % 8 == 7:
                    last.then_inc(c_pe, 1)
            pe.wait_ge(c_dve, 6)
            for q in range(nb // 8):
                last = pe.transpose(C[q // 4][:, (q % 4) * P:(q % 4) * P + P], hb[:, 8 * q:8 * q + 8, :].rearrange("p b n -> p (b n)"), ident)
            last.then_inc(c_pe, 1)
            pe.wait_ge(c_act, 3)
            for q in range(nb // 8):
                for h in range(2):
                    if q >= 2:
                        pe.wait_ge(c_added, groups + 2 * (q - 2) + h + 1)
                    pe.matmul((A, B)[q % 2][h][:], hT[:, q, :], back8.rearrange("p b d -> p (b d)")[:, 512 * h:512 * h + 512],
                              start=True, stop=True).then_inc(c_pe, 1)
            finish(pe, 2)

            enter(pe, 3)
            pe.wait_ge(dw_in, 6 * 16)
            pe.wait_ge(d_prep_dve, 1)
            for k, w in enumerate((aq, ak, av)):
                pe.matmul(D[:, k:k + 1], w, be1_col, start=True, stop=True)
            pe.matmul(D[:, 8:8 + MOE_E], be2_all, router_w, start=True, stop=True).then_inc(d_prep_pe, 1)
            pe.wait_ge(d_prep_dve, 2)
            pe.matmul(D[:, 64:64 + P], bv_all, ao, start=True, stop=True).then_inc(d_prep_pe, 1)
            pe.wait_ge(d_prep_dve, 3)

            def attend(j, par):
                if on(j + 1):
                    wait(pe, d_qv, j + 1)
                    wait(pe, d_ts, j + 2)
                    pe.matmul(A[1][:, 0:P], aq, turned[:, 0, :], start=True, stop=True)
                    pe.matmul(A[1][:, P:2 * P], ak, turned[:, 0, :], start=True, stop=True)
                    pe.matmul(A[1][:, 2 * P:3 * P], turned[:, 0, :], av, start=True, stop=True).then_inc(d_qkv, 1)
                if on(j):
                    wait(pe, d_qv, j + 1)
                    for h, ready in enumerate((d_km0, d_km1)):
                        wait(pe, ready, j + 1)
                        wait(pe, d_exp, 2 * j + h - 1)
                        pe.matmul(C[h][:], qT[:, par % 2], half(km, h), start=True, stop=True).then_inc(d_s, 1)
                if on(j - 4) or on(j - 7):
                    wait(pe, d_ts, j + 2)
                    wait(pe, d_x2, upto(j - 4))
                    wait(pe, d_lg, j - 7)
                    if on(j - 4):
                        last = pe.matmul(E[:, 0:P], turned[:, 1, :], ao, start=True, stop=True)
                    if on(j - 7):
                        last = pe.matmul(E[:, P:P + MOE_E], turned[:, 2, :], router_w, start=True, stop=True)
                    last.then_inc(d_wl, 1)
                if on(j + 2) or on(j - 3) or on(j - 6):
                    wait(pe, d_ts, j + 2)
                    for k, (o, src, ready) in enumerate(((2, n2[:, par % 2], d_n2), (-3, ctxs, d_ctx), (-6, n3[:, par % 2], d_n3))):
                        if on(j + o):
                            wait(pe, ready, j + o + 1)
                            last = pe.transpose(A[0][:, k * P:k * P + P], src, ident)
                    last.then_inc(d_t3, 1)
                if on(j - 2):
                    wait(pe, d_ctx, j - 2)
                    wait(pe, d_pts, 2 * j - 2)
                    for h in range(HEADS):
                        last = pe.matmul(D[:, h * (DK + 1):(h + 1) * (DK + 1)], pts2[:, h, :], vals[:, (par - 2) % 4, h, :],
                                         start=True, stop=True)
                    last.then_inc(d_pv, 1)
                if on(j - 1):
                    for h in range(2):
                        wait(pe, d_pts, 2 * j + h - 3)
                        wait(pe, d_exp, 2 * j + h - 1)
                        for k in range(4):
                            last = pe.transpose(B[h][:, k * P:k * P + P], prob2[:, (par + 1) % 2, 4 * h + k, :], ident)
                        last.then_inc(d_pt, 1)

            run_steps(pe, attend, **D_STEPS)
            finish(pe, 3)

            enter(pe, 4)
            n8 = nb * MOE_E
            for src, banks, ready in ((chosen, A, 2), (final, B, 3)):
                pe.wait_ge(e_dve, ready)
                flat = src.rearrange("p b e -> p (b e)")
                pe.matmul(banks[0][:, 0:n8], const("before"), flat, start=True, stop=True)
                pe.matmul(banks[1][:, 0:n8], const("ones"), flat, start=True, stop=True).then_inc(e_pe, 1)
            pe.wait_ge(moe_in, 48)
            for e in range(MOE_E):
                for c in range(MOE_C):
                    k = e * MOE_C + c
                    last = pe.matmul(D[:, k:k + 1], w1[:, e, c * P:c * P + P], be2_col, start=True, stop=True)
            last.then_inc(e_pe, 1)
            enter(pe, 5)

            def tile(i, k):
                t = 4 * i + k
                if ontile(t + 1):
                    n = (k + 1) % 4
                    wait(pe, f_xt, t)
                    wait(pe, f_in[n], 16 * (i + (k + 1) // 4) + 16)
                    pe.transpose(A[n % 2][:, 0:P], tile_x[:, n, 0:P], ident).then_inc(f_t, 1)
                if ontile(t):
                    wait(pe, f_g, t - 1)
                    wait(pe, f_w, t + 1)
                    wait(pe, f_xt, t + 1)
                    for c in range(MOE_C):
                        last = pe.matmul(B[k % 2][:, c * P:c * P + P], tile_w1[:, k, c * P:c * P + P], tile_xT[:, k % 2, :],
                                         start=True, stop=True)
                    last.then_inc(f_u, 1)
                if ontile(t - 1):
                    n = (k - 1) % 2
                    e = pe.value_load(table_i[0:1, at(t - 1)], min_val=0, max_val=MOE_E - 1)
                    wait(pe, f_y, t - 2)
                    wait(pe, f_g, t)
                    for c in range(MOE_C):
                        last = pe.matmul(C[n][:, 0:P], tile_h[:, n, c, :], w2[:, at(e), c, :], start=c == 0,
                                         stop=c == MOE_C - 1)
                    last.then_inc(f_d, 1)

            run_tiles(pe, tile)


INPUTS = ["x", "L0_tok_token_table", "L0_tok_pos_table", "L0_tok_row_table", "L0_tok_col_table", "L0_tok_w_spatial",
          "L0_tok_ln_gamma", "L0_tok_ln_beta", "L0_attn_Wq", "L0_attn_bq", "L0_attn_Wk", "L0_attn_bk", "L0_attn_Wv",
          "L0_attn_bv", "L0_attn_Wp", "L0_attn_bp", "L0_ffn_router_w", "L0_ffn_W1", "L0_ffn_b1", "L0_ffn_W2",
          "L0_ffn_b2", "L1_attn_input_proj", "L1_attn_output_proj", "L1_attn_a_log", "L1_attn_b_proj",
          "L1_attn_c_proj", "L1_attn_dt_proj", "L1_attn_skip_proj", "L1_attn_amplitudes_real",
          "L1_attn_amplitudes_imag", "L1_attn_rotation_angles", "L1_attn_walk_hamiltonian", "L1_ffn_ln1_g",
          "L1_ffn_ln1_b", "L1_ffn_ln2_g", "L1_ffn_ln2_b", "L1_ffn_wq", "L1_ffn_bq", "L1_ffn_wk", "L1_ffn_bk",
          "L1_ffn_wv", "L1_ffn_bv", "L1_ffn_wo", "L1_ffn_bo", "L1_ffn_router_w", "L1_ffn_router_b", "L1_ffn_w1",
          "L1_ffn_b1", "L1_ffn_w2", "L1_ffn_b2"]


def kernel(**inputs):
    import concourse.bacc as bacc
    from concourse.bass_utils import run_bass_kernel_spmd

    nb = inputs["x"].shape[0]
    blob, where = constants(nb)
    nc = bacc.Bacc("TRN2", target_bir_lowering=False, num_devices=1)
    arrays, io = {}, {}
    for name in INPUTS + ["constants"]:
        a = blob if name == "constants" else np.ascontiguousarray(inputs[name])
        arrays[f"in_{name}"] = a
        io[name] = nc.dram_tensor(f"in_{name}", a.shape, mybir.dt.from_np(a.dtype), kind="ExternalInput").ap()
    out = nc.dram_tensor("out_0", (nb, P, P), F32, kind="ExternalOutput").ap()
    build(nc, io, out, nb, where)
    r = run_bass_kernel_spmd(nc, [arrays], core_ids=[0])
    return r.results[0]["out_0"]
```
